# Optimizing a Trainium2 kernel written in Bass

```python
import numpy as np
import jax
import jax.numpy as jnp

def _softmax(x, axis=-1):
    return jax.nn.softmax(x, axis=axis)

def _gelu(x):
    return jax.nn.gelu(x, approximate=True)

def _silu(x):
    return jax.nn.silu(x)

def _sigmoid(x):
    return jax.nn.sigmoid(x)

def _layernorm(x, axis=-1, eps=1e-05):
    m = jnp.mean(x, axis=axis, keepdims=True)
    v = jnp.var(x, axis=axis, keepdims=True)
    return (x - m) / jnp.sqrt(v + eps)

def _scatter_add(tgt, idx, src, axis=0):
    return tgt.at[idx].add(src)

def _segment_sum(src, seg, n):
    return jax.ops.segment_sum(src, seg, n)
kernel_name = 'mk_gps_d1_gnn_r8_d510b8'

def setup_inputs(seed: int=0):
    np.random.seed(seed)
    _w = jnp.asarray

    def _rec_inputs():
        import jax
        import jax.numpy as jnp
        _gk = jax.random.key(seed)
        x = -6.415e-05 + 1 * jax.random.normal(jax.random.fold_in(_gk, 1), (2500, 512), jnp.float32)
        _s = jax.random.randint(jax.random.fold_in(_gk, 2), (20000,), 0, 2500, jnp.int32)
        _d = jax.random.randint(jax.random.fold_in(_gk, 3), (20000,), 0, 2500, jnp.int32)
        _loop = jnp.arange(2500, dtype=jnp.int32)
        src = jnp.concatenate([_s, _d, _loop])
        dst = jnp.concatenate([_d, _s, _loop])
        _o = jnp.argsort(dst, stable=True)
        src = src[_o]
        dst = dst[_o]
        edge_type_8 = jax.random.randint(jax.random.fold_in(_gk, 12), (42500,), 0, 8, jnp.int32)
        return (x, src, dst, edge_type_8)
    x, src, dst, edge_type_8 = _rec_inputs()

    def _L0_gnn_setup():
        import jax, jax.numpy as jnp
        import numpy as np
        N = 2500
        E = 20000
        D = 512
        R = 8
        key = jax.random.key(seed)
        ks = jax.random.split(key, 8)
        inp = {'input': jax.random.normal(ks[0], (N, D), dtype=jnp.float32), 'heads': jax.random.randint(ks[1], (E,), 0, N), 'tails': jax.random.randint(ks[2], (E,), 0, N), 'rel': jax.random.randint(ks[3], (E,), 0, R), 'W_self': jax.random.normal(ks[4], (D, D), dtype=jnp.float32) * 0.03, 'b_self': jnp.zeros((D,), dtype=jnp.float32), 'W_rel': jax.random.normal(ks[5], (2 * R, D, D), dtype=jnp.float32) * 0.03, 'b_rel': jnp.zeros((2 * R, D), dtype=jnp.float32)}
        return inp
    _L0_gnn_all = _L0_gnn_setup()
    _L0_gnn_in = {k: v for k, v in _L0_gnn_all.items() if k in ('W_self', 'b_self', 'W_rel', 'b_rel')}
    del _L0_gnn_all

    def _L0_mix_setup():
        import jax, jax.numpy as jnp
        import numpy as np
        HEADS = 8
        EPS_LN = 1e-05
        EPS_NORM = 1e-08
        key = jax.random.key(seed)
        ks = jax.random.split(key, 3)
        B, N, C = (4, 1024, 512)
        x = jax.random.normal(ks[0], (B, N, C), dtype=jnp.float32)
        qkv_w = jax.random.normal(ks[1], (3 * C, C), dtype=jnp.float32) / np.sqrt(C)
        qkv_b = jnp.zeros((3 * C,), dtype=jnp.float32)
        out_w = jax.random.normal(ks[2], (C, C), dtype=jnp.float32) / np.sqrt(C)
        out_b = jnp.zeros((C,), dtype=jnp.float32)
        ln_gamma = jnp.ones((C,), dtype=jnp.float32)
        ln_beta = jnp.zeros((C,), dtype=jnp.float32)
        return {'x': x, 'qkv_w': qkv_w, 'qkv_b': qkv_b, 'out_w': out_w, 'out_b': out_b, 'ln_gamma': ln_gamma, 'ln_beta': ln_beta}
    _L0_mix_all = _L0_mix_setup()
    _L0_mix_in = {k: v for k, v in _L0_mix_all.items() if k in ('qkv_w', 'qkv_b', 'out_w', 'out_b', 'ln_gamma', 'ln_beta')}
    del _L0_mix_all

    def _L0_ffn_setup():
        import jax, jax.numpy as jnp
        import numpy as np
        B, C, IN_LEN, OUT_LEN, E, TOP_K, N_I = (1, 1024, 512, 512, 8, 2, 16)
        key = jax.random.key(seed)
        ks = jax.random.split(key, 8)
        w = lambda k, shape, sc=0.02: jax.random.normal(k, shape, dtype=jnp.float32) * sc
        return {'x': jax.random.normal(ks[0], (B, C, IN_LEN), dtype=jnp.float32), 'Ins_tk': jax.random.normal(ks[1], (B, N_I, OUT_LEN), dtype=jnp.float32), 'gate_w': w(ks[2], (IN_LEN, E)), 'expert_w': w(ks[3], (E, IN_LEN, OUT_LEN)), 'expert_b': jnp.zeros((E, OUT_LEN), dtype=jnp.float32), 'gamma_w': w(ks[4], (E, OUT_LEN)), 'beta_w': w(ks[5], (E, OUT_LEN, OUT_LEN)), 'rmod_w': w(ks[6], (OUT_LEN, E))}
    _L0_ffn_all = _L0_ffn_setup()
    _L0_ffn_in = {k: v for k, v in _L0_ffn_all.items() if k in ('Ins_tk', 'gate_w', 'expert_w', 'expert_b', 'gamma_w', 'beta_w', 'rmod_w')}
    del _L0_ffn_all
    return {'x': x, 'src': src, 'dst': dst, 'edge_type_8': edge_type_8, 'L0_gnn_W_self': _L0_gnn_in['W_self'], 'L0_gnn_b_self': _L0_gnn_in['b_self'], 'L0_gnn_W_rel': _L0_gnn_in['W_rel'], 'L0_gnn_b_rel': _L0_gnn_in['b_rel'], 'L0_mix_qkv_w': _L0_mix_in['qkv_w'], 'L0_mix_qkv_b': _L0_mix_in['qkv_b'], 'L0_mix_out_w': _L0_mix_in['out_w'], 'L0_mix_out_b': _L0_mix_in['out_b'], 'L0_mix_ln_gamma': _L0_mix_in['ln_gamma'], 'L0_mix_ln_beta': _L0_mix_in['ln_beta'], 'L0_ffn_Ins_tk': _L0_ffn_in['Ins_tk'], 'L0_ffn_gate_w': _L0_ffn_in['gate_w'], 'L0_ffn_expert_w': _L0_ffn_in['expert_w'], 'L0_ffn_expert_b': _L0_ffn_in['expert_b'], 'L0_ffn_gamma_w': _L0_ffn_in['gamma_w'], 'L0_ffn_beta_w': _L0_ffn_in['beta_w'], 'L0_ffn_rmod_w': _L0_ffn_in['rmod_w']}

def reference(x, src, dst, edge_type_8, L0_gnn_W_self, L0_gnn_b_self, L0_gnn_W_rel, L0_gnn_b_rel, L0_mix_qkv_w, L0_mix_qkv_b, L0_mix_out_w, L0_mix_out_b, L0_mix_ln_gamma, L0_mix_ln_beta, L0_ffn_Ins_tk, L0_ffn_gate_w, L0_ffn_expert_w, L0_ffn_expert_b, L0_ffn_gamma_w, L0_ffn_beta_w, L0_ffn_rmod_w):
    import jax
    import jax.numpy as jnp

    def _L0_gnn_ref(input, heads, tails, rel, W_self, b_self, W_rel, b_rel):
        import jax, jax.numpy as jnp
        import numpy as np
        N = 2500
        E = 20000
        D = 512
        R = 8
        h_self = input @ W_self.T + b_self
        H_all = jnp.einsum('rod,nd->rno', W_rel, input) + b_rel[:, None, :]
        msg_to_heads = H_all[rel, tails]
        msg_to_tails = H_all[rel + R, heads]
        agg = jax.ops.segment_sum(msg_to_heads, heads, num_segments=N) + jax.ops.segment_sum(msg_to_tails, tails, num_segments=N)
        return jax.nn.relu(h_self + agg)

    def _L0_mix_ref(x, qkv_w, qkv_b, out_w, out_b, ln_gamma, ln_beta):
        import jax, jax.numpy as jnp
        import numpy as np
        HEADS = 8
        EPS_LN = 1e-05
        EPS_NORM = 1e-08
        B, N, C = x.shape
        h = HEADS
        d = C // h
        residual = x
        mu = jnp.mean(x, axis=-1, keepdims=True)
        var = jnp.var(x, axis=-1, keepdims=True)
        xn = (x - mu) / jnp.sqrt(var + EPS_LN) * ln_gamma + ln_beta
        qkv = xn @ qkv_w.T + qkv_b
        qkv = qkv.reshape(B, N, 3, h, d).transpose(2, 0, 3, 1, 4)
        q, k, v = (qkv[0], qkv[1], qkv[2])
        q = jax.nn.elu(q) + 1.0
        k = jax.nn.elu(k) + 1.0
        kv = jnp.einsum('bhnd,bhne->bhde', k, v)
        k_sum = jnp.sum(k, axis=2)
        out = jnp.einsum('bhnd,bhde->bhne', q, kv)
        normalizer = jnp.einsum('bhnd,bhd->bhn', q, k_sum)
        out = out / (normalizer[..., None] + EPS_NORM)
        out = out.transpose(0, 2, 1, 3).reshape(B, N, C)
        out = out @ out_w.T + out_b
        return out + residual

    def _L0_ffn_ref(x, Ins_tk, gate_w, expert_w, expert_b, gamma_w, beta_w, rmod_w):
        import jax, jax.numpy as jnp
        import numpy as np
        B, C, IN_LEN, OUT_LEN, E, TOP_K, N_I = (1, 1024, 512, 512, 8, 2, 16)
        Bx, Cx, L = x.shape
        xf = x.reshape(-1, L)
        ins = Ins_tk[0]
        router_gamma = jnp.mean(ins @ rmod_w, axis=0)
        logits = xf @ gate_w + router_gamma
        probs = jax.nn.softmax(logits.astype(jnp.float32), axis=-1)
        rw, sel = jax.lax.top_k(probs, TOP_K)
        combine = jnp.sum(jax.nn.one_hot(sel, E, dtype=rw.dtype) * rw[..., None], axis=1)
        gam = jnp.mean(ins @ gamma_w.T, axis=0)
        bet = jnp.einsum('nh,ehd->ed', ins, beta_w) / N_I
        eo = jnp.einsum('nl,eld->end', xf, expert_w) + expert_b[:, None, :]
        mod = gam[:, None, None] * eo + bet[:, None, :]
        out = jnp.einsum('ne,end->nd', combine, mod)
        return out.reshape(Bx, Cx, OUT_LEN)
    xn = _layernorm(x, axis=-1)
    x = x + _L0_gnn_ref(xn, src, dst, edge_type_8, L0_gnn_W_self, L0_gnn_b_self, L0_gnn_W_rel, L0_gnn_b_rel) + _L0_mix_ref(xn[None], L0_mix_qkv_w, L0_mix_qkv_b, L0_mix_out_w, L0_mix_out_b, L0_mix_ln_gamma, L0_mix_ln_beta)[0]
    x = x + _L0_ffn_ref(_layernorm(x, axis=-1)[None], L0_ffn_Ins_tk, L0_ffn_gate_w, L0_ffn_expert_w, L0_ffn_expert_b, L0_ffn_gamma_w, L0_ffn_beta_w, L0_ffn_rmod_w)[0]
    return x

_drawn_inputs = setup_inputs


def setup_inputs(seed=0):
    import zlib

    import numpy as np

    out = dict(_drawn_inputs(seed))
    spreads = {'L0_gnn_b_self': (0.0, 0.384),
     'L0_gnn_b_rel': (0.0, 0.1),
     'L0_mix_qkv_b': (0.0, 0.281),
     'L0_mix_out_b': (0.0, 0.268),
     'L0_mix_ln_gamma': (1.0, 0.6),
     'L0_mix_ln_beta': (0.0, 0.28),
     'L0_ffn_expert_b': (0.0, 0.8)}
    factors = {'L0_ffn_Ins_tk': 5.75,
     'L0_ffn_gate_w': 6.401,
     'L0_ffn_expert_w': 8.0,
     'L0_ffn_gamma_w': 8.0,
     'L0_ffn_beta_w': 6.281,
     'L0_ffn_rmod_w': 8.0}
    for name, (base, spread) in spreads.items():
        noise = np.random.default_rng([zlib.crc32(name.encode()), seed]).standard_normal(out[name].shape)
        drawn = base * np.exp(spread * noise) if base else spread * noise
        out[name] = jnp.asarray(drawn.astype(out[name].dtype))
    for name, factor in factors.items():
        out[name] = (out[name] * factor).astype(out[name].dtype)
    return out
```

```python
from contextlib import ExitStack

import concourse.bass as bass
from concourse import mybir

F32 = mybir.dt.float32
F32R = mybir.dt.float32r
I32 = mybir.dt.int32
ALU = mybir.AluOpType
ACT = mybir.ActivationFunctionType
AX = mybir.AxisListType

P = 128
N = 2500
NT = 20
NPAD = NT * P
D = 512
KC = D // P
R = 8
NREL = 2 * R
E = 42500
ECOL = E // P
ETAIL = E - ECOL * P
EC = ECOL + 1
MC = 2 * EC
ST = (MC * P - NT) // (2 * P) + NT
GT = 2 * ST
IT = 44
SPI = ST // IT
SCH = 9
NX = 8
NI = 16
EPS = 1e-5
EPSN = 1e-8
HB = 4
GB = 8
assert SPI * IT == ST and MC % (2 * SCH) == 0

SELF, WQ, WK, WV, WO, WX = 16, 17, 18, 19, 20, 21


def build(nc, x, src, dst, et, w_all, b_all, gam_col, bet_col, insT, gate, rmod, gamw, betw, out,
          h_d, xn_d, z_d, tab_d):
    with ExitStack() as ctx:
        def sb(name, shape, dt=F32):
            return ctx.enter_context(nc.sbuf_tensor(name, shape, dt))

        sems = {}

        def sem(name):
            if name not in sems:
                sems[name] = ctx.enter_context(nc.semaphore(name))
            return sems[name]

        xTh = sb("xTh", [P, KC * NPAD], F32R)
        xTl = sb("xTl", [P, KC * NPAD], F32R)
        acc = sb("acc", [P, NT * D])
        with nc.sbuf_tensor("Wh", [P, 2, KC, D], F32R) as Wh, nc.sbuf_tensor("Wl", [P, 2, KC, D], F32R) as Wl:
            pass
        UM = sb("UM", [P, 16, D])
        G = sb("G", [P, GB, D])
        with nc.sbuf_tensor("sph", [P, 2, D], F32R) as sph, nc.sbuf_tensor("spl", [P, 2, D], F32R) as spl:
            pass
        msg = sb("msg", [P, 4 * D], I32)
        HS = sb("HS", [P, HB, D])
        Wraw = sb("Wraw", [P, 2, D])
        brd = sb("brd", [P, 2, D])
        tbl = sb("tbl", [P, GT, 2], I32)
        ident = sb("ident", [P, P])
        iotaf = sb("iotaf", [P, P])
        ltri = sb("ltri", [P, P])
        ones = sb("ones", [P, P])
        ohr = sb("ohr", [P, 2, P], F32R)
        ohf = sb("ohf", [P, 2, P])
        idxr = sb("idxr", [P, 2, 8], I32)
        scr_i = sb("scr_i", [P, 2, SCH], I32)
        scr_v = sb("scr_v", [P, 2, SCH, 2], I32)
        stn = sb("stn", [P, 5, 6])
        mv = sb("mv", [P, NT, 2])
        ve = sb("ve", [P, NT])
        rs = sb("rs", [P, NT])
        mv2 = sb("mv2", [P, NT, 2])
        ve2 = sb("ve2", [P, NT])
        rs2 = sb("rs2", [P, NT])
        mhalf = sb("mhalf", [P, NT])
        vbias = sb("vbias", [P, NT])
        cnt = sb("cnt", [P, NT])
        nsti = sb("nsti", [P, NT], I32)
        nst = sb("nst", [P, NT])
        excl = sb("excl", [P, NT])
        off = sb("off", [P, NT])
        stoff = sb("stoff", [1, ST], I32)
        gcol = sb("gcol", [P, KC])
        bcol = sb("bcol", [P, KC])
        ins_s = sb("ins_s", [P, KC, NI])
        isum = sb("isum", [P, KC])
        rmg = sb("rmg", [P, KC, 3 * NX])
        gth = sb("gth", [P, KC, NX], F32R)
        gtl = sb("gtl", [P, KC, NX], F32R)
        rg = sb("rg", [P, 2 * NX])
        cgm = sb("cgm", [P, NX * NT])
        rt = sb("rt", [P, 16, NX])
        rtg = sb("rtg", [P, 2, NX, NX])
        tri8 = sb("tri8", [P, NX, NX])

        id8 = sb("id8", [P, NX, NX])
        g8 = sb("g8", [NX, 2])
        psb = [ctx.enter_context(nc.psum_tensor(f"ps{i}", [P, D], F32)) for i in range(8)]

        zb, xb, zz, xmf, kt, vt, kE, kR = (UM[:, i, :] for i in range(8))
        kvs = UM[:, 8:10, :].rearrange("p a b -> p (a b)").rearrange("p (k c) -> p k c", k=KC)
        bw = UM[:, 10:12, :]
        bb = brd[:, 0, :]
        eb = UM[:, 13, :]
        ibr = UM[:, 12, 0:SPI * NX].rearrange("p (s e) -> p s e", e=NX)
        isb = UM[:, 14, :].rearrange("p (k c) -> p k c", k=KC)
        cT = G[:, 6, 0:2 * P]

        gf = G[:, :, :].rearrange("p a b -> p (a b)")
        bk, msk, scn, pos, tmp = (gf[:, i * MC:(i + 1) * MC] for i in range(5))
        spf = gf[:, 5 * MC:5 * MC + 2 * ST]
        eI = UM[:, 12:14, :].rearrange("p a b -> p (a b)").bitcast(I32)[:, 0:3 * EC].rearrange("p (a b) -> p a b", a=3)
        pay = msg[:, 0:2 * MC].rearrange("p (t c) -> p t c", c=2)
        adr = msg[:, 2 * MC:3 * MC]
        loc = tbl[:, :, :].bitcast(F32)

        def xt(T, k, i):
            return T[:, k * NPAD + i * P:k * NPAD + (i + 1) * P]

        def xt3(T, i):
            return T[:, :].rearrange("p (k n) -> p k n", k=KC)[:, :, i * P:(i + 1) * P]

        def mw(T, q, k):
            return T[:, (q * KC + k) * D:(q * KC + k + 1) * D]

        def mx(T, s, k):
            o = 4 * KC * D + s * D + k * P
            return T[:, o:o + P]

        def mxs(T, s):
            o = 4 * KC * D + s * D
            return T[:, o:o + D]

        def rc(i):
            return rt[:, 8 + i % 2, :]

        def at(i):
            return acc[:, i * D:(i + 1) * D]

        S = sem
        CE = HB
        C1, C16 = 1, 16
        wsrc = w_all.rearrange("m (k p) n -> (m k) p n", p=P)

        class Chain:

            def __init__(self, eng, name):
                self.eng, self.sem, self.n, self.base = eng, sem(name), 0, 0

            def __call__(self, ins):
                ins.then_inc(self.sem, 1)
                self.n += 1
                self.eng.wait_ge(self.sem, self.base + self.n)

            def enter(self, i, per):
                self.n0, self.per, self.keep = self.n, per, self.base
                self.base = self.base + i * per

            def leave(self, steps):
                assert self.n - self.n0 == self.per, (self.n - self.n0, self.per)
                self.base = self.keep
                self.n = self.n0 + steps * self.per

        def load_w(sp, q, k):
            sp.wait_ge(S("w_lo"), 4 * q + k + 1)
            row = wsrc[4 * q + k] if isinstance(q, int) else wsrc[bass.ds(4 * q + k, 1)].rearrange("a p n -> (a p) n")
            sp.dma_start(Wraw[:, k % 2, :], row).then_inc(S(f"w_raw{k % 2}"), 16)

        def hi_w(act, q, k, dst):
            act.wait_ge(S(f"w_raw{k % 2}"), 16 * (2 * q + k // 2 + 1))
            act.activation(dst, Wraw[:, k % 2, :], ACT.Copy).then_inc(S("w_hi"), 1)

        def lo_w(dve, q, k, dst, hi):
            dve.wait_ge(S("w_hi"), 4 * q + k + 1)
            dve.tensor_tensor(dst, Wraw[:, k % 2, :], hi.bitcast(F32), ALU.subtract).then_inc(S("w_lo"), 1)

        block = ctx.enter_context(nc.Block())

        @block.sync
        def _(sp):
            for j, v in enumerate((src, dst, et)):
                sp.dma_start(eI[:, j, 0:ECOL], v[0:ECOL * P].rearrange("(p c) -> p c", p=P)).then_inc(S("e_in"), 16)
            sp.wait_ge(S("e_dummy"), 3)
            for j, v in enumerate((src, dst, et)):
                sp.dma_start(eI[0:ETAIL, j, ECOL:EC], v[ECOL * P:E].rearrange("(p c) -> p c", c=1)).then_inc(S("e_in"), 16)
            for g in range(4):
                a, b = 5 * g, min(5 * g + 5, NT - 1)
                sp.dma_start(acc[:, a * D:b * D].rearrange("p (i d) -> p i d", d=D),
                             x[a * P:b * P, :].rearrange("(i p) d -> p i d", p=P)).then_inc(S(f"x_in{g}"), 16)
            sp.wait_ge(S("x_pad"), 1)
            sp.dma_start(acc[0:N - (NT - 1) * P, (NT - 1) * D:NT * D], x[(NT - 1) * P:N, :]).then_inc(S("x_in3"), 16)
            for k in range(2):
                load_w(sp, 0, k)
            sp.dma_start(brd[:, 0, :], b_all[0:1, :].to_broadcast([P, D])).then_inc(S("b_in0"), 16)
            sp.wait_ge(S("t_fill"), 2)
            sp.dma_start(tab_d.rearrange("(p t) c -> p (t c)", p=P),
                         HS[:, :, :].rearrange("p a b -> p (a b)")[:, 0:2 * GT].bitcast(I32)).then_inc(S("t_init"), 16)
            for k in range(2, KC):
                load_w(sp, 0, k)
            for ap, v in ((gcol, gam_col), (bcol, bet_col), (ins_s, insT)):
                sp.dma_start(ap[:], v).then_inc(S("c_in"), 16)
            for j, v in enumerate((gate, rmod, gamw)):
                sp.dma_start(rmg[:, :, j * NX:(j + 1) * NX], v).then_inc(S("c_in"), 16)
            for g in range(4):
                sp.wait_ge(S("xn_ok"), g + 1)
                sp.dma_start(xn_d[5 * g * P:(5 * g + 5) * P, :].rearrange("(i p) d -> p i d", p=P),
                             acc[:, 5 * g * D:(5 * g + 5) * D].rearrange("p (i d) -> p i d", d=D)).then_inc(S("xn_out"), 16)

            def h_matrix(m, par):
                for k in range(2):
                    load_w(sp, m + 1, k)
                sp.wait_ge(S("h_ev"), CE + 20 * m)
                sp.dma_start(brd[:, 1 - par, :], b_all[bass.ds(m + 1, 1), :].to_broadcast([P, D])).then_inc(S(f"b_in{1 - par}"), 16)
                for i in range(NT):
                    sp.wait_ge(S("h_ev"), CE + 20 * m + i + 1)
                    sp.dma_start(h_d[bass.ds((m * NT + i) * P, P), :], HS[:, i % HB, :]).then_inc(S(f"h_out{i % HB}"), 16)
                    if i in (6, 12):
                        load_w(sp, m + 1, 2 + (i == 12))

            with sp.Fori(0, NREL // 2) as j:
                h_matrix(2 * j, 0)
                h_matrix(2 * j + 1, 1)
            for h in range(2):
                sp.wait_ge(S(f"sc{h}"), 16 * SCH * (MC // SCH // 2))
            sp.dma_start(tbl[:, :, :].rearrange("p t c -> p (t c)"), tab_d.rearrange("(p t) c -> p (t c)", p=P)).then_inc(S("t_in"), 16)
            for q in range(4):
                for k in range(KC):
                    load_w(sp, WQ + q, k)
            sp.wait_ge(S("h_ev"), CE + 20 * (NREL + 1))
            for j, m in enumerate((WK, WV)):
                sp.dma_start(brd[:, j, :], b_all[m:m + 1, :].to_broadcast([P, D])).then_inc(S("mb_in"), 16)
            sp.wait_ge(S("xn_out"), 64)

            with sp.Fori(0, NT) as i:
                sp.wait_ge(S("m_tr"), C1 + i)
                sp.dma_start(zb, xn_d[bass.ds(i * P, P), :]).then_inc(S("z_in"), 16)
            sp.dma_start(eb[0:NX, :], b_all[WX:WX + NX, :]).then_inc(S("eb_in"), 16)
            with sp.Fori(0, NX * KC // 2) as c:
                for h in range(2):
                    sp.wait_ge(S("bw_used"), 2 * c + h + 1)
                    sp.dma_start(bw[:, h, :], betw[bass.ds((2 * c + h) * P, P), :]).then_inc(S(f"bw_in{h}"), 16)
            sp.wait_ge(S("m_v"), C1 + NT)
            for j, m in enumerate((WQ, WO)):
                sp.dma_start(brd[:, j, :], b_all[m:m + 1, :].to_broadcast([P, D])).then_inc(S("mb_in"), 16)
            with sp.Fori(0, NT - 1) as i:
                sp.wait_ge(S("m_y"), C1 + i)
                sp.dma_start(zb, xn_d[bass.ds(i * P, P), :]).then_inc(S("z_in"), 16)
                sp.dma_start(xb, x[bass.ds(i * P, P), :]).then_inc(S("xb_in"), 16)
                sp.wait_ge(S("m_y"), C1 + i + 1)
                sp.dma_start(z_d[bass.ds(i * P, P), :], kt).then_inc(S("z_out"), 16)
            i = NT - 1
            sp.wait_ge(S("m_y"), C1 + i)
            sp.dma_start(zb, xn_d[i * P:NPAD, :]).then_inc(S("z_in"), 16)
            sp.dma_start(xb[0:N - i * P, :], x[i * P:N, :]).then_inc(S("xb_in"), 16)
            sp.wait_ge(S("m_y"), C1 + i + 1)
            sp.dma_start(z_d[i * P:NPAD, :], kt).then_inc(S("z_out"), 16)
            sp.wait_ge(S("z_out"), C16 + 16 * NT)
            for k in range(2):
                load_w(sp, WX, k)
            for i in range(HB):
                sp.dma_start(HS[:, i % HB, :], z_d[i * P:(i + 1) * P, :]).then_inc(S(f"f_in{i % HB}"), 16)
            for k in range(2, KC):
                load_w(sp, WX, k)
            for k in range(2):
                load_w(sp, WX + 1, k)
            for i in range(HB, NT):
                sp.wait_ge(S("f_x1"), i - HB + 1)
                sp.dma_start(HS[:, i % HB, :], z_d[i * P:(i + 1) * P, :]).then_inc(S(f"f_in{i % HB}"), 16)
                if i in (11, 16):
                    load_w(sp, WX + 1, 2 + (i == 16))
            with sp.Fori(0, NX - 2) as e:
                for k in range(KC):
                    load_w(sp, WX + 2 + e, k)
            for i in range(NT):
                rows = min(P, N - i * P)
                sp.wait_ge(S("x_ev"), CE + NT * (NX - 1) + i + 1)
                sp.dma_start(out[i * P:i * P + rows, :], acc[0:rows, i * D:(i + 1) * D]).then_inc(S("out_ok"), 16)
            sp.wait_ge(S("out_ok"), 16 * NT)

        @block.gpsimd
        def _(pool):
            ch = Chain(pool, "pool_ch")

            def waited():
                pool.sem_inc(S("pool_waited"), 1)

            pool.memset(eI[:, 0:2, ECOL:EC], NPAD - 1).then_inc(S("e_dummy"), 2)
            pool.memset(eI[:, 2:3, ECOL:EC], 0).then_inc(S("e_dummy"), 1)
            pool.wait_ge(S("e_dummy"), 3)
            pool.memset(acc[64:P, (NT - 1) * D:NT * D], 0.0).then_inc(S("x_pad"), 1)
            pool.wait_ge(S("x_pad"), 1)
            ch(pool.memset(ltri[:], 1.0))
            pool.affine_select(out=ltri[:], in_=ltri[:], compare_op=ALU.is_gt, fill=0.0, base=0,
                               pattern=[[1, P]], channel_multiplier=-1)
            pool.memset(ones[:], 1.0).then_inc(S("k_cst"), 1)
            ch(pool.memset(ident[:], 0.0))
            pool.affine_select(out=ident[:], in_=ident[:], compare_op=ALU.not_equal, fill=1.0, base=0,
                               pattern=[[-1, P]], channel_multiplier=1).then_inc(S("k_id"), 1)
            hs = HS[:, :, :].rearrange("p a b -> p (a b)")[:, 0:2 * GT].bitcast(I32).rearrange("p (t c) -> p t c", c=2)
            pool.memset(hs[:, :, 0:1], 0).then_inc(S("t_fill"), 1)
            pool.memset(hs[:, :, 1:2], -1).then_inc(S("t_fill"), 1)
            pool.iota(iotaf[:], pattern=[[1, P]], base=0, channel_multiplier=0,
                      allow_small_or_imprecise_dtypes=True).then_inc(S("k_iota"), 1)
            pool.iota(spf[0:1, 0:ST], pattern=[[1, ST]], base=0, channel_multiplier=0,
                      allow_small_or_imprecise_dtypes=True).then_inc(S("k_iota"), 1)
            pool.memset(mhalf[:], -0.5)
            ch(pool.memset(vbias[:], 0.0))
            pool.affine_select(out=vbias[:, NT - 1:NT], in_=vbias[:, NT - 1:NT], compare_op=ALU.is_gt, fill=-1e30,
                               base=N - (NT - 1) * P, pattern=[[0, 1]], channel_multiplier=-1)
            ch(pool.memset(tri8[:], 1.0))
            pool.affine_select(out=tri8[:], in_=tri8[:], compare_op=ALU.is_gt, fill=0.0, base=0,
                               pattern=[[1, NX], [-1, NX]], channel_multiplier=0)
            ch(pool.memset(id8[:], 0.0))
            pool.affine_select(out=id8[:], in_=id8[:], compare_op=ALU.not_equal, fill=1.0, base=0,
                               pattern=[[1, NX], [-1, NX]], channel_multiplier=0).then_inc(S("k_tri"), 1)
            for g in range(4):
                pool.wait_ge(S("ve"), g + 1)
                pool.tensor_tensor(rs[:, 5 * g:5 * g + 5], ve[:, 5 * g:5 * g + 5], mhalf[:, 0:5], ALU.pow).then_inc(S("rs"), 1)
            pool.wait_ge(S("adr"), 1)
            pool.wait_ge(S("t_init"), 16)
            def scatter(j):
                for h in range(2):
                    c = (2 * j + h) * SCH
                    if not isinstance(j, int):
                        pool.wait_ge(S(f"sc{h}"), 16 * SCH * j)
                        waited()
                    pool.tensor_copy(scr_i[:, h, :], adr[:, bass.ds(c, SCH)])
                    ch(pool.tensor_copy(scr_v[:, h, :, :], pay[:, bass.ds(c, SCH), :]))
                    if not isinstance(j, int):
                        waited()
                    for u in range(SCH):
                        pool.indirect_dma_start(
                            out=tab_d, out_offset=bass.IndirectOffsetOnAxis(ap=scr_i[:, h, u:u + 1], axis=0),
                            in_=scr_v[:, h, u, :], in_offset=None).then_inc(S(f"sc{h}"), 16)

            scatter(0)
            with pool.Fori(1, MC // SCH // 2) as j:
                ch.enter(j - 1, 2)
                scatter(j)
                ch.leave(MC // SCH // 2 - 1)
            pool.wait_ge(S("ve2"), 1)
            pool.tensor_tensor(rs2[:], ve2[:], mhalf[:], ALU.pow).then_inc(S("rs2"), 1)
            pool.wait_ge(S("t_in"), 16)
            for h in range(HB):
                pool.wait_ge(S(f"h_out{h}"), 16 * NREL * NT // HB)
            with pool.Fori(0, IT) as it:
                ch.enter(it, 2)
                for h in range(2):
                    ch(pool.tensor_copy(idxr[:, h, :], tbl[:, bass.ds(16 * it + 8 * h, 8), 0]))
                    for u in range(GB):
                        s = 4 * h + u // 2
                        pool.wait_ge(S("st_pe" if u % 2 else "st_lo"), SPI * it + s + 1)
                        waited()
                        pool.indirect_dma_start(
                            out=G[:, u, :], out_offset=None, in_=h_d,
                            in_offset=bass.IndirectOffsetOnAxis(ap=idxr[:, h, u:u + 1], axis=0)).then_inc(S(f"g_in{u}"), 16)
                ch.leave(IT)
            for i in range(NT):
                pool.wait_ge(S("f_ve"), i + 1)
                pool.tensor_tensor(rs[:, i:i + 1], ve[:, i:i + 1], mhalf[:, 0:1], ALU.pow).then_inc(S("f_rs"), 1)

        @block.scalar
        def _(act):
            ch = Chain(act, "act_ch")

            def w_half(q, par, ks=range(KC)):
                for k in ks:
                    hi_w(act, q, k, Wh[:, par, k, :])

            for i in range(NT):
                act.wait_ge(S("t_pe"), i + 1)
                act.activation(xt3(xTh, i), psb[4 + i % 2][:].rearrange("p (k c) -> p k c", k=KC), ACT.Copy).then_inc(S("t_hi"), 1)
                if i in (4, 8, 12, 16):
                    w_half(0, 0, [i // 4 - 1])
            with act.Fori(0, NREL // 2) as j:
                for par in range(2):
                    act.wait_ge(S("h_pe"), C1 + NT * (2 * j + par))
                    w_half(2 * j + par + 1, 1 - par)
            act.wait_ge(S("h_pe"), C1 + NT * (NREL + 1))
            for q in range(4):
                for k in range(KC):
                    hi_w(act, WQ + q, k, mw(xTh, q, k))

            def st_step(it, s):
                st = SPI * it + s
                act.wait_ge(S(f"g_in{2 * (s % 4)}"), 16 * (2 * it + s // 4 + 1))
                act.wait_ge(S("st_pe"), st + 3)
                act.activation(sph[:, s % 2, :], G[:, 2 * (s % 4), :], ACT.Copy).then_inc(S("st_hi"), 1)

            def xm_part(i, used):
                act.wait_ge(S("m_tr"), C1 + i + 1)
                act.wait_ge(S("m_lo"), C1 + i)
                for k in range(KC):
                    xa = act.activation(xmf[:, k * P:(k + 1) * P], psb[4][:, k * P:(k + 1) * P], ACT.Identity,
                                        bias=bcol[:, k:k + 1], scale=gcol[:, k:k + 1])
                ch(xa)
                act.wait_ge(S(used), C1 + i)
                act.activation(mxs(xTh, 0), xmf, ACT.Copy).then_inc(S("m_hi"), 1)

            def elu_part(i):
                act.wait_ge(S("m_k2"), i + 1)
                b = vbias[:, bass.ds(i, 1)]
                act.activation(kE, kt, ACT.Exp, bias=b)
                act.activation(kR, kt, ACT.Relu, bias=b).then_inc(S("m_e"), 1)

            act.wait_ge(S("c_in"), 96)
            act.wait_ge(S("k_tri"), 1)
            with act.Fori(0, NT) as it:
                ch.enter(it, 1)
                for s in range(SPI):
                    if s == 2:
                        xm_part(it, "m_p1")
                    if s == 7:
                        elu_part(it)
                    st_step(it, s)
                ch.leave(NT)
            with act.Fori(0, IT - 2 * NT) as jt:
                for s in range(SPI):
                    st_step(NT + jt, s)
            act.wait_ge(S("m_p1"), C1 + NT)
            with act.Fori(0, NT) as jt:
                ch.enter(jt, 1)
                it = IT - NT + jt
                i = NT + jt
                for s in range(SPI):
                    if s == 1:
                        xm_part(i, "m_k")
                    if s == 4:
                        act.wait_ge(S("m_k2"), i + 1)
                        act.activation(kE, kt, ACT.Exp)
                        act.activation(kR, kt, ACT.Relu).then_inc(S("m_e"), 1)
                    if s == 5:
                        act.wait_ge(S("q_tr"), jt + 1)
                        act.activation(zz, psb[4][:], ACT.Copy).then_inc(S("q_t"), 1)
                    if s == 7:
                        act.wait_ge(S("o_f"), C1 + jt + 1)
                        act.activation(mxs(xTh, 1), xmf, ACT.Copy).then_inc(S("o_hi"), 1)
                    st_step(it, s)
                ch.leave(NT)
            act.wait_ge(S("z_out"), C16 + 16 * NT)
            act.wait_ge(S("m_y"), C1 + NT)
            act.wait_ge(S("bb_ok"), 1)
            w_half(WX, 0)
            for i in range(NT):
                act.wait_ge(S("f_tr"), i + 1)
                act.activation(xt3(xTh, i), psb[4 + i % 2][:].rearrange("p (k c) -> p k c", k=KC), ACT.Copy).then_inc(S("f_hi"), 1)
                act.wait_ge(S("f_lg"), i + 1)
                act.activation(rt[:, 2, :], rt[:, 0, :], ACT.Exp, bias=rt[:, 1, 0:1], accum_out=rt[:, 1, 1:2]).then_inc(S("f_ex"), 1)
                if i % 5 == 4:
                    w_half(WX + 1, 1, [i // 5])
            for e in range(2, NX):
                act.wait_ge(S("x_pe"), NT * (e - 1))
                w_half(WX + e, e % 2)

        @block.tensor
        def _(pe):
            def three(ps, lh, ll, rh, rl, first=True, last=True):
                for k in range(KC):
                    a = pe.matmul(ps, lh(k), rh(k), start=(first and k == 0), stop=False)
                    a = pe.matmul(ps, lh(k), rl(k), start=False, stop=False)
                    a = pe.matmul(ps, ll(k), rh(k), start=False, stop=(last and k == KC - 1))
                return a

            pe.wait_ge(S("k_cst"), 1)
            pe.wait_ge(S("cnt"), NT)
            pe.matmul(psb[7][:, 0:NT], ltri[:], cnt[:], start=True, stop=True)
            pe.matmul(psb[7][:, 32:32 + NT], ones[:], cnt[:], start=True, stop=True).then_inc(S("pre"), 1)
            pe.wait_ge(S("k_id"), 1)
            for i in range(NT):
                if i % 5 == 0:
                    pe.wait_ge(S("xn_ok"), i // 5 + 1)
                if i >= 2:
                    pe.wait_ge(S("t_lo"), i - 1)
                for k in range(KC):
                    a = pe.transpose(psb[4 + i % 2][:, k * P:(k + 1) * P], acc[:, i * D + k * P:i * D + (k + 1) * P], ident[:])
                a.then_inc(S("t_pe"), 1)
            pe.wait_ge(S("t_lo"), NT)

            def h_matrix(m, par):
                pe.wait_ge(S("w_lo"), 2 + 4 * (m + 1))
                for i in range(NT):
                    pe.wait_ge(S("h_ev"), 20 * m + i + 1)
                    three(psb[i % HB][:], lambda k: xt(xTh, k, i), lambda k: xt(xTl, k, i),
                          lambda k: Wh[:, par, k, :], lambda k: Wl[:, par, k, :]).then_inc(S("h_pe"), 1)

            with pe.Fori(0, NREL // 2) as j:
                h_matrix(2 * j, 0)
                h_matrix(2 * j + 1, 1)
            h_matrix(NREL, 0)

            def st_step(it, s):
                st = SPI * it + s
                pe.wait_ge(S("st_ev"), st + 1)
                pe.wait_ge(S("st_lo"), 4 + st + 1)
                ps = psb[s % 2][:]
                pe.matmul(ps, ohr[:, s % 2, :], sph[:, s % 2, :], start=True, stop=False)
                pe.matmul(ps, ohr[:, s % 2, :], spl[:, s % 2, :], start=False, stop=False)
                u = 2 * (s % 4) + 1
                pe.wait_ge(S(f"g_in{u}"), 16 * (2 * it + s // 4 + 1))
                pe.matmul(ps, ohf[:, s % 2, :], G[:, u, :], start=False, stop=True).then_inc(S("st_pe"), 1)

            def xm_tr(i):
                pe.wait_ge(S("m_z"), i + 1)
                pe.wait_ge(S("m_hi"), C1 + i)
                for k in range(KC):
                    a = pe.transpose(psb[4][:, k * P:(k + 1) * P], zz[:, k * P:(k + 1) * P], ident[:])
                a.then_inc(S("m_tr"), 1)

            def proj(ps, s, q, name):
                three(ps, lambda k: mx(xTh, s, k), lambda k: mx(xTl, s, k),
                      lambda k: mw(xTh, q, k), lambda k: mw(xTl, q, k)).then_inc(S(name), 1)

            pe.wait_ge(S("h_ev"), CE + 20 * (NREL + 1))
            pe.wait_ge(S("zeros"), 1)
            for b in (5, 6):
                pe.matmul(psb[b][:], ltri[:], UM[:, 15, :], start=True, stop=False, skip_group_check=True)
            with pe.Fori(0, NT) as it:
                for s in range(SPI):
                    if s == 1:
                        xm_tr(it)
                    if s == 5:
                        pe.wait_ge(S("w_lo"), 2 + 4 * WX)
                        pe.wait_ge(S("m_lo"), C1 + it + 1)
                        pe.wait_ge(S("m_v"), C1 + it)
                        proj(psb[2][:], 0, 1, "m_k")
                        proj(psb[3][:], 0, 2, "m_p1")
                    st_step(it, s)
                pe.wait_ge(S("m_k3"), it + 1)
                for k in range(KC):
                    c = slice(k * P, (k + 1) * P)
                    pe.matmul(psb[5][:, c], kt[:, c], vt[:, c], start=False, stop=False, skip_group_check=True)
                    a = pe.matmul(psb[6][:, c], kt[:, c], ones[:], start=False, stop=False, skip_group_check=True)
                a.then_inc(S("m_kv"), 1)
            pe.wait_ge(S("ib_ok"), 1)
            pe.wait_ge(S("m_v"), C1 + NT)
            for k in range(KC):
                pe.matmul(psb[2][:, 0:2 * NX], isb[:, k, :], rmg[:, k, NX:3 * NX], start=(k == 0), stop=(k == KC - 1))
            for k in range(KC):
                a = pe.matmul(psb[3][0:NX, 0:2], rmg[:, k, 2 * NX:3 * NX], isb[:, k, 0:2], start=(k == 0), stop=(k == KC - 1))
            a.then_inc(S("rg_pe"), 1)
            pe.matmul(psb[7][0:NX, :], ltri[:, 0:NX], UM[:, 15, :], start=True, stop=False, skip_group_check=True)
            with pe.Fori(0, IT - 2 * NT) as jt:
                pe.wait_ge(S("ib_e"), jt + 1)
                for s in range(SPI):
                    pe.wait_ge(S(f"bw_in{s % 2}"), 16 * (SPI // 2 * jt + s // 2 + 1))
                    pe.matmul(psb[7][0:NX, :], ibr[:, s, :], bw[:, s % 2, :],
                              start=False, stop=False, skip_group_check=True).then_inc(S("bw_used"), 1)
                    st_step(NT + jt, s)
            pe.wait_ge(S("rg_ok"), 1)
            with pe.Fori(0, NT) as jt:
                it = IT - NT + jt
                i = NT + jt
                for s in range(SPI):
                    if s == 0:
                        xm_tr(i)
                    if s == 3:
                        pe.wait_ge(S("m_lo"), C1 + i + 1)
                        pe.wait_ge(S("m_k2"), i)
                        proj(psb[2][:], 0, 0, "m_k")
                    if s == 5:
                        pe.wait_ge(S("m_k3"), i + 1)
                        for k in range(KC):
                            a = pe.transpose(psb[4][:, k * P:(k + 1) * P], kt[:, k * P:(k + 1) * P], ident[:])
                        a.then_inc(S("q_tr"), 1)
                    if s == 6:
                        pe.wait_ge(S("kvs_ok"), 1)
                        pe.wait_ge(S("q_t"), jt + 1)
                        pe.wait_ge(S("o_f"), C1 + jt)
                        for k in range(KC):
                            c = slice(k * P, (k + 1) * P)
                            pe.matmul(psb[5][:, c], kvs[:, k, 0:P], zz[:, c], start=(k == 0), stop=(k == KC - 1), skip_group_check=True)
                            a = pe.matmul(psb[6][:, c], kvs[:, k, P:2 * P], zz[:, c], start=(k == 0), stop=(k == KC - 1), skip_group_check=True)
                        a.then_inc(S("o_pe"), 1)
                    st_step(it, s)
                pe.wait_ge(S("o_lo"), jt + 1)
                pe.wait_ge(S("m_y"), C1 + jt)
                proj(psb[3][:], 1, 3, "o_p")
            pe.wait_ge(S("m_y"), C1 + NT)
            pe.wait_ge(S("st_ev"), 2 + ST)
            pe.wait_ge(S("bb_ok"), 1)

            def expert(e, par, pre=None):
                pe.wait_ge(S("w_lo"), 2 + 4 * (WX + e + 1))
                for i in range(NT):
                    if pre:
                        pre(i)
                    pe.wait_ge(S("x_ev"), NT * e + i + 1)
                    three(psb[i % HB][:], lambda k: xt(xTh, k, i), lambda k: xt(xTl, k, i),
                          lambda k: Wh[:, par, k, :], lambda k: Wl[:, par, k, :]).then_inc(S("x_pe"), 1)

            def tr(i):
                pe.wait_ge(S("f_z"), i + 1)
                if i >= 2:
                    pe.wait_ge(S("f_lo"), i - 1)
                for k in range(KC):
                    a = pe.transpose(psb[4 + i % 2][:, k * P:(k + 1) * P], G[:, i % 2, k * P:(k + 1) * P], ident[:])
                a.then_inc(S("f_tr"), 1)

            def gate_i(i):
                pe.wait_ge(S("f_lo"), i + 1)
                if i >= 1:
                    pe.wait_ge(S("f_lg"), i)
                three(psb[6][:, 0:NX], lambda k: xt(xTh, k, i), lambda k: xt(xTl, k, i),
                      lambda k: gth[:, k, :], lambda k: gtl[:, k, :]).then_inc(S("f_gt"), 1)

            def bias_i(i):
                pe.wait_ge(S("f_c"), i + 1)
                if i >= 1:
                    pe.wait_ge(S("f_b2"), i)
                pe.transpose(psb[7][0:NX, 0:P], rc(i), ident[:]).then_inc(S("f_c1"), 1)
                pe.wait_ge(S("f_ct"), i + 1)
                pe.matmul(psb[7][:], cT[0:NX, 0:P], bb[0:NX, :], start=True, stop=True).then_inc(S("f_b"), 1)

            tr(0)

            def pre(i):
                if i + 1 < NT:
                    tr(i + 1)
                gate_i(i)
                if i >= 1:
                    bias_i(i - 1)

            expert(0, 0, pre)
            bias_i(NT - 1)
            with pe.Fori(0, (NX - 2) // 2) as j:
                expert(2 * j + 1, 1)
                expert(2 * j + 2, 0)
            expert(NX - 1, 1)

        @block.vector
        def _(dve):
            ch = Chain(dve, "dve_ch")
            dve.sem_inc(S("h_ev"), HB)
            dve.sem_inc(S("x_ev"), HB)
            for name in ("m_tr", "m_y", "h_pe", "m_lo", "m_p1", "m_k", "m_hi", "m_v", "o_f", "m_kv"):
                dve.sem_inc(S(name), C1)
            dve.sem_inc(S("z_out"), C16)
            dve.sem_inc(S("w_lo"), 2)
            dve.sem_inc(S("st_ev"), 2)
            dve.sem_inc(S("st_lo"), 4)
            dve.sem_inc(S("bw_used"), 2)
            dve.sem_inc(S("st_pe"), 4)
            dve.wait_ge(S("e_in"), 96)
            T = eI[:, 0:2, :].rearrange("p a b -> p (a b)")
            ti = tmp.bitcast(I32)
            ch(dve.tensor_scalar(ti, T, 7, None, ALU.arith_shift_right))
            ch(dve.tensor_copy(bk, ti))
            dve.tensor_scalar(pay[:, 0:MC, 1], T, P - 1, None, ALU.bitwise_and)
            for b in range(NT):
                dve.tensor_scalar(msk, bk, float(b), None, ALU.is_equal, ALU.add, accum_out=cnt[:, b:b + 1]).then_inc(S("cnt"), 1)
                dve.wait_ge(S("cnt"), b + 1)
            dve.scalar_tensor_tensor(pay[:, 0:EC, 0], eI[:, 2, :], float(NPAD), eI[:, 1, :], ALU.mult, ALU.add)
            ch(dve.tensor_scalar(ti[:, 0:EC], eI[:, 2, :], float(NPAD), float(R * NPAD), ALU.mult, ALU.add))
            dve.tensor_tensor(pay[:, EC:MC, 0], ti[:, 0:EC], eI[:, 0, :], ALU.add)
            ch(dve.memset(pos, 0.0))

            def stats(mvt, g):
                for i in range(5 * g, 5 * g + 5):
                    a = dve.bn_stats(stn[:, i - 5 * g, :], at(i))
                ch(a)
                for i in range(5 * g, 5 * g + 5):
                    a = dve.bn_aggr(mvt[:, i, :], stn[:, i - 5 * g, :])
                ch(a)

            def norm(g):
                dve.wait_ge(S("rs"), g + 1)
                for i in range(5 * g, 5 * g + 5):
                    a = dve.tensor_scalar(at(i), at(i), mv[:, i, 0:1], rs[:, i:i + 1], ALU.subtract, ALU.mult)
                a.then_inc(S("xn_ok"), 1)

            for g in range(4):
                dve.wait_ge(S(f"x_in{g}"), 16 if g < 3 else 32)
                stats(mv, g)
                dve.tensor_scalar(ve[:, 5 * g:5 * g + 5], mv[:, 5 * g:5 * g + 5, 1], EPS, None, ALU.add).then_inc(S("ve"), 1)
                if g:
                    norm(g - 1)
            norm(3)
            dve.wait_ge(S("pre"), 1)
            ch(dve.tensor_scalar(nsti[:], psb[7][:, 32:32 + NT], float(2 * P - 1), None, ALU.add))
            ch(dve.tensor_scalar(nsti[:], nsti[:], 8, None, ALU.arith_shift_right))
            ch(dve.tensor_copy(nst[:], nsti[:]))
            ch(dve.tensor_tensor_scan(excl[:], nst[:], nst[:], 0.0, ALU.add, ALU.max))
            ch(dve.tensor_tensor(excl[:], excl[:], nst[:], ALU.subtract))
            ch(dve.scalar_tensor_tensor(off[:], excl[:], float(2 * P), psb[7][:, 0:NT], ALU.mult, ALU.add))
            ch(dve.tensor_scalar(off[:], off[:], -1.0, None, ALU.add))

            def sort_ops():
                for b in range(NT):
                    yield lambda b=b: ch(dve.tensor_scalar(msk, bk, float(b), None, ALU.is_equal))
                    yield lambda b=b: ch(dve.tensor_tensor_scan(scn, msk, msk, 0.0, ALU.add, ALU.max))
                    yield lambda b=b: ch(dve.scalar_tensor_tensor(tmp, scn, off[:, b:b + 1], msk, ALU.add, ALU.mult))
                    yield lambda b=b: ch(dve.tensor_tensor(pos, pos, tmp, ALU.add))
                si, mi = scn.bitcast(I32), msk.bitcast(I32)
                yield lambda: ch(dve.tensor_copy(si, pos))
                yield lambda: dve.tensor_scalar(mi, si, P - 1, None, ALU.bitwise_and)
                yield lambda: ch(dve.tensor_scalar(ti, si, 7, None, ALU.arith_shift_right))
                yield lambda: dve.scalar_tensor_tensor(adr, mi, float(GT), ti, ALU.mult, ALU.add).then_inc(S("adr"), 1)
                yield lambda: dve.wait_ge(S("k_iota"), 2)
                yield lambda: ch(dve.memset(spf[0:1, ST:2 * ST], 0.0))
                for b in range(1, NT):
                    yield lambda b=b: ch(dve.scalar_tensor_tensor(
                        spf[0:1, ST:2 * ST], spf[0:1, 0:ST], excl[0:1, b:b + 1], spf[0:1, ST:2 * ST], ALU.is_ge, ALU.add))
                yield lambda: ch(dve.tensor_scalar(stoff[:], spf[0:1, ST:2 * ST], float(D), None, ALU.mult))
                for g in range(4):
                    yield lambda g=g: stats(mv2, g)
                yield lambda: dve.tensor_scalar(ve2[:], mv2[:, :, 1], EPS, None, ALU.add).then_inc(S("ve2"), 1)

            for i in range(NT):
                dve.wait_ge(S("t_hi"), i + 1)
                dve.tensor_tensor(xt3(xTl, i), psb[4 + i % 2][:].rearrange("p (k c) -> p k c", k=KC),
                                  xt3(xTh, i).bitcast(F32), ALU.subtract).then_inc(S("t_lo"), 1)
                if i in (4, 8, 12, 16):
                    k = i // 4 - 1
                    lo_w(dve, 0, k, Wl[:, 0, k, :], Wh[:, 0, k, :])

            def h_matrix(j, par, nxt=True, between=None):
                m = 2 * j + par
                dve.wait_ge(S(f"b_in{par}"), 16 * (j + 1))
                for i in range(NT):
                    if between:
                        for _ in range(4):
                            op = next(between, None)
                            if op:
                                op()
                    dve.wait_ge(S("h_pe"), C1 + 20 * m + i + 1)
                    if nxt:
                        dve.wait_ge(S(f"h_out{i % HB}"), 16 * (5 * m + i // HB))
                    dst = HS[:, i % HB, :] if nxt else at(i)
                    dve.tensor_tensor(dst, psb[i % HB][:], brd[:, par, :], ALU.add).then_inc(S("h_ev"), 1)
                    if nxt and i % 5 == 3:
                        lo_w(dve, m + 1, i // 5, Wl[:, 1 - par, i // 5, :], Wh[:, 1 - par, i // 5, :])

            dve.wait_ge(S("t_init"), 16)
            ops = sort_ops()
            h_matrix(0, 0, between=ops)
            h_matrix(0, 1, between=ops)
            assert next(ops, None) is None
            with dve.Fori(1, NREL // 2) as mj:
                h_matrix(mj, 0)
                h_matrix(mj, 1)
            dve.wait_ge(S("xn_out"), 64)
            h_matrix(NREL // 2, 0, nxt=False)
            for q in range(4):
                for k in range(KC):
                    lo_w(dve, WQ + q, k, mw(xTl, q, k), mw(xTh, q, k))
            dve.memset(UM[:, 15, :], 0.0)
            dve.memset(ltri[:], 0.0).then_inc(S("zeros"), 1)
            dve.wait_ge(S("t_in"), 16)
            ch(dve.tensor_copy(loc[:, :, 1], tbl[:, :, 1]))
            dve.wait_ge(S("rs2"), 1)
            dve.wait_ge(S("mb_in"), 32)

            def st_step(it, s):
                st = SPI * it + s
                dve.wait_ge(S("st_pe"), st + 3)
                dve.tensor_scalar(ohr[:, s % 2, :], iotaf[:], loc[:, bass.ds(2 * st, 1), 1], None, ALU.is_equal)
                dve.tensor_scalar(ohf[:, s % 2, :], iotaf[:], loc[:, bass.ds(2 * st + 1, 1), 1], None, ALU.is_equal)
                dve.wait_ge(S("st_hi"), st + 1)
                dve.tensor_tensor(spl[:, s % 2, :], G[:, 2 * (s % 4), :], sph[:, s % 2, :].bitcast(F32),
                                  ALU.subtract).then_inc(S("st_lo"), 1)

            def st_add(it, s):
                st = SPI * it + s
                col = dve.value_load(stoff[0:1, bass.ds(st, 1)], min_val=0, max_val=(NT - 1) * D)
                dve.wait_ge(S("st_pe"), 4 + st + 1)
                dve.wait_ge(S("st_ev"), 2 + st)
                dve.tensor_tensor(acc[:, bass.ds(col, D)], psb[s % 2][:], acc[:, bass.ds(col, D)], ALU.add).then_inc(S("st_ev"), 1)

            def z_part(i, tile):
                dve.wait_ge(S("z_in"), 16 * (i + 1))
                dve.tensor_scalar(zz, zb, mv2[:, bass.ds(tile, 1), 0], rs2[:, bass.ds(tile, 1)],
                                  ALU.subtract, ALU.mult).then_inc(S("m_z"), 1)

            def xm_lo(i):
                dve.wait_ge(S("m_hi"), C1 + i + 1)
                dve.tensor_tensor(mxs(xTl, 0), xmf, mxs(xTh, 0).bitcast(F32), ALU.subtract).then_inc(S("m_lo"), 1)

            def agg(it, hooks):
                for s in range(SPI):
                    if s in hooks:
                        hooks[s]()
                    st_step(it, s)
                    if s:
                        st_add(it, s - 1)
                if "end" in hooks:
                    hooks["end"]()
                st_add(it, SPI - 1)
                if "post" in hooks:
                    hooks["post"]()

            with dve.Fori(0, NT) as it:
                def kv_in():
                    dve.wait_ge(S("m_k"), C1 + it + 1)
                    dve.wait_ge(S("m_kv"), C1 + it)
                    dve.tensor_tensor(kt, psb[2][:], brd[:, 0, :], ALU.add).then_inc(S("m_k2"), 1)
                    dve.wait_ge(S("m_p1"), C1 + it + 1)
                    dve.tensor_tensor(vt, psb[3][:], brd[:, 1, :], ALU.add).then_inc(S("m_v"), 1)

                def kp():
                    dve.wait_ge(S("m_e"), it + 1)
                    dve.scalar_tensor_tensor(kt, kE, 1.0, kR, ALU.min, ALU.add).then_inc(S("m_k3"), 1)

                agg(it, {0: lambda: z_part(it, it), 4: lambda: xm_lo(it), 6: kv_in, "end": kp})

            dve.wait_ge(S("m_kv"), C1 + NT)
            ch(dve.memset(kvs[:, :, :], 0.0))
            for h in range(2):
                r = slice(64 * h, 64 * h + 64)
                for half, b in ((0, 5), (1, 6)):
                    a = dve.tensor_copy(kvs[r, :, half * P + 64 * h:half * P + 64 * h + 64],
                                        psb[b][r, :].rearrange("p (k c) -> p k c", k=KC)[:, :, 64 * h:64 * h + 64])
            a.then_inc(S("kvs_ok"), 1)
            ch(dve.tensor_reduce(isum[:], ins_s[:], AX.X, ALU.add))
            ch(dve.tensor_scalar(isum[:], isum[:], 1.0 / NI, None, ALU.mult))
            for k in range(KC):
                a = dve.tensor_scalar(isb[:, k, :], ones[:], isum[:, k:k + 1], None, ALU.mult)
            a.then_inc(S("ib_ok"), 1)
            ch(dve.tensor_copy(gth[:], rmg[:, :, 0:NX]))
            dve.tensor_tensor(gtl[:], rmg[:, :, 0:NX], gth[:].bitcast(F32), ALU.subtract)
            dve.wait_ge(S("rg_pe"), 1)
            dve.tensor_copy(rg[:], psb[2][:, 0:2 * NX])
            dve.tensor_copy(g8[:], psb[3][0:NX, 0:2]).then_inc(S("rg_ok"), 1)
            with dve.Fori(0, IT - 2 * NT) as jt:
                dve.wait_ge(S("bw_used"), 2 + SPI * jt)
                for s in range(SPI):
                    a = dve.tensor_scalar(ibr[:, s, :], id8[:, bass.ds(2 * jt + s // KC, 1), :].rearrange("p a e -> p (a e)"),
                                          isum[:, s % KC:s % KC + 1], None, ALU.mult)
                a.then_inc(S("ib_e"), 1)
                agg(NT + jt, {})
            dve.wait_ge(S("mb_in"), 64)
            with dve.Fori(0, NT) as jt:
                ch.enter(jt, 4)
                i = NT + jt

                def q_in():
                    dve.wait_ge(S("m_k"), C1 + i + 1)
                    dve.wait_ge(S("z_out"), C16 + 16 * jt)
                    dve.tensor_tensor(kt, psb[2][:], brd[:, 0, :], ALU.add).then_inc(S("m_k2"), 1)

                def qp():
                    dve.wait_ge(S("m_e"), i + 1)
                    dve.scalar_tensor_tensor(kt, kE, 1.0, kR, ALU.min, ALU.add).then_inc(S("m_k3"), 1)

                def o_f():
                    dve.wait_ge(S("o_pe"), jt + 1)
                    ch(dve.tensor_scalar(kR, psb[6][:], EPSN, None, ALU.add))
                    ch(dve.reciprocal(kR, kR))
                    dve.tensor_tensor(xmf, psb[5][:], kR, ALU.mult).then_inc(S("o_f"), 1)

                def o_lo():
                    dve.wait_ge(S("o_hi"), jt + 1)
                    dve.tensor_tensor(mxs(xTl, 1), xmf, mxs(xTh, 1).bitcast(F32), ALU.subtract).then_inc(S("o_lo"), 1)

                def y():
                    dve.wait_ge(S("o_p"), jt + 1)
                    ch(dve.tensor_tensor(kt, psb[3][:], brd[:, 1, :], ALU.add))
                    ch(dve.tensor_tensor(kt, kt, zb, ALU.add))
                    dve.wait_ge(S("xb_in"), 16 * (jt + 1))
                    dve.tensor_tensor(kt, kt, xb, ALU.add).then_inc(S("m_y"), 1)

                agg(IT - NT + jt, {0: lambda: z_part(i, jt), 2: lambda: xm_lo(i), 4: q_in, 5: qp, 7: o_f,
                                   "end": o_lo, "post": y})
                ch.leave(NT)
            dve.wait_ge(S("eb_in"), 16)
            dve.wait_ge(S("bw_used"), 2 + NX * KC)
            dve.scalar_tensor_tensor(bb[0:NX, :], eb[0:NX, :], g8[:, 0:1], psb[7][0:NX, :], ALU.mult, ALU.add).then_inc(S("bb_ok"), 1)

            def lo_x(e, k):
                lo_w(dve, WX + e, k, Wl[:, e % 2 if isinstance(e, int) else pr, k, :],
                     Wh[:, e % 2 if isinstance(e, int) else pr, k, :])

            for k in range(KC):
                lo_x(0, k)

            def x_part(i):
                dve.wait_ge(S(f"f_in{i % HB}"), 16 * (i // HB + 1))
                a = dve.scalar_tensor_tensor(at(i), at(i), 0.0, HS[:, i % HB, :], ALU.max, ALU.add)
                a.then_inc(S("f_x1"), 1)
                dve.wait_ge(S("f_x1"), i + 1)
                ch(dve.bn_stats(stn[:, 0, :], at(i)))
                ch(dve.bn_aggr(mv[:, i, :], stn[:, 0, :]))
                dve.tensor_scalar(ve[:, i:i + 1], mv[:, i, 1:2], EPS, None, ALU.add).then_inc(S("f_ve"), 1)

            def n_part(i):
                dve.wait_ge(S("f_rs"), i + 1)
                dve.tensor_scalar(G[:, i % 2, :], at(i), mv[:, i, 0:1], rs[:, i:i + 1], ALU.subtract, ALU.mult).then_inc(S("f_z"), 1)

            def t_lo(i):
                dve.wait_ge(S("f_hi"), i + 1)
                dve.tensor_tensor(xt3(xTl, i), psb[4 + i % 2][:].rearrange("p (k c) -> p k c", k=KC),
                                  xt3(xTh, i).bitcast(F32), ALU.subtract).then_inc(S("f_lo"), 1)

            def route(i):
                dve.wait_ge(S("f_gt"), i + 1)
                ch(dve.tensor_tensor(rt[:, 0, :], psb[6][:, 0:NX], rg[:, 0:NX], ALU.add))
                dve.tensor_reduce(rt[:, 1, 0:1], rt[:, 0, :], AX.X, ALU.max, negate=True).then_inc(S("f_lg"), 1)
                dve.wait_ge(S("f_ex"), i + 1)
                ch(dve.reciprocal(rt[:, 3, 0:1], rt[:, 1, 1:2]))
                ch(dve.tensor_scalar(rt[:, 4, :], rt[:, 2, :], rt[:, 3, 0:1], None, ALU.mult))
                pj = rt[:, 4:5, :].to_broadcast([P, NX, NX])
                pe_ = rt[:, 4, :].unsqueeze(2).to_broadcast([P, NX, NX])
                dve.tensor_tensor(rtg[:, 0, :, :], pj, pe_, ALU.is_gt)
                ch(dve.tensor_tensor(rtg[:, 1, :, :], pj, pe_, ALU.is_equal))
                ch(dve.tensor_tensor(rtg[:, 1, :, :], rtg[:, 1, :, :], tri8[:], ALU.mult))
                ch(dve.tensor_tensor(rtg[:, 0, :, :], rtg[:, 0, :, :], rtg[:, 1, :, :], ALU.add))
                ch(dve.tensor_reduce(rt[:, 5, :], rtg[:, 0, :, :], AX.X, ALU.add))
                dve.scalar_tensor_tensor(rc(i), rt[:, 5, :], 2.0, rt[:, 4, :], ALU.is_lt, ALU.mult).then_inc(S("f_c"), 1)
                dve.wait_ge(S("f_c"), i + 1)
                ch(dve.tensor_tensor(cgm[:, :].rearrange("p (e i) -> p e i", i=NT)[:, :, i], rc(i), rg[:, NX:2 * NX], ALU.mult))

            def bias_add(i):
                dve.wait_ge(S("f_c1"), i + 1)
                dve.tensor_copy(cT[0:NX, 0:P], psb[7][0:NX, 0:P]).then_inc(S("f_ct"), 1)
                dve.wait_ge(S("f_b"), i + 1)
                dve.tensor_tensor(at(i), at(i), psb[7][:], ALU.add).then_inc(S("f_b2"), 1)

            def x_add(e, i):
                dve.wait_ge(S("x_pe"), NT * e + i + 1)
                c = e * NT + i
                dve.scalar_tensor_tensor(at(i), psb[i % HB][:], cgm[:, bass.ds(c, 1)], at(i), ALU.mult, ALU.add).then_inc(S("x_ev"), 1)

            x_part(0)
            n_part(0)
            for i in range(NT):
                if i + 1 < NT:
                    x_part(i + 1)
                t_lo(i)
                if i + 1 < NT:
                    n_part(i + 1)
                route(i)
                if i:
                    bias_add(i - 1)
                    dve.wait_ge(S("f_b2"), i)
                    x_add(0, i - 1)
                if i % 5 == 4:
                    lo_x(1, i // 5)
            bias_add(NT - 1)
            dve.wait_ge(S("f_b2"), NT)
            x_add(0, NT - 1)

            def expert(e, par, nxt=True):
                dve.wait_ge(S("x_ev"), HB + NT * e)
                for i in range(NT):
                    x_add(e, i)
                    if nxt and i % 5 == 3:
                        k = i // 5
                        lo_w(dve, WX + e + 1, k, Wl[:, 1 - par, k, :], Wh[:, 1 - par, k, :])

            with dve.Fori(0, (NX - 2) // 2) as j:
                expert(2 * j + 1, 1)
                expert(2 * j + 2, 0)
            expert(NX - 1, 1, nxt=False)


def kernel(x, src, dst, edge_type_8, L0_gnn_W_self, L0_gnn_b_self, L0_gnn_W_rel, L0_gnn_b_rel, L0_mix_qkv_w,
           L0_mix_qkv_b, L0_mix_out_w, L0_mix_out_b, L0_mix_ln_gamma, L0_mix_ln_beta, L0_ffn_Ins_tk, L0_ffn_gate_w,
           L0_ffn_expert_w, L0_ffn_expert_b, L0_ffn_gamma_w, L0_ffn_beta_w, L0_ffn_rmod_w):
    import numpy as np
    import concourse.bacc as bacc
    from concourse.bass_utils import run_bass_kernel_spmd as run

    A = np.asarray
    w_all = np.concatenate([
        A(L0_gnn_W_rel).transpose(0, 2, 1), A(L0_gnn_W_self).T[None],
        A(L0_mix_qkv_w).reshape(3, D, D).transpose(0, 2, 1), A(L0_mix_out_w).T[None], A(L0_ffn_expert_w)])
    b_all = np.concatenate([A(L0_gnn_b_rel), A(L0_gnn_b_self)[None], A(L0_mix_qkv_b).reshape(3, D),
                            A(L0_mix_out_b)[None], A(L0_ffn_expert_b)])

    def by_k(a):
        return A(a).reshape(KC, P, -1).transpose(1, 0, 2)

    ins = {
        "x": A(x), "src": A(src), "dst": A(dst), "et": A(edge_type_8),
        "w_all": w_all.reshape(-1, D, D), "b_all": b_all,
        "gam_col": A(L0_mix_ln_gamma).reshape(KC, P).T, "bet_col": A(L0_mix_ln_beta).reshape(KC, P).T,
        "insT": by_k(A(L0_ffn_Ins_tk)[0].T), "gate": by_k(L0_ffn_gate_w), "rmod": by_k(L0_ffn_rmod_w),
        "gamw": by_k(A(L0_ffn_gamma_w).T), "betw": A(L0_ffn_beta_w).reshape(NX * D, D),
    }
    ins = {k: np.ascontiguousarray(v) for k, v in ins.items()}
    nc = bacc.Bacc("TRN2", target_bir_lowering=False, num_devices=1)
    aps = [nc.dram_tensor(f"in_{k}", v.shape, mybir.dt.from_np(v.dtype), kind="ExternalInput").ap() for k, v in ins.items()]
    out = nc.dram_tensor("out_0", (N, D), F32, kind="ExternalOutput").ap()
    h_d = nc.dram_tensor("h_scratch", (NREL * NPAD, D), F32, kind="Internal").ap()
    xn_d = nc.dram_tensor("xn_scratch", (NPAD, D), F32, kind="Internal").ap()
    z_d = nc.dram_tensor("z_scratch", (NPAD, D), F32, kind="Internal").ap()
    tab_d = nc.dram_tensor("table_scratch", (GT * P, 2), I32, kind="Internal").ap()
    build(nc, *aps, out, h_d, xn_d, z_d, tab_d)
    r = run(nc, [{f"in_{k}": v for k, v in ins.items()}], core_ids=[0])
    return r.results[0]["out_0"]
```

```python
from contextlib import ExitStack

import concourse.bass as bass
from concourse import mybir

F32 = mybir.dt.float32
F32R = mybir.dt.float32r
I32 = mybir.dt.int32
ALU = mybir.AluOpType
ACT = mybir.ActivationFunctionType
AX = mybir.AxisListType

P = 128
N = 2500
NT = 20
NPAD = NT * P
D = 512
KC = D // P
R = 8
NREL = 2 * R
E = 42500
ECOL = E // P
ETAIL = E - ECOL * P
EC = ECOL + 1
MC = 2 * EC
ST = (MC * P - NT) // (2 * P) + NT
GT = 2 * ST
IT = 44
SPI = ST // IT
SCH = 9
NX = 8
NI = 16
EPS = 1e-5
EPSN = 1e-8
HB = 4
GB = 8
assert SPI * IT == ST and MC % (2 * SCH) == 0

SELF, WQ, WK, WV, WO, WX = 16, 17, 18, 19, 20, 21


def build(nc, x, src, dst, et, w_all, b_all, gam_col, bet_col, insT, gate, rmod, gamw, betw, out,
          h_d, xn_d, z_d, tab_d):
    with ExitStack() as ctx:
        def sb(name, shape, dt=F32):
            return ctx.enter_context(nc.sbuf_tensor(name, shape, dt))

        sems = {}

        def sem(name):
            if name not in sems:
                sems[name] = ctx.enter_context(nc.semaphore(name))
            return sems[name]

        xTh = sb("xTh", [P, KC * NPAD], F32R)
        xTl = sb("xTl", [P, KC * NPAD], F32R)
        acc = sb("acc", [P, NT * D])
        with nc.sbuf_tensor("Wh", [P, 2, KC, D], F32R) as Wh, nc.sbuf_tensor("Wl", [P, 2, KC, D], F32R) as Wl:
            pass
        UM = sb("UM", [P, 16, D])
        G = sb("G", [P, GB, D])
        with nc.sbuf_tensor("sph", [P, 2, D], F32R) as sph, nc.sbuf_tensor("spl", [P, 2, D], F32R) as spl:
            pass
        msg = sb("msg", [P, 4 * D], I32)
        HS = sb("HS", [P, HB, D])
        Wraw = sb("Wraw", [P, 2, D])
        brd = sb("brd", [P, 2, D])
        tbl = sb("tbl", [P, GT, 2], I32)
        ident = sb("ident", [P, P])
        iotaf = sb("iotaf", [P, P])
        ltri = sb("ltri", [P, P])
        ones = sb("ones", [P, P])
        ohr = sb("ohr", [P, 2, P], F32R)
        ohf = sb("ohf", [P, 2, P])
        idxr = sb("idxr", [P, 2, 8], I32)
        scr_i = sb("scr_i", [P, 2, SCH], I32)
        scr_v = sb("scr_v", [P, 2, SCH, 2], I32)
        stn = sb("stn", [P, 5, 6])
        mv = sb("mv", [P, NT, 2])
        ve = sb("ve", [P, NT])
        rs = sb("rs", [P, NT])
        mv2 = sb("mv2", [P, NT, 2])
        ve2 = sb("ve2", [P, NT])
        rs2 = sb("rs2", [P, NT])
        mhalf = sb("mhalf", [P, NT])
        nb2 = sb("nb2", [P, NT])
        nb = sb("nb", [P, NT])
        vbias = sb("vbias", [P, NT])
        cnt = sb("cnt", [P, NT])
        nsti = sb("nsti", [P, NT], I32)
        nst = sb("nst", [P, NT])
        excl = sb("excl", [P, NT])
        off = sb("off", [P, NT])
        stoff = sb("stoff", [1, ST], I32)
        gcol = sb("gcol", [P, KC])
        bcol = sb("bcol", [P, KC])
        ins_s = sb("ins_s", [P, KC, NI])
        isum = sb("isum", [P, KC])
        rmg = sb("rmg", [P, KC, 3 * NX])
        gth = sb("gth", [P, KC, NX], F32R)
        gtl = sb("gtl", [P, KC, NX], F32R)
        rg = sb("rg", [P, 2 * NX])
        cgm = sb("cgm", [P, NX * NT])
        rt = sb("rt", [P, 16, NX])
        rtg = brd[:, 0, :].rearrange("p (t a e f) -> p t a e f", t=4, a=2, e=NX)
        rtk = brd[:, 1, 0:4 * NX].rearrange("p (t e) -> p t e", t=4)
        tri8 = sb("tri8", [P, NX, NX])

        id8 = sb("id8", [P, NX, NX])
        g8 = sb("g8", [NX, 2])
        psb = [ctx.enter_context(nc.psum_tensor(f"ps{i}", [P, D], F32)) for i in range(8)]

        zb, zz, xmf, kt, vt, kE, kR, kb = (UM[:, i, :] for i in range(8))
        kvs = UM[:, 8, :].rearrange("p (k c) -> p k c", k=KC)
        ks2 = UM[:, 9, 0:2 * KC].rearrange("p (k c) -> p k c", c=2)
        nrm = UM[:, 9, 16:32]
        on = UM[:, 4, :]
        bw = UM[:, 10:12, :]
        yb, yo = UM[:, 10, :], UM[:, 11, :]
        qT = UM[:, 15, :]
        bb = HS[:, 3, :]
        eb = UM[:, 13, :]
        ibr = UM[:, 12, 0:SPI * NX].rearrange("p (s e) -> p s e", e=NX)
        isb = UM[:, 14, :].rearrange("p (k c) -> p k c", k=KC)
        cT = G[:, 6, :]

        gf = G[:, :, :].rearrange("p a b -> p (a b)")
        bk, msk, scn, pos, tmp = (gf[:, i * MC:(i + 1) * MC] for i in range(5))
        spf = gf[:, 5 * MC:5 * MC + 2 * ST]
        eI = UM[:, 12:14, :].rearrange("p a b -> p (a b)").bitcast(I32)[:, 0:3 * EC].rearrange("p (a b) -> p a b", a=3)
        pay = msg[:, 0:2 * MC].rearrange("p (t c) -> p t c", c=2)
        adr = msg[:, 2 * MC:3 * MC]
        loc = tbl[:, :, :].bitcast(F32)

        def schedule(eng, step):
            with eng.Fori(0, 3) as it:
                step(it, W=it)
            step(3, W=3, A=0)
            step(4, A=1, L=0, B=0)
            with eng.Fori(5, 23) as it:
                step(it, A=it - 3, L=it - 4, B=it - 4, C=it - 5)
            step(23, A=20, L=19, B=19, C=18)
            step(24, A=21, L=20, C=19, Q=0)
            with eng.Fori(25, 43) as it:
                step(it, A=it - 3, L=it - 4, Q=it - 24, O=it - 25)
            step(43, L=39, Q=19, O=18)

        def second(it, Q):
            return Q is not None or isinstance(it, int) and it == 23

        def xt(T, k, i):
            return T[:, k * NPAD + i * P:k * NPAD + (i + 1) * P]

        def xt3(T, i):
            return T[:, :].rearrange("p (k n) -> p k n", k=KC)[:, :, i * P:(i + 1) * P]

        def mw(T, q, k):
            return T[:, (q * KC + k) * D:(q * KC + k + 1) * D]

        def mx(T, s, k):
            o = 4 * KC * D + s * D + k * P
            return T[:, o:o + P]

        def mxs(T, s):
            o = 4 * KC * D + s * D
            return T[:, o:o + D]

        def rc(i):
            return rt[:, 8 + i % 4, :]

        def at(i):
            return acc[:, i * D:(i + 1) * D]

        S = sem
        CE = HB
        C1, C16 = 1, 16
        wsrc = w_all.rearrange("m (k p) n -> (m k) p n", p=P)

        class Chain:

            def __init__(self, eng, name):
                self.eng, self.sem, self.n, self.base = eng, sem(name), 0, 0

            def __call__(self, ins):
                ins.then_inc(self.sem, 1)
                self.n += 1
                self.eng.wait_ge(self.sem, self.base + self.n)

            def enter(self, i, per):
                self.n0, self.per, self.keep = self.n, per, self.base
                self.base = self.base + i * per

            def leave(self, steps):
                assert self.n - self.n0 == self.per, (self.n - self.n0, self.per)
                self.base = self.keep
                self.n = self.n0 + steps * self.per

        def load_w(sp, q, k):
            sp.wait_ge(S("w_lo"), 4 * q + k + 1)
            row = wsrc[4 * q + k] if isinstance(q, int) else wsrc[bass.ds(4 * q + k, 1)].rearrange("a p n -> (a p) n")
            sp.dma_start(Wraw[:, k % 2, :], row).then_inc(S(f"w_raw{k % 2}"), 16)

        def hi_w(act, q, k, dst):
            act.wait_ge(S(f"w_raw{k % 2}"), 16 * (2 * q + k // 2 + 1))
            act.activation(dst, Wraw[:, k % 2, :], ACT.Copy).then_inc(S("w_hi"), 1)

        def lo_w(dve, q, k, dst, hi):
            dve.wait_ge(S("w_hi"), 4 * q + k + 1)
            dve.tensor_tensor(dst, Wraw[:, k % 2, :], hi.bitcast(F32), ALU.subtract).then_inc(S("w_lo"), 1)

        block = ctx.enter_context(nc.Block())

        @block.sync
        def _(sp):
            for j, v in enumerate((src, dst, et)):
                sp.dma_start(eI[:, j, 0:ECOL], v[0:ECOL * P].rearrange("(p c) -> p c", p=P)).then_inc(S("e_in"), 16)
            sp.wait_ge(S("e_dummy"), 3)
            for j, v in enumerate((src, dst, et)):
                sp.dma_start(eI[0:ETAIL, j, ECOL:EC], v[ECOL * P:E].rearrange("(p c) -> p c", c=1)).then_inc(S("e_in"), 16)
            for g in range(4):
                a, b = 5 * g, min(5 * g + 5, NT - 1)
                sp.dma_start(acc[:, a * D:b * D].rearrange("p (i d) -> p i d", d=D),
                             x[a * P:b * P, :].rearrange("(i p) d -> p i d", p=P)).then_inc(S(f"x_in{g}"), 16)
            sp.wait_ge(S("x_pad"), 1)
            sp.dma_start(acc[0:N - (NT - 1) * P, (NT - 1) * D:NT * D], x[(NT - 1) * P:N, :]).then_inc(S("x_in3"), 16)
            for k in range(2):
                load_w(sp, 0, k)
            sp.dma_start(brd[:, 0, :], b_all[0:1, :].to_broadcast([P, D])).then_inc(S("b_in0"), 16)
            sp.wait_ge(S("t_fill"), 2)
            sp.dma_start(tab_d.rearrange("(p t) c -> p (t c)", p=P),
                         HS[:, :, :].rearrange("p a b -> p (a b)")[:, 0:2 * GT].bitcast(I32)).then_inc(S("t_init"), 16)
            for k in range(2, KC):
                load_w(sp, 0, k)
            for ap, v in ((gcol, gam_col), (bcol, bet_col), (ins_s, insT)):
                sp.dma_start(ap[:], v).then_inc(S("c_in"), 16)
            for j, v in enumerate((gate, rmod, gamw)):
                sp.dma_start(rmg[:, :, j * NX:(j + 1) * NX], v).then_inc(S("c_in"), 16)
            for g in range(4):
                sp.wait_ge(S("xn_ok"), g + 1)
                sp.dma_start(xn_d[5 * g * P:(5 * g + 5) * P, :].rearrange("(i p) d -> p i d", p=P),
                             acc[:, 5 * g * D:(5 * g + 5) * D].rearrange("p (i d) -> p i d", d=D)).then_inc(S("xn_out"), 16)

            def h_matrix(m, par, more=None):
                for k in range(2):
                    load_w(sp, m + 1, k)
                sp.wait_ge(S("h_ev"), CE + 20 * m)
                sp.dma_start(brd[:, 1 - par, :], b_all[bass.ds(m + 1, 1), :].to_broadcast([P, D])).then_inc(S(f"b_in{1 - par}"), 16)
                for i in range(NT):
                    sp.wait_ge(S("h_ev"), CE + 20 * m + i + 1)
                    sp.dma_start(h_d[bass.ds((m * NT + i) * P, P), :], HS[:, i % HB, :]).then_inc(S(f"h_out{i % HB}"), 16)
                    if i in (6, 12):
                        load_w(sp, m + 1, 2 + (i == 12))
                    if more:
                        more(i)

            def load_x(i):
                rows = min(P, N - i * P)
                sp.dma_start(G[0:rows, i % 4, :], x[i * P:i * P + rows, :]).then_inc(S(f"xr{i % 4}"), 16)

            def residual(i):
                sp.wait_ge(S("res"), i + 1)
                sp.dma_start(z_d[i * P:(i + 1) * P, :], G[:, i % 4, :]).then_inc(S(f"r_out{i % 4}"), 16)
                if 2 <= i < NT - 2:
                    sp.wait_ge(S(f"r_out{(i + 2) % 4}"), 16 * ((i - 2) // 4 + 1))
                    load_x(i + 2)

            for m in range(3):
                h_matrix(m, m % 2)
            sp.wait_ge(S("ve2"), 1)
            sp.dma_start(G[:, 7, :], b_all[WO:WO + 1, :].to_broadcast([P, D])).then_inc(S("xrb"), 16)
            for i in range(4):
                load_x(i)
            h_matrix(3, 1, residual)
            with sp.Fori(2, NREL // 2) as j:
                h_matrix(2 * j, 0)
                h_matrix(2 * j + 1, 1)
            for h in range(2):
                sp.wait_ge(S(f"sc{h}"), 16 * SCH * (MC // SCH // 2))
            sp.dma_start(tbl[:, :, :].rearrange("p t c -> p (t c)"), tab_d.rearrange("(p t) c -> p (t c)", p=P)).then_inc(S("t_in"), 16)
            sp.wait_ge(S("h_ev"), CE + 20 * (NREL + 1))
            for j, m in enumerate((WK, WV)):
                sp.dma_start(brd[:, j, :], b_all[m:m + 1, :].to_broadcast([P, D])).then_inc(S("mb_in"), 16)
            sp.dma_start(eb[0:NX, :], b_all[WX:WX + NX, :]).then_inc(S("eb_in"), 16)
            sp.wait_ge(S("xn_out"), 64)
            for s in range(4):
                sp.wait_ge(S(f"r_out{s}"), 16 * NT // 4)

            def step(it, W=None, A=None, L=None, B=None, C=None, Q=None, O=None):
                if A is not None:
                    sp.wait_ge(S("m_z"), C1 + A)
                    tile = A - NT if second(it, Q) else A
                    sp.dma_start(zb, xn_d[bass.ds(tile * P, P), :]).then_inc(S("z_in"), 16)
                if W is not None:
                    for s in range(SPI):
                        sp.wait_ge(S("bw_used"), SPI * W + s + 1)
                        sp.dma_start(bw[:, s % 2, :], betw[bass.ds((SPI * W + s) * P, P), :]).then_inc(S(f"bw_in{s % 2}"), 16)
                        if s % 2:
                            load_w(sp, W + WQ, s // 2)
                if isinstance(it, int) and it == 24:
                    sp.wait_ge(S("m_k2"), NT)
                    sp.dma_start(brd[:, 0, :], b_all[WQ:WQ + 1, :].to_broadcast([P, D])).then_inc(S("mb_in"), 16)
                if O is not None:
                    out_tile(O)

            def out_tile(O):
                sp.wait_ge(S("m_y"), C1 + O)
                sp.dma_start(yb, z_d[bass.ds(O * P, P), :]).then_inc(S("y_in"), 16)
                sp.wait_ge(S("m_y"), C1 + O + 1)
                sp.dma_start(z_d[bass.ds(O * P, P), :], yo).then_inc(S("z_out"), 16)

            schedule(sp, step)
            out_tile(NT - 1)
            sp.wait_ge(S("z_out"), C16 + 16 * NT)
            for k in range(2):
                load_w(sp, WX, k)
            for i in range(3):
                sp.dma_start(HS[:, i % 3, :], z_d[i * P:(i + 1) * P, :]).then_inc(S(f"f_in{i % 3}"), 16)
            for k in range(2, KC):
                load_w(sp, WX, k)
            for k in range(2):
                load_w(sp, WX + 1, k)
            for i in range(3, NT):
                sp.wait_ge(S("f_x1"), i - 2)
                sp.dma_start(HS[:, i % 3, :], z_d[i * P:(i + 1) * P, :]).then_inc(S(f"f_in{i % 3}"), 16)
                if i in (15, 19):
                    load_w(sp, WX + 1, 2 + (i == 19))
            with sp.Fori(0, NX - 2) as e:
                for k in range(KC):
                    load_w(sp, WX + 2 + e, k)
            for i in range(NT):
                rows = min(P, N - i * P)
                sp.wait_ge(S("x_ev"), CE + NT * NX + i + 1)
                sp.dma_start(out[i * P:i * P + rows, :], acc[0:rows, i * D:(i + 1) * D]).then_inc(S("out_ok"), 16)
            sp.wait_ge(S("out_ok"), 16 * NT)

        @block.gpsimd
        def _(pool):
            ch = Chain(pool, "pool_ch")

            def waited():
                pool.sem_inc(S("pool_waited"), 1)

            pool.memset(eI[:, 0:2, ECOL:EC], NPAD - 1).then_inc(S("e_dummy"), 2)
            pool.memset(eI[:, 2:3, ECOL:EC], 0).then_inc(S("e_dummy"), 1)
            pool.wait_ge(S("e_dummy"), 3)
            pool.memset(acc[64:P, (NT - 1) * D:NT * D], 0.0).then_inc(S("x_pad"), 1)
            pool.wait_ge(S("x_pad"), 1)
            ch(pool.memset(ltri[:], 1.0))
            pool.affine_select(out=ltri[:], in_=ltri[:], compare_op=ALU.is_gt, fill=0.0, base=0,
                               pattern=[[1, P]], channel_multiplier=-1)
            pool.memset(ones[:], 1.0).then_inc(S("k_cst"), 1)
            ch(pool.memset(ident[:], 0.0))
            pool.affine_select(out=ident[:], in_=ident[:], compare_op=ALU.not_equal, fill=1.0, base=0,
                               pattern=[[-1, P]], channel_multiplier=1).then_inc(S("k_id"), 1)
            hs = HS[:, :, :].rearrange("p a b -> p (a b)")[:, 0:2 * GT].bitcast(I32).rearrange("p (t c) -> p t c", c=2)
            pool.memset(hs[:, :, 0:1], 0).then_inc(S("t_fill"), 1)
            pool.memset(hs[:, :, 1:2], -1).then_inc(S("t_fill"), 1)
            pool.iota(iotaf[:], pattern=[[1, P]], base=0, channel_multiplier=0,
                      allow_small_or_imprecise_dtypes=True).then_inc(S("k_iota"), 1)
            pool.iota(spf[0:1, 0:ST], pattern=[[1, ST]], base=0, channel_multiplier=0,
                      allow_small_or_imprecise_dtypes=True).then_inc(S("k_iota"), 1)
            pool.memset(mhalf[:], -0.5)
            ch(pool.memset(vbias[:], 0.0))
            pool.affine_select(out=vbias[:, NT - 1:NT], in_=vbias[:, NT - 1:NT], compare_op=ALU.is_gt, fill=-1e30,
                               base=N - (NT - 1) * P, pattern=[[0, 1]], channel_multiplier=-1)
            ch(pool.memset(tri8[:], 1.0))
            pool.affine_select(out=tri8[:], in_=tri8[:], compare_op=ALU.is_gt, fill=0.0, base=0,
                               pattern=[[1, NX], [-1, NX]], channel_multiplier=0)
            ch(pool.memset(id8[:], 0.0))
            pool.affine_select(out=id8[:], in_=id8[:], compare_op=ALU.not_equal, fill=1.0, base=0,
                               pattern=[[1, NX], [-1, NX]], channel_multiplier=0).then_inc(S("k_tri"), 1)
            for g in range(4):
                pool.wait_ge(S("ve"), g + 1)
                pool.tensor_tensor(rs[:, 5 * g:5 * g + 5], ve[:, 5 * g:5 * g + 5], mhalf[:, 0:5], ALU.pow).then_inc(S("rs"), 1)
            pool.wait_ge(S("adr"), 1)
            pool.wait_ge(S("t_init"), 16)
            def scatter(j):
                for h in range(2):
                    c = (2 * j + h) * SCH
                    if not isinstance(j, int):
                        pool.wait_ge(S(f"sc{h}"), 16 * SCH * j)
                        waited()
                    pool.tensor_copy(scr_i[:, h, :], adr[:, bass.ds(c, SCH)])
                    ch(pool.tensor_copy(scr_v[:, h, :, :], pay[:, bass.ds(c, SCH), :]))
                    if not isinstance(j, int):
                        waited()
                    for u in range(SCH):
                        pool.indirect_dma_start(
                            out=tab_d, out_offset=bass.IndirectOffsetOnAxis(ap=scr_i[:, h, u:u + 1], axis=0),
                            in_=scr_v[:, h, u, :], in_offset=None).then_inc(S(f"sc{h}"), 16)

            scatter(0)
            with pool.Fori(1, MC // SCH // 2) as j:
                ch.enter(j - 1, 2)
                scatter(j)
                ch.leave(MC // SCH // 2 - 1)
            pool.wait_ge(S("ve2"), 1)
            pool.tensor_tensor(rs2[:], ve2[:], mhalf[:], ALU.pow).then_inc(S("rs2"), 1)
            pool.wait_ge(S("t_in"), 16)
            for h in range(HB):
                pool.wait_ge(S(f"h_out{h}"), 16 * NREL * NT // HB)
            with pool.Fori(0, IT) as it:
                ch.enter(it, 2)
                for h in range(2):
                    ch(pool.tensor_copy(idxr[:, h, :], tbl[:, bass.ds(16 * it + 8 * h, 8), 0]))
                    for u in range(GB):
                        s = 4 * h + u // 2
                        pool.wait_ge(S("st_pe" if u % 2 else "st_lo"), SPI * it + s + 1)
                        waited()
                        pool.indirect_dma_start(
                            out=G[:, u, :], out_offset=None, in_=h_d,
                            in_offset=bass.IndirectOffsetOnAxis(ap=idxr[:, h, u:u + 1], axis=0)).then_inc(S(f"g_in{u}"), 16)
                ch.leave(IT)
            for g in range(NT // 4):
                pool.wait_ge(S("f_ve"), g + 1)
                pool.tensor_tensor(rs[:, 4 * g:4 * g + 4], ve[:, 4 * g:4 * g + 4], mhalf[:, 0:4], ALU.pow).then_inc(S("f_rs"), 1)

        @block.scalar
        def _(act):
            ch = Chain(act, "act_ch")

            def w_half(q, par, ks=range(KC)):
                for k in ks:
                    hi_w(act, q, k, Wh[:, par, k, :])

            for i in range(NT):
                act.wait_ge(S("t_pe"), i + 1)
                act.activation(xt3(xTh, i), psb[4 + i % 2][:].rearrange("p (k c) -> p k c", k=KC), ACT.Copy).then_inc(S("t_hi"), 1)
                if i in (4, 8, 12, 16):
                    w_half(0, 0, [i // 4 - 1])
            with act.Fori(0, NREL // 2) as j:
                for par in range(2):
                    act.wait_ge(S("h_pe"), C1 + NT * (2 * j + par))
                    w_half(2 * j + par + 1, 1 - par)
            def st_step(it, s):
                st = SPI * it + s
                act.wait_ge(S(f"g_in{2 * (s % 4)}"), 16 * (2 * it + s // 4 + 1))
                act.wait_ge(S("st_pe"), st + 3)
                act.activation(sph[:, s % 2, :], G[:, 2 * (s % 4), :], ACT.Copy).then_inc(S("st_hi"), 1)

            def z_part(A, tile):
                act.wait_ge(S("z_in"), 16 * (A + 1))
                act.wait_ge(S("m_tr"), C1 + A)
                act.activation(zz, zb, ACT.Identity, bias=nb2[:, bass.ds(tile, 1)],
                               scale=rs2[:, bass.ds(tile, 1)]).then_inc(S("m_z"), 1)

            def xm_part(A, last, n):
                act.wait_ge(S("m_tr"), C1 + A + 1)
                act.wait_ge(S("m_lo"), C1 + A)
                for k in range(KC):
                    xa = act.activation(xmf[:, k * P:(k + 1) * P], psb[4][:, k * P:(k + 1) * P], ACT.Identity,
                                        bias=bcol[:, k:k + 1], scale=gcol[:, k:k + 1])
                ch(xa)
                if last:
                    act.wait_ge(S(last), n)
                act.activation(mxs(xTh, 0), xmf, ACT.Copy).then_inc(S("m_hi"), 1)

            def step(it, W=None, A=None, L=None, B=None, C=None, Q=None, O=None):
                if not isinstance(it, int) and A is not None:
                    ch.enter(it - (25 if Q is not None else 5), 1)
                for s in range(SPI):
                    if W is not None and s % 2:
                        k = s // 2
                        c = W * KC + k
                        hi_w(act, W + WQ, k, xTh[:, bass.ds(c * D, D)])
                    if s == 1 and A is not None:
                        z_part(A, A - NT if second(it, Q) else A)
                    if s == 2 and O is not None:
                        o_hi(O)
                    if s == 3 and B is not None:
                        act.wait_ge(S("m_k2"), B + 1)
                        act.activation(kE, kb, ACT.Exp, bias=vbias[:, bass.ds(B, 1)])
                        act.activation(kR, kb, ACT.Relu, bias=vbias[:, bass.ds(B, 1)]).then_inc(S("m_e"), 1)
                    if s == 3 and Q is not None:
                        act.wait_ge(S("m_k2"), NT + Q + 1)
                        act.activation(kE, kb, ACT.Exp)
                        act.activation(kR, kb, ACT.Relu).then_inc(S("m_e"), 1)
                    if s == 5 and A is not None:
                        if second(it, Q):
                            xm_part(A, "m_k", C1 + A) if Q is not None else xm_part(A, "m_p1", C1 + NT)
                        else:
                            xm_part(A, None if isinstance(A, int) and A == 0 else "m_p1", C1 + A)
                    if s == 6 and Q is not None:
                        act.wait_ge(S("q_tr"), Q + 1)
                        act.activation(qT, psb[7][:], ACT.Copy).then_inc(S("q_t"), 1)
                    if s == 7 and B is not None:
                        act.wait_ge(S("m_p1"), C1 + B + 1)
                        act.wait_ge(S("m_kv"), C1 + B)
                        act.activation(vt, psb[3][:], ACT.Copy).then_inc(S("m_v"), 1)
                    st_step(it, s)
                if not isinstance(it, int) and A is not None:
                    ch.leave(18)

            def o_hi(O):
                act.wait_ge(S("o_tr"), O + 1)
                act.wait_ge(S("o_p"), C1 + O)
                act.activation(mxs(xTh, 1), psb[6][:], ACT.Copy).then_inc(S("o_hi"), 1)

            act.wait_ge(S("c_in"), 96)
            act.wait_ge(S("k_tri"), 1)
            act.wait_ge(S("h_pe"), C1 + NT * (NREL + 1))
            act.wait_ge(S("nb2"), 1)
            schedule(act, step)
            o_hi(NT - 1)
            act.wait_ge(S("m_y"), C1 + NT)
            act.wait_ge(S("z_out"), C16 + 16 * NT)
            act.wait_ge(S("bb_ok"), 1)
            w_half(WX, 0)

            def zf(i):
                if i % 4 == 0:
                    act.wait_ge(S("f_nb"), i // 4 + 1)
                if i >= 4:
                    act.wait_ge(S("f_tr"), i - 3)
                act.activation(G[:, i % 4, :], at(i), ACT.Identity, bias=nb[:, i:i + 1], scale=rs[:, i:i + 1]).then_inc(S("f_z"), 1)

            zf(0)
            for i in range(NT):
                if i + 1 < NT:
                    zf(i + 1)
                act.wait_ge(S("f_tr"), i + 1)
                act.activation(xt3(xTh, i), psb[4 + i % 2][:].rearrange("p (k c) -> p k c", k=KC), ACT.Copy).then_inc(S("f_hi"), 1)
                if i % 4 == 3:
                    act.wait_ge(S("f_lg"), i // 4 + 1)
                    act.activation(rt[:, 4:8, :], rt[:, 0:4, :], ACT.Exp).then_inc(S("f_ex"), 1)
                    if i // 4 < 4:
                        w_half(WX + 1, 1, [i // 4])
            for e in range(2, NX):
                act.wait_ge(S("x_pe"), NT * e)
                w_half(WX + e, e % 2)

        @block.tensor
        def _(pe):
            def three(ps, lh, ll, rh, rl, first=True, last=True):
                for k in range(KC):
                    a = pe.matmul(ps, lh(k), rh(k), start=(first and k == 0), stop=False)
                    a = pe.matmul(ps, lh(k), rl(k), start=False, stop=False)
                    a = pe.matmul(ps, ll(k), rh(k), start=False, stop=(last and k == KC - 1))
                return a

            pe.wait_ge(S("k_cst"), 1)
            pe.wait_ge(S("cnt"), NT)
            pe.matmul(psb[7][:, 0:NT], ltri[:], cnt[:], start=True, stop=True)
            pe.matmul(psb[7][:, 32:32 + NT], ones[:], cnt[:], start=True, stop=True).then_inc(S("pre"), 1)
            pe.wait_ge(S("k_id"), 1)
            for i in range(NT):
                if i % 5 == 0:
                    pe.wait_ge(S("xn_ok"), i // 5 + 1)
                if i >= 2:
                    pe.wait_ge(S("t_lo"), i - 1)
                for k in range(KC):
                    a = pe.transpose(psb[4 + i % 2][:, k * P:(k + 1) * P], acc[:, i * D + k * P:i * D + (k + 1) * P], ident[:])
                a.then_inc(S("t_pe"), 1)
            pe.wait_ge(S("t_lo"), NT)

            def h_matrix(m, par):
                pe.wait_ge(S("w_lo"), 2 + 4 * (m + 1))
                for i in range(NT):
                    pe.wait_ge(S("h_ev"), 20 * m + i + 1)
                    three(psb[i % HB][:], lambda k: xt(xTh, k, i), lambda k: xt(xTl, k, i),
                          lambda k: Wh[:, par, k, :], lambda k: Wl[:, par, k, :]).then_inc(S("h_pe"), 1)

            with pe.Fori(0, NREL // 2) as j:
                h_matrix(2 * j, 0)
                h_matrix(2 * j + 1, 1)
            h_matrix(NREL, 0)

            def st_step(it, s):
                st = SPI * it + s
                pe.wait_ge(S("st_ev"), st + 1)
                pe.wait_ge(S("st_lo"), 4 + st + 1)
                ps = psb[s % 2][:]
                pe.matmul(ps, ohr[:, s % 2, :], sph[:, s % 2, :], start=True, stop=False)
                pe.matmul(ps, ohr[:, s % 2, :], spl[:, s % 2, :], start=False, stop=False)
                u = 2 * (s % 4) + 1
                pe.wait_ge(S(f"g_in{u}"), 16 * (2 * it + s // 4 + 1))
                pe.matmul(ps, ohf[:, s % 2, :], G[:, u, :], start=False, stop=True).then_inc(S("st_pe"), 1)

            def proj(ps, s, q, name):
                three(ps, lambda k: mx(xTh, s, k), lambda k: mx(xTl, s, k),
                      lambda k: mw(xTh, q, k), lambda k: mw(xTl, q, k)).then_inc(S(name), 1)

            def o_tr(O):
                pe.wait_ge(S("o_n"), O + 1)
                for k in range(KC):
                    a = pe.transpose(psb[6][:, k * P:(k + 1) * P], on[:, k * P:(k + 1) * P], ident[:])
                a.then_inc(S("o_tr"), 1)

            def o_proj(O):
                pe.wait_ge(S("o_lo"), C1 + O + 1)
                pe.wait_ge(S("m_y"), C1 + O)
                proj(psb[3][:], 1, 3, "o_p")

            def step(it, W=None, A=None, L=None, B=None, C=None, Q=None, O=None):
                if W is not None:
                    pe.wait_ge(S("ib_e"), W + 1)
                for s in range(SPI):
                    if W is not None:
                        pe.wait_ge(S(f"bw_in{s % 2}"), 16 * (SPI // 2 * W + s // 2 + 1))
                        pe.matmul(psb[7][0:NX, :], ibr[:, s, :], bw[:, s % 2, :],
                                  start=False, stop=False, skip_group_check=True).then_inc(S("bw_used"), 1)
                    if s == 1 and B is not None:
                        pe.wait_ge(S("m_lo"), C1 + B + 1)
                        if not (isinstance(B, int) and B == 0):
                            pe.wait_ge(S("m_k2"), B)
                        proj(psb[2][:], 0, 1, "m_k")
                    if s == 1 and Q is not None:
                        pe.wait_ge(S("m_lo"), C1 + NT + Q + 1)
                        pe.wait_ge(S("m_k2"), NT + Q)
                        proj(psb[2][:], 0, 0, "m_k")
                        if O is not None:
                            o_tr(O)
                    if s == 3 and B is not None:
                        pe.wait_ge(S("m_v"), C1 + B)
                        proj(psb[3][:], 0, 2, "m_p1")
                    if s == (3 if Q is not None else 4) and A is not None:
                        pe.wait_ge(S("m_z"), C1 + A + 1)
                        pe.wait_ge(S("m_hi"), C1 + A)
                        for k in range(KC):
                            a = pe.transpose(psb[4][:, k * P:(k + 1) * P], zz[:, k * P:(k + 1) * P], ident[:])
                        a.then_inc(S("m_tr"), 1)
                    if s == 4 and O is not None:
                        o_proj(O)
                    if s == (5 if Q is None else 3) and C is not None:
                        pe.wait_ge(S("m_k3"), C + 1)
                        pe.wait_ge(S("m_v"), C1 + C + 1)
                        for k in range(KC):
                            c = slice(k * P, (k + 1) * P)
                            pe.matmul(psb[5][:, c], kt[:, c], vt[:, c], start=False, stop=False, skip_group_check=True)
                            a = pe.matmul(psb[6][:, c], kt[:, c], ones[:], start=False, stop=False, skip_group_check=True)
                        a.then_inc(S("m_kv"), 1)
                    if s == 5 and Q is not None:
                        pe.wait_ge(S("m_k3"), NT + Q + 1)
                        for k in range(KC):
                            a = pe.transpose(psb[7][:, k * P:(k + 1) * P], kt[:, k * P:(k + 1) * P], ident[:])
                        a.then_inc(S("q_tr"), 1)
                    if s == 7 and Q is not None:
                        pe.wait_ge(S("kvs_ok"), 1)
                        pe.wait_ge(S("q_t"), Q + 1)
                        pe.wait_ge(S("o_lo"), C1 + Q)
                        for k in range(KC):
                            c = slice(k * P, (k + 1) * P)
                            pe.matmul(psb[5][:, c], qT[:, c], kvs[:, k, :], start=(k == 0), stop=(k == KC - 1), skip_group_check=True)
                            a = pe.matmul(psb[6][:, 2 * k:2 * k + 2], qT[:, c], ks2[:, k, :], start=(k == 0), stop=(k == KC - 1), skip_group_check=True)
                        a.then_inc(S("o_pe"), 1)
                    st_step(it, s)

            pe.wait_ge(S("h_ev"), CE + 20 * (NREL + 1))
            pe.wait_ge(S("zeros"), 1)
            for b in (5, 6):
                pe.matmul(psb[b][:], ltri[:], qT, start=True, stop=False, skip_group_check=True)
            pe.matmul(psb[7][0:NX, :], ltri[:, 0:NX], qT, start=True, stop=False, skip_group_check=True)
            pe.wait_ge(S("ib_ok"), 1)
            for k in range(KC):
                pe.matmul(psb[2][:, 0:2 * NX], isb[:, k, :], rmg[:, k, NX:3 * NX], start=(k == 0), stop=(k == KC - 1))
            for k in range(KC):
                a = pe.matmul(psb[3][0:NX, 0:2], rmg[:, k, 2 * NX:3 * NX], isb[:, k, 0:2], start=(k == 0), stop=(k == KC - 1))
            a.then_inc(S("rg_pe"), 1)
            schedule(pe, step)
            o_tr(NT - 1)
            o_proj(NT - 1)
            pe.wait_ge(S("m_y"), C1 + NT)
            pe.wait_ge(S("st_ev"), 2 + ST)
            pe.wait_ge(S("bb_ok"), 1)

            def product(i, par):
                return three(psb[i % HB][:], lambda k: xt(xTh, k, i), lambda k: xt(xTl, k, i),
                             lambda k: Wh[:, par, k, :], lambda k: Wl[:, par, k, :])

            def expert(e, par):
                pe.wait_ge(S("w_lo"), 2 + 4 * (WX + e + 1))
                for i in range(NT):
                    pe.wait_ge(S("x_ev"), NT * (e + 1) + i + 1)
                    product(i, par).then_inc(S("x_pe"), 1)

            def tr_gate(g):
                for i in range(4 * g, 4 * g + 4):
                    pe.wait_ge(S("f_z"), i + 1)
                    if i >= 2:
                        pe.wait_ge(S("f_lo"), i - 1)
                    for k in range(KC):
                        a = pe.transpose(psb[4 + i % 2][:, k * P:(k + 1) * P], G[:, i % 4, k * P:(k + 1) * P], ident[:])
                    a.then_inc(S("f_tr"), 1)
                    if i >= 4 * g + 1:
                        gate_i(i - 1)
                gate_i(4 * g + 3)

            def gate_i(i):
                pe.wait_ge(S("f_lo"), i + 1)
                if i % 4 == 0 and i:
                    pe.wait_ge(S("f_lg"), i // 4)
                j = i % 4
                a = three(psb[6][:, j * NX:(j + 1) * NX], lambda k: xt(xTh, k, i), lambda k: xt(xTl, k, i),
                          lambda k: gth[:, k, :], lambda k: gtl[:, k, :])
                if j == 3:
                    a.then_inc(S("f_gt"), 1)

            tr_gate(0)
            for g in range(NT // 4):
                if g + 1 < NT // 4:
                    tr_gate(g + 1)
                pe.wait_ge(S("f_c"), g + 1)
                for j in range(4):
                    a = pe.transpose(psb[7][0:NX, j * P:(j + 1) * P], rc(4 * g + j), ident[:])
                a.then_inc(S("f_c1"), 1)
                if g == 0:
                    pe.wait_ge(S("w_lo"), 2 + 4 * (WX + 1))
                for i in range(4 * g, 4 * g + 4):
                    pe.wait_ge(S("x_ev"), 2 * i + 1)
                    three(psb[2 * i % HB][:], lambda k: xt(xTh, k, i), lambda k: xt(xTl, k, i),
                          lambda k: Wh[:, 0, k, :], lambda k: Wl[:, 0, k, :]).then_inc(S("x_pe"), 1)
                    pe.wait_ge(S("f_ct"), g + 1)
                    pe.wait_ge(S("x_ev"), 2 * i + 2)
                    pe.matmul(psb[(2 * i + 1) % HB][:], cT[0:NX, (i % 4) * P:(i % 4 + 1) * P], bb[0:NX, :],
                              start=True, stop=True).then_inc(S("x_pe"), 1)
            with pe.Fori(0, (NX - 2) // 2) as j:
                expert(2 * j + 1, 1)
                expert(2 * j + 2, 0)
            expert(NX - 1, 1)

        @block.vector
        def _(dve):
            ch = Chain(dve, "dve_ch")
            dve.sem_inc(S("h_ev"), HB)
            dve.sem_inc(S("x_ev"), HB)
            for name in ("m_tr", "m_y", "h_pe", "m_lo", "m_p1", "m_k", "m_hi", "m_v", "m_kv", "m_z", "o_lo", "o_p"):
                dve.sem_inc(S(name), C1)
            dve.sem_inc(S("z_out"), C16)
            dve.sem_inc(S("w_lo"), 2)
            dve.sem_inc(S("st_ev"), 2)
            dve.sem_inc(S("st_lo"), 4)
            dve.sem_inc(S("bw_used"), 2)
            dve.sem_inc(S("st_pe"), 4)
            dve.wait_ge(S("e_in"), 96)
            T = eI[:, 0:2, :].rearrange("p a b -> p (a b)")
            ti = tmp.bitcast(I32)
            ch(dve.tensor_scalar(ti, T, 7, None, ALU.arith_shift_right))
            ch(dve.tensor_copy(bk, ti))
            dve.tensor_scalar(pay[:, 0:MC, 1], T, P - 1, None, ALU.bitwise_and)
            for b in range(NT):
                dve.tensor_scalar(msk, bk, float(b), None, ALU.is_equal, ALU.add, accum_out=cnt[:, b:b + 1]).then_inc(S("cnt"), 1)
                dve.wait_ge(S("cnt"), b + 1)
            dve.scalar_tensor_tensor(pay[:, 0:EC, 0], eI[:, 2, :], float(NPAD), eI[:, 1, :], ALU.mult, ALU.add)
            ch(dve.tensor_scalar(ti[:, 0:EC], eI[:, 2, :], float(NPAD), float(R * NPAD), ALU.mult, ALU.add))
            dve.tensor_tensor(pay[:, EC:MC, 0], ti[:, 0:EC], eI[:, 0, :], ALU.add)
            ch(dve.memset(pos, 0.0))

            def stats(mvt, g):
                for i in range(5 * g, 5 * g + 5):
                    a = dve.bn_stats(stn[:, i - 5 * g, :], at(i))
                ch(a)
                for i in range(5 * g, 5 * g + 5):
                    a = dve.bn_aggr(mvt[:, i, :], stn[:, i - 5 * g, :])
                ch(a)

            def norm(g):
                dve.wait_ge(S("rs"), g + 1)
                for i in range(5 * g, 5 * g + 5):
                    a = dve.tensor_scalar(at(i), at(i), mv[:, i, 0:1], rs[:, i:i + 1], ALU.subtract, ALU.mult)
                a.then_inc(S("xn_ok"), 1)

            for g in range(4):
                dve.wait_ge(S(f"x_in{g}"), 16 if g < 3 else 32)
                stats(mv, g)
                dve.tensor_scalar(ve[:, 5 * g:5 * g + 5], mv[:, 5 * g:5 * g + 5, 1], EPS, None, ALU.add).then_inc(S("ve"), 1)
                if g:
                    norm(g - 1)
            norm(3)
            dve.wait_ge(S("pre"), 1)
            ch(dve.tensor_scalar(nsti[:], psb[7][:, 32:32 + NT], float(2 * P - 1), None, ALU.add))
            ch(dve.tensor_scalar(nsti[:], nsti[:], 8, None, ALU.arith_shift_right))
            ch(dve.tensor_copy(nst[:], nsti[:]))
            ch(dve.tensor_tensor_scan(excl[:], nst[:], nst[:], 0.0, ALU.add, ALU.max))
            ch(dve.tensor_tensor(excl[:], excl[:], nst[:], ALU.subtract))
            ch(dve.scalar_tensor_tensor(off[:], excl[:], float(2 * P), psb[7][:, 0:NT], ALU.mult, ALU.add))
            ch(dve.tensor_scalar(off[:], off[:], -1.0, None, ALU.add))

            def sort_ops():
                for b in range(NT):
                    yield lambda b=b: ch(dve.tensor_scalar(msk, bk, float(b), None, ALU.is_equal))
                    yield lambda b=b: ch(dve.tensor_tensor_scan(scn, msk, msk, 0.0, ALU.add, ALU.max))
                    yield lambda b=b: ch(dve.scalar_tensor_tensor(tmp, scn, off[:, b:b + 1], msk, ALU.add, ALU.mult))
                    yield lambda b=b: ch(dve.tensor_tensor(pos, pos, tmp, ALU.add))
                si, mi = scn.bitcast(I32), msk.bitcast(I32)
                yield lambda: ch(dve.tensor_copy(si, pos))
                yield lambda: dve.tensor_scalar(mi, si, P - 1, None, ALU.bitwise_and)
                yield lambda: ch(dve.tensor_scalar(ti, si, 7, None, ALU.arith_shift_right))
                yield lambda: dve.scalar_tensor_tensor(adr, mi, float(GT), ti, ALU.mult, ALU.add).then_inc(S("adr"), 1)
                yield lambda: dve.wait_ge(S("k_iota"), 2)
                yield lambda: ch(dve.memset(spf[0:1, ST:2 * ST], 0.0))
                for b in range(1, NT):
                    yield lambda b=b: ch(dve.scalar_tensor_tensor(
                        spf[0:1, ST:2 * ST], spf[0:1, 0:ST], excl[0:1, b:b + 1], spf[0:1, ST:2 * ST], ALU.is_ge, ALU.add))
                yield lambda: ch(dve.tensor_scalar(stoff[:], spf[0:1, ST:2 * ST], float(D), None, ALU.mult))
                for g in range(4):
                    yield lambda g=g: stats(mv2, g)
                yield lambda: dve.tensor_scalar(ve2[:], mv2[:, :, 1], EPS, None, ALU.add).then_inc(S("ve2"), 1)

            for i in range(NT):
                dve.wait_ge(S("t_hi"), i + 1)
                dve.tensor_tensor(xt3(xTl, i), psb[4 + i % 2][:].rearrange("p (k c) -> p k c", k=KC),
                                  xt3(xTh, i).bitcast(F32), ALU.subtract).then_inc(S("t_lo"), 1)
                if i in (4, 8, 12, 16):
                    k = i // 4 - 1
                    lo_w(dve, 0, k, Wl[:, 0, k, :], Wh[:, 0, k, :])

            def residual(i):
                g = G[:, i % 4, :]
                dve.wait_ge(S(f"xr{i % 4}"), 16 * (i // 4 + 1))
                ch(dve.tensor_tensor(g, g, at(i), ALU.add))
                dve.wait_ge(S("xrb"), 16)
                dve.tensor_tensor(g, g, G[:, 7, :], ALU.add).then_inc(S("res"), 1)

            def h_matrix(j, par, nxt=True, between=None, more=None):
                m = 2 * j + par
                dve.wait_ge(S(f"b_in{par}"), 16 * (j + 1))
                for i in range(NT):
                    if between:
                        for _ in range(2):
                            op = next(between, None)
                            if op:
                                op()
                    dve.wait_ge(S("h_pe"), C1 + 20 * m + i + 1)
                    if nxt:
                        dve.wait_ge(S(f"h_out{i % HB}"), 16 * (5 * m + i // HB))
                    dst = HS[:, i % HB, :] if nxt else at(i)
                    dve.tensor_tensor(dst, psb[i % HB][:], brd[:, par, :], ALU.add).then_inc(S("h_ev"), 1)
                    if more:
                        more(i)
                    if nxt and i % 5 == 3:
                        lo_w(dve, m + 1, i // 5, Wl[:, 1 - par, i // 5, :], Wh[:, 1 - par, i // 5, :])

            dve.wait_ge(S("t_init"), 16)
            ops = sort_ops()
            h_matrix(0, 0, between=ops)
            h_matrix(0, 1, between=ops)
            h_matrix(1, 0, between=ops)
            assert next(ops, None) is None
            h_matrix(1, 1, more=residual)
            with dve.Fori(2, NREL // 2) as mj:
                h_matrix(mj, 0)
                h_matrix(mj, 1)
            dve.wait_ge(S("xn_out"), 64)
            h_matrix(NREL // 2, 0, nxt=False)
            dve.memset(qT, 0.0)
            dve.memset(ltri[:], 0.0).then_inc(S("zeros"), 1)
            ch(dve.tensor_reduce(isum[:], ins_s[:], AX.X, ALU.add))
            ch(dve.tensor_scalar(isum[:], isum[:], 1.0 / NI, None, ALU.mult))
            for k in range(KC):
                a = dve.tensor_scalar(isb[:, k, :], ones[:], isum[:, k:k + 1], None, ALU.mult)
            a.then_inc(S("ib_ok"), 1)
            ch(dve.tensor_copy(gth[:], rmg[:, :, 0:NX]))
            dve.tensor_tensor(gtl[:], rmg[:, :, 0:NX], gth[:].bitcast(F32), ALU.subtract)
            dve.wait_ge(S("rs2"), 1)
            dve.scalar_tensor_tensor(nb2[:], mv2[:, :, 0], -1.0, rs2[:], ALU.mult, ALU.mult).then_inc(S("nb2"), 1)
            dve.wait_ge(S("t_in"), 16)
            ch(dve.tensor_copy(loc[:, :, 1], tbl[:, :, 1]))
            dve.wait_ge(S("mb_in"), 32)

            def st_step(it, s):
                st = SPI * it + s
                dve.wait_ge(S("st_pe"), st + 3)
                dve.tensor_scalar(ohr[:, s % 2, :], iotaf[:], loc[:, bass.ds(2 * st, 1), 1], None, ALU.is_equal)
                dve.tensor_scalar(ohf[:, s % 2, :], iotaf[:], loc[:, bass.ds(2 * st + 1, 1), 1], None, ALU.is_equal)
                dve.wait_ge(S("st_hi"), st + 1)
                dve.tensor_tensor(spl[:, s % 2, :], G[:, 2 * (s % 4), :], sph[:, s % 2, :].bitcast(F32),
                                  ALU.subtract).then_inc(S("st_lo"), 1)

            def st_add(it, s):
                st = SPI * it + s
                col = dve.value_load(stoff[0:1, bass.ds(st, 1)], min_val=0, max_val=(NT - 1) * D)
                dve.wait_ge(S("st_pe"), 4 + st + 1)
                dve.wait_ge(S("st_ev"), 2 + st)
                dve.tensor_tensor(acc[:, bass.ds(col, D)], psb[s % 2][:], acc[:, bass.ds(col, D)], ALU.add).then_inc(S("st_ev"), 1)

            def o_lo(O):
                dve.wait_ge(S("o_hi"), O + 1)
                dve.tensor_tensor(mxs(xTl, 1), psb[6][:], mxs(xTh, 1).bitcast(F32), ALU.subtract).then_inc(S("o_lo"), 1)

            def o_n(O):
                dve.wait_ge(S("o_pe"), O + 1)
                ch(dve.tensor_scalar(nrm[:, 0:NX], psb[6][:, 0:NX], EPSN, None, ALU.add))
                ch(dve.reciprocal(nrm[:, NX:2 * NX], nrm[:, 0:NX]))
                dve.tensor_tensor(on.rearrange("p (h e) -> p h e", h=NX), psb[5][:].rearrange("p (h e) -> p h e", h=NX),
                                  nrm[:, NX:2 * NX].unsqueeze(2).to_broadcast([P, NX, D // NX]), ALU.mult).then_inc(S("o_n"), 1)

            def y(O):
                dve.wait_ge(S("o_p"), C1 + O + 1)
                dve.wait_ge(S("y_in"), 16 * (O + 1))
                dve.wait_ge(S("z_out"), C16 + 16 * O)
                dve.tensor_tensor(yo, psb[3][:], yb, ALU.add).then_inc(S("m_y"), 1)

            def step(it, W=None, A=None, L=None, B=None, C=None, Q=None, O=None):
                if W is not None:
                    dve.wait_ge(S("bw_used"), 2 + SPI * W)
                    for s in range(SPI):
                        a = dve.tensor_scalar(ibr[:, s, :], id8[:, bass.ds(2 * W + s // KC, 1), :].rearrange("p a e -> p (a e)"),
                                              isum[:, s % KC:s % KC + 1], None, ALU.mult)
                    a.then_inc(S("ib_e"), 1)
                if not isinstance(it, int) and O is not None:
                    ch.enter(it - 25, 2)
                for s in range(SPI):
                    if s == 0 and L is not None:
                        dve.wait_ge(S("m_hi"), C1 + L + 1)
                        dve.tensor_tensor(mxs(xTl, 0), xmf, mxs(xTh, 0).bitcast(F32), ALU.subtract).then_inc(S("m_lo"), 1)
                    if s == 0 and O is not None:
                        o_n(O)
                    if s == 2 and B is not None:
                        dve.wait_ge(S("m_k"), C1 + B + 1)
                        dve.tensor_tensor(kb, psb[2][:], brd[:, 0, :], ALU.add).then_inc(S("m_k2"), 1)
                    if s == 2 and Q is not None:
                        if isinstance(Q, int) and Q == 0:
                            dve.wait_ge(S("mb_in"), 48)
                        dve.wait_ge(S("m_k"), C1 + NT + Q + 1)
                        dve.tensor_tensor(kb, psb[2][:], brd[:, 0, :], ALU.add).then_inc(S("m_k2"), 1)
                    if s == 3 and O is not None:
                        o_lo(O)
                    if s == 4 and Q is not None:
                        dve.wait_ge(S("m_e"), NT + Q + 1)
                        if isinstance(Q, int) and Q == 0:
                            dve.wait_ge(S("m_kv"), C1 + NT)
                        dve.scalar_tensor_tensor(kt, kE, 1.0, kR, ALU.min, ALU.add).then_inc(S("m_k3"), 1)
                    if s == 6 and B is not None:
                        dve.wait_ge(S("m_e"), B + 1)
                        dve.wait_ge(S("m_kv"), C1 + B)
                        dve.scalar_tensor_tensor(kt, kE, 1.0, kR, ALU.min, ALU.add).then_inc(S("m_k3"), 1)
                    if s == 6 and O is not None:
                        y(O)
                    if s == 6 and isinstance(it, int) and it == 24:
                        kv_end()
                    if W is not None and s % 2:
                        k = s // 2
                        c = W * KC + k
                        lo_w(dve, W + WQ, k, xTl[:, bass.ds(c * D, D)], xTh[:, bass.ds(c * D, D)])
                    st_step(it, s)
                    if s:
                        st_add(it, s - 1)
                st_add(it, SPI - 1)
                if isinstance(it, int) and it == 3:
                    dve.wait_ge(S("rg_pe"), 1)
                    dve.tensor_copy(rg[:], psb[2][:, 0:2 * NX])
                    ch(dve.tensor_copy(g8[:], psb[3][0:NX, 0:2]))
                    dve.wait_ge(S("eb_in"), 16)
                    dve.wait_ge(S("bw_used"), 2 + NX * KC)
                    dve.scalar_tensor_tensor(bb[0:NX, :], eb[0:NX, :], g8[:, 0:1], psb[7][0:NX, :], ALU.mult, ALU.add).then_inc(S("bb_ok"), 1)
                if isinstance(it, int) and it == 23:
                    ch(dve.memset(kvs[:, :, :], 0.0))
                    ch(dve.memset(ks2[:, :, :], 0.0))
                if not isinstance(it, int) and O is not None:
                    ch.leave(18)

            def kv_end():
                dve.wait_ge(S("m_kv"), C1 + NT)
                ch(dve.tensor_tensor(vt, psb[6][:], brd[:, 1, :], ALU.mult))
                for h in range(2):
                    r = slice(64 * h, 64 * h + 64)
                    c = slice(64 * h, 64 * h + 64)
                    dve.tensor_tensor(kvs[r, :, c], psb[5][r, :].rearrange("p (k c) -> p k c", k=KC)[:, :, c],
                                      vt[r, :].rearrange("p (k c) -> p k c", k=KC)[:, :, c], ALU.add)
                    a = dve.tensor_copy(ks2[r, :, h:h + 1], psb[6][r, :].rearrange("p (k c) -> p k c", k=KC)[:, :, 0:1])
                a.then_inc(S("kvs_ok"), 1)

            schedule(dve, step)
            o_n(NT - 1)
            o_lo(NT - 1)
            y(NT - 1)
            def lo_x(e, k):
                lo_w(dve, WX + e, k, Wl[:, e % 2 if isinstance(e, int) else pr, k, :],
                     Wh[:, e % 2 if isinstance(e, int) else pr, k, :])

            for k in range(KC):
                lo_x(0, k)

            def x_part(g):
                for i in range(4 * g, 4 * g + 4):
                    dve.wait_ge(S(f"f_in{i % 3}"), 16 * (i // 3 + 1))
                    dve.scalar_tensor_tensor(at(i), at(i), 0.0, HS[:, i % 3, :], ALU.max, ALU.add).then_inc(S("f_x1"), 1)
                    if i > 4 * g:
                        dve.wait_ge(S("f_x1"), i)
                        dve.bn_stats(stn[:, i - 1 - 4 * g, :], at(i - 1))
                dve.wait_ge(S("f_x1"), 4 * g + 4)
                ch(dve.bn_stats(stn[:, 3, :], at(4 * g + 3)))
                for i in range(4 * g, 4 * g + 4):
                    a = dve.bn_aggr(mv[:, i, :], stn[:, i - 4 * g, :])
                ch(a)
                q = slice(4 * g, 4 * g + 4)
                dve.tensor_scalar(ve[:, q], mv[:, q, 1], EPS, None, ALU.add).then_inc(S("f_ve"), 1)

            def nb_part(g):
                q = slice(4 * g, 4 * g + 4)
                dve.wait_ge(S("f_rs"), g + 1)
                dve.scalar_tensor_tensor(nb[:, q], mv[:, q, 0], -1.0, rs[:, q], ALU.mult, ALU.mult).then_inc(S("f_nb"), 1)

            def t_lo(i):
                dve.wait_ge(S("f_hi"), i + 1)
                dve.tensor_tensor(xt3(xTl, i), psb[4 + i % 2][:].rearrange("p (k c) -> p k c", k=KC),
                                  xt3(xTh, i).bitcast(F32), ALU.subtract).then_inc(S("f_lo"), 1)

            def route(g):
                lg, ex, c4 = rt[:, 0:4, :], rt[:, 4:8, :], rt[:, 8:12, :]
                sm, rk = rt[:, 12, :], rtk
                dve.wait_ge(S("f_gt"), g + 1)
                ch(dve.tensor_tensor(lg, psb[6][:, 0:4 * NX].rearrange("p (t e) -> p t e", t=4),
                                     rg[:, 0:NX].unsqueeze(1).to_broadcast([P, 4, NX]), ALU.add))
                ch(dve.tensor_reduce(sm[:, 0:4], lg, AX.X, ALU.max))
                dve.tensor_tensor(lg, lg, sm[:, 0:4].unsqueeze(2).to_broadcast([P, 4, NX]), ALU.subtract).then_inc(S("f_lg"), 1)
                dve.wait_ge(S("f_ex"), g + 1)
                ch(dve.tensor_reduce(sm[:, 4:8], ex, AX.X, ALU.add))
                ch(dve.reciprocal(sm[:, 4:8], sm[:, 4:8]))
                ch(dve.tensor_tensor(ex, ex, sm[:, 4:8].unsqueeze(2).to_broadcast([P, 4, NX]), ALU.mult))
                for j in range(4):
                    pj = ex[:, j:j + 1, :].to_broadcast([P, NX, NX])
                    pi = ex[:, j, :].unsqueeze(2).to_broadcast([P, NX, NX])
                    dve.tensor_tensor(rtg[:, j, 0], pj, pi, ALU.is_gt)
                    a = dve.tensor_tensor(rtg[:, j, 1], pj, pi, ALU.is_equal)
                ch(a)
                ch(dve.tensor_tensor(rtg[:, :, 1], rtg[:, :, 1], tri8[:].unsqueeze(1).to_broadcast([P, 4, NX, NX]), ALU.mult))
                ch(dve.tensor_tensor(rtg[:, :, 0], rtg[:, :, 0], rtg[:, :, 1], ALU.add))
                ch(dve.tensor_reduce(rk, rtg[:, :, 0], AX.X, ALU.add))
                if g:
                    dve.wait_ge(S("f_c1"), g)
                dve.scalar_tensor_tensor(c4, rk, 2.0, ex, ALU.is_lt, ALU.mult).then_inc(S("f_c"), 1)
                dve.wait_ge(S("f_c"), g + 1)
                ch(dve.tensor_tensor(cgm[:, :].rearrange("p (e i) -> p i e", i=NT)[:, 4 * g:4 * g + 4, :], c4,
                                     rg[:, NX:2 * NX].unsqueeze(1).to_broadcast([P, 4, NX]), ALU.mult))

            def x_add(n, i, c):
                dve.wait_ge(S("x_pe"), n + 1)
                dve.scalar_tensor_tensor(at(i), psb[n_bank(n, i)][:], cgm[:, bass.ds(c, 1)], at(i), ALU.mult, ALU.add).then_inc(S("x_ev"), 1)

            def n_bank(n, i):
                return n % HB if isinstance(n, int) else i % HB

            x_part(0)
            nb_part(0)
            x_part(1)
            nb_part(1)
            for i in range(4):
                t_lo(i)
            route(0)
            for g in range(NT // 4):
                if g + 2 < NT // 4:
                    x_part(g + 2)
                    nb_part(g + 2)
                if g + 1 < NT // 4:
                    for i in range(4 * g + 4, 4 * g + 8):
                        t_lo(i)
                    route(g + 1)
                dve.wait_ge(S("f_c1"), g + 1)
                dve.tensor_copy(cT[0:NX, :], psb[7][0:NX, :]).then_inc(S("f_ct"), 1)
                for i in range(4 * g, 4 * g + 4):
                    x_add(2 * i, i, i)
                    dve.wait_ge(S("x_pe"), 2 * i + 2)
                    dve.wait_ge(S("x_ev"), HB + 2 * i + 1)
                    dve.tensor_tensor(at(i), at(i), psb[(2 * i + 1) % HB][:], ALU.add).then_inc(S("x_ev"), 1)
                if g < 4:
                    lo_x(1, g)

            def expert(e, par, nxt=True):
                dve.wait_ge(S("x_ev"), HB + NT * (e + 1))
                for i in range(NT):
                    x_add(NT * (e + 1) + i, i, e * NT + i)
                    if nxt and i % 5 == 3:
                        k = i // 5
                        lo_w(dve, WX + e + 1, k, Wl[:, 1 - par, k, :], Wh[:, 1 - par, k, :])

            with dve.Fori(0, (NX - 2) // 2) as j:
                expert(2 * j + 1, 1)
                expert(2 * j + 2, 0)
            expert(NX - 1, 1, nxt=False)


def kernel(x, src, dst, edge_type_8, L0_gnn_W_self, L0_gnn_b_self, L0_gnn_W_rel, L0_gnn_b_rel, L0_mix_qkv_w,
           L0_mix_qkv_b, L0_mix_out_w, L0_mix_out_b, L0_mix_ln_gamma, L0_mix_ln_beta, L0_ffn_Ins_tk, L0_ffn_gate_w,
           L0_ffn_expert_w, L0_ffn_expert_b, L0_ffn_gamma_w, L0_ffn_beta_w, L0_ffn_rmod_w):
    import numpy as np
    import concourse.bacc as bacc
    from concourse.bass_utils import run_bass_kernel_spmd as run

    A = np.asarray
    w_all = np.concatenate([
        A(L0_gnn_W_rel).transpose(0, 2, 1), A(L0_gnn_W_self).T[None],
        A(L0_mix_qkv_w).reshape(3, D, D).transpose(0, 2, 1), A(L0_mix_out_w).T[None], A(L0_ffn_expert_w)])
    b_all = np.concatenate([A(L0_gnn_b_rel), A(L0_gnn_b_self)[None], A(L0_mix_qkv_b).reshape(3, D),
                            A(L0_mix_out_b)[None], A(L0_ffn_expert_b)])

    def by_k(a):
        return A(a).reshape(KC, P, -1).transpose(1, 0, 2)

    ins = {
        "x": A(x), "src": A(src), "dst": A(dst), "et": A(edge_type_8),
        "w_all": w_all.reshape(-1, D, D), "b_all": b_all,
        "gam_col": A(L0_mix_ln_gamma).reshape(KC, P).T, "bet_col": A(L0_mix_ln_beta).reshape(KC, P).T,
        "insT": by_k(A(L0_ffn_Ins_tk)[0].T), "gate": by_k(L0_ffn_gate_w), "rmod": by_k(L0_ffn_rmod_w),
        "gamw": by_k(A(L0_ffn_gamma_w).T), "betw": A(L0_ffn_beta_w).reshape(NX * D, D),
    }
    ins = {k: np.ascontiguousarray(v) for k, v in ins.items()}
    nc = bacc.Bacc("TRN2", target_bir_lowering=False, num_devices=1)
    aps = [nc.dram_tensor(f"in_{k}", v.shape, mybir.dt.from_np(v.dtype), kind="ExternalInput").ap() for k, v in ins.items()]
    out = nc.dram_tensor("out_0", (N, D), F32, kind="ExternalOutput").ap()
    h_d = nc.dram_tensor("h_scratch", (NREL * NPAD, D), F32, kind="Internal").ap()
    xn_d = nc.dram_tensor("xn_scratch", (NPAD, D), F32, kind="Internal").ap()
    z_d = nc.dram_tensor("z_scratch", (NPAD, D), F32, kind="Internal").ap()
    tab_d = nc.dram_tensor("table_scratch", (GT * P, 2), I32, kind="Internal").ap()
    build(nc, *aps, out, h_d, xn_d, z_d, tab_d)
    r = run(nc, [{f"in_{k}": v for k, v in ins.items()}], core_ids=[0])
    return r.results[0]["out_0"]
```

```python
from contextlib import ExitStack

import concourse.bass as bass
from concourse import mybir

F32 = mybir.dt.float32
F32R = mybir.dt.float32r
I32 = mybir.dt.int32
ALU = mybir.AluOpType
ACT = mybir.ActivationFunctionType
AX = mybir.AxisListType

P = 128
N = 2500
NT = 20
NPAD = NT * P
D = 512
KC = D // P
R = 8
NREL = 2 * R
E = 42500
ECOL = E // P
ETAIL = E - ECOL * P
EC = ECOL + 1
MC = 2 * EC
ST = (MC * P - NT) // (2 * P) + NT
GT = 2 * ST
IT = 44
SPI = ST // IT
SCH = 9
NX = 8
NI = 16
NSL = (2 * NPAD - NX) // P + NX
EPS = 1e-5
EPSN = 1e-8
HB = 4
SR = 4
assert SPI * IT == ST and MC % (2 * SCH) == 0

SELF, WQ, WK, WV, WO, WX = 16, 17, 18, 19, 20, 21


def build(nc, x, src, dst, et, w_all, b_all, gam_col, bet_col, insT, gate, rmod, gamw, betw, out,
          h_d, xn_d, z_d, tab_d):
    with ExitStack() as ctx:
        def sb(name, shape, dt=F32):
            return ctx.enter_context(nc.sbuf_tensor(name, shape, dt))

        sems = {}

        def sem(name):
            if name not in sems:
                sems[name] = ctx.enter_context(nc.semaphore(name))
            return sems[name]

        with nc.sbuf_tensor("We", [P, NX * KC, 2, D], F32R) as We:
            pass
        with nc.sbuf_tensor("xf", [P, NT, 2, D], F32) as xf:
            pass
        xTh = sb("xTh", [P, KC * NPAD], F32R)
        xTl = sb("xTl", [P, KC * NPAD], F32R)
        with nc.sbuf_tensor("Wh", [P, 2, KC, D], F32R) as Wh, nc.sbuf_tensor("Wl", [P, 2, KC, D], F32R) as Wl:
            pass
        UM = sb("UM", [P, 16, D])
        G = sb("G", [P, 8, D])
        acc = sb("acc", [P, NT * D])
        with nc.sbuf_tensor("sph", [P, 2, D], F32R) as sph, nc.sbuf_tensor("spl", [P, 2, D], F32R) as spl:
            pass
        msg = sb("msg", [P, 4 * D], I32)
        HS = sb("HS", [P, HB, D])
        Wraw = sb("Wraw", [P, 2, D])
        brd = sb("brd", [P, 2, D])
        tbl = sb("tbl", [P, GT, 2], I32)
        ident = sb("ident", [P, P])
        iotaf = sb("iotaf", [P, P])
        ltri = sb("ltri", [P, P])             
        ones = sb("ones", [P, P])
        with nc.sbuf_tensor("br", [P, SR * P], F32) as br:
            pass
        ohr = sb("ohr", [P, SR, P], F32R)
        idxr = sb("idxr", [P, 2, 8], I32)
        scr_i = sb("scr_i", [P, 2, SCH], I32)
        scr_v = sb("scr_v", [P, 2, SCH, 2], I32)
        stn = sb("stn", [P, 5, 6])
        mv = sb("mv", [P, NT, 2])
        ve = sb("ve", [P, NT])
        rs = sb("rs", [P, NT])
        mv2 = sb("mv2", [P, NT, 2])
        ve2 = sb("ve2", [P, NT])
        rs2 = sb("rs2", [P, NT])
        mhalf = sb("mhalf", [P, NT])
        nb2 = sb("nb2", [P, NT])
        nb = sb("nb", [P, NT])
        vbias = sb("vbias", [P, NT])
        cnt = sb("cnt", [P, NT])
        nsti = sb("nsti", [P, NT], I32)
        nst = sb("nst", [P, NT])
        excl = sb("excl", [P, NT])
        off = sb("off", [P, NT])
        stoff = sb("stoff", [1, ST], I32)
        gcol = sb("gcol", [P, KC])
        bcol = sb("bcol", [P, KC])
        ins_s = sb("ins_s", [P, KC, NI])
        isum = sb("isum", [P, KC])
        rmg = sb("rmg", [P, KC, 3 * NX])
        gth = sb("gth", [P, KC, NX], F32R)
        gtl = sb("gtl", [P, KC, NX], F32R)
        rg = sb("rg", [P, 2 * NX])
        cgw = sb("cgw", [P, 2, NT])
        rt = sb("rt", [P, 16, NX])
        slot = sb("slot", [P, 2, NT], I32)
        tokn = sb("tokn", [P, NT])
        toks = sb("toks", [P, NSL], I32)
        ecol = sb("ecol", [1, NSL], I32)
        id8 = sb("id8", [P, NX, NX])
        g8 = sb("g8", [NX, 2])
        psb = [ctx.enter_context(nc.psum_tensor(f"ps{i}", [P, D], F32)) for i in range(8)]

        zb, zz, xmf, kt, vt, kE, kR, kb = (UM[:, i, :] for i in range(8))
        kvs = UM[:, 8, :].rearrange("p (k c) -> p k c", k=KC)
        ks2 = UM[:, 9, 0:2 * KC].rearrange("p (k c) -> p k c", c=2)
        nrm = UM[:, 9, 16:32]
        on = UM[:, 4, :]
        bw = UM[:, 4:12, :].rearrange("p (r k) d -> p r k d", r=2)
        yb = UM[:, 10, :]
        qT = UM[:, 15, :]
        bb = HS[:, 3, :]
        ohf = UM[:, 13, :].rearrange("p (a b) -> p a b", a=SR)
        ibr = UM[:, 12, 0:NX * KC * NX].rearrange("p (e k j) -> p e k j", e=NX, k=KC)
        isb = UM[:, 14, :].rearrange("p (k c) -> p k c", k=KC)
        umf = UM[:, :, :].rearrange("p (c h) d -> p c h d", h=2)
        gf4 = G[:, :, :].rearrange("p (c h) d -> p c h d", h=2)

        def raw_x(c, n=1):
            T, o = (xf[:, :, :, :], 0) if c < 20 else (umf, 20) if c < 28 else (gf4, 28)
            return T[:, c - o:c - o + n, 1, :] if n > 1 else T[:, c - o, 1, :]

        tf = tbl[:, :, :].rearrange("p a b -> p (a b)").bitcast(F32)
        cT = tf[:, 0:4 * P]
        oh_p = Wraw[:, :, :].rearrange("p a (b c) -> p a b c", c=P)
        oh_t = tf[:, 4 * P:4 * P + 8 * NSL].rearrange("p (a b c) -> p a b c", a=2, b=4)
        bf = brd[:, :, :].rearrange("p a b -> p (a b)")
        nr = NT * NX
        r_ex, r_c, r_rk, r_m, r_pos, r_tmp = (bf[:, i * nr:(i + 1) * nr] for i in range(6))
        r_mx, r_sum = bf[:, 6 * nr:6 * nr + NT], bf[:, 6 * nr + NT:6 * nr + 2 * NT]
        posf = bf[:, 6 * nr:6 * nr + 2 * NT].rearrange("p (j t) -> p j t", j=2)
        r_gt = tbl[:, :, :].rearrange("p a b -> p (a b)").bitcast(F32)[:, 0:nr * NX].rearrange(
            "p (t e j) -> p t e j", t=NT, e=NX)

        def by_t(a):
            return a.rearrange("p (t e) -> p t e", e=NX)

        def by_e(a):
            return a.rearrange("p (e t) -> p e t", e=NX)

        gf = G[:, :, :].rearrange("p a b -> p (a b)")
        bk, msk, scn, pos, tmp = (gf[:, i * MC:(i + 1) * MC] for i in range(5))
        spf = gf[:, 5 * MC:5 * MC + 2 * ST]
        eI = tbl[:, :, :].rearrange("p a b -> p (a b)")[:, 0:3 * EC].rearrange("p (a b) -> p a b", a=3)
        pay = msg[:, 0:2 * MC].rearrange("p (t c) -> p t c", c=2)
        adr = msg[:, 2 * MC:3 * MC]
        even = [G[:, 2 * u, :] for u in range(4)]
        odd = [G[:, 2 * u + 1, :] for u in range(4)] + [HS[:, u, :] for u in range(3)] + [UM[:, 14, :]]
        loc = tbl[:, :, :].bitcast(F32)

        def schedule(eng, step):
            step(0, M=0)
            step(1, M=1, A=0)
            step(2, A=1, L=0, B=0)
            with eng.Fori(LOOP1, 21) as it:
                step(it, A=it - 1, L=it - 2, B=it - 2, C=it - 3)
            step(21, A=20, L=19, B=19, C=18)
            step(22, A=21, L=20, C=19, Q=0)
            step(23, A=22, L=21, Q=1, U=0)
            step(24, A=23, L=22, Q=2, U=1, O=0)
            step(25, A=24, L=23, Q=3, U=2, O=1, V=0)
            with eng.Fori(LOOP2, 41) as it:
                step(it, A=it - 1, L=it - 2, Q=it - 22, U=it - 23, O=it - 24, V=it - 25, Y=it - 26)
            step(41, L=39, Q=19, U=18, O=17, V=16, Y=15)
            step(42, U=19, O=18, V=17, Y=16)
            step(43, O=19, V=18, Y=17)

        LOOP1, LOOP2 = 3, 26

        def second(it, Q):
            return Q is not None or isinstance(it, int) and it == 21

        def xt(T, k, i):
            return T[:, k * NPAD + i * P:k * NPAD + (i + 1) * P]

        def xt3(T, i):
            return T[:, :].rearrange("p (k n) -> p k n", k=KC)[:, :, i * P:(i + 1) * P]

        def mw(T, q, k):
            place = (1, 3, 4, 2)[q] if T is xTh else (2, 0, 1, 3)[q]
            return T[:, (place * KC + k) * D:(place * KC + k + 1) * D]

        def mx(T, s, k):
            return mxs(T, s)[:, k * P:(k + 1) * P]

        def mxs(T, s):
            o = s * D + (0 if T is xTh else 4 * KC * D)
            return T[:, o:o + D]

        def zmix(i):
            if isinstance(i, int) and i >= 16:
                return (Wraw[:, 0, :], Wraw[:, 1, :], UM[:, 12, :], UM[:, 11, :])[i - 16]
            return xf[:, :, :, :].rearrange("p c h d -> p (c h d)")[:, bass.ds(i * D + 3 * KC * D, D)]

        def at(i):
            return acc[:, i * D:(i + 1) * D]

        S = sem
        CE = HB
        C1 = 1
        XO = (0, 4, 5, 1, 2, 3, 6, 7)
        gate_bank = (0, 1, 2, 3, 7)
        G_PAIR, G_BACK = 32 * IT, 16 * IT
        CP = 8

        def cut(T, X, s):
            return T[:, s % SR, :] if s % SR < 2 else mxs(X, s % SR)

        wsrc = w_all.rearrange("m (k p) n -> (m k) p n", p=P)

        class Chain:

            def __init__(self, eng, name):
                self.eng, self.sem, self.n, self.base = eng, sem(name), 0, 0

            def __call__(self, ins):
                ins.then_inc(self.sem, 1)
                self.n += 1
                self.eng.wait_ge(self.sem, self.base + self.n)

            def enter(self, i, per):
                self.n0, self.per, self.keep = self.n, per, self.base
                self.base = self.base + i * per

            def leave(self, steps):
                assert self.n - self.n0 == self.per, (self.n - self.n0, self.per)
                self.base = self.keep
                self.n = self.n0 + steps * self.per

        def load_w(sp, q, k):
            sp.wait_ge(S("w_lo"), 4 * q + k + 1)
            row = wsrc[4 * q + k] if isinstance(q, int) else wsrc[bass.ds(4 * q + k, 1)].rearrange("a p n -> (a p) n")
            sp.dma_start(Wraw[:, k % 2, :], row).then_inc(S(f"w_raw{k % 2}"), 16)

        def hi_w(act, q, k, dst):
            act.wait_ge(S(f"w_raw{k % 2}"), 16 * (2 * q + k // 2 + 1))
            act.activation(dst, Wraw[:, k % 2, :], ACT.Copy).then_inc(S("w_hi"), 1)

        def lo_w(dve, q, k, dst, hi):
            dve.wait_ge(S("w_hi"), 4 * q + k + 1)
            dve.tensor_tensor(dst, Wraw[:, k % 2, :], hi.bitcast(F32), ALU.subtract).then_inc(S("w_lo"), 1)

        block = ctx.enter_context(nc.Block())

        @block.sync
        def _(sp):
            def load_group(g):
                a, b = 5 * g, min(5 * g + 5, NT - 1)
                sp.dma_start(acc[:, a * D:b * D].rearrange("p (i d) -> p i d", d=D),
                             x[a * P:b * P, :].rearrange("(i p) d -> p i d", p=P)).then_inc(S(f"x_in{g}"), 16)

            load_group(0)
            for k in range(2):
                load_w(sp, 0, k)
            load_group(1)
            sp.dma_start(brd[:, 0, :], b_all[0:1, :].to_broadcast([P, D])).then_inc(S("b_in0"), 16)
            for k in range(2, KC):
                load_w(sp, 0, k)
            for g in (2, 3):
                load_group(g)
            sp.wait_ge(S("x_pad"), 1)
            sp.dma_start(acc[0:N - (NT - 1) * P, (NT - 1) * D:NT * D], x[(NT - 1) * P:N, :]).then_inc(S("x_in3"), 16)
            for j, v in enumerate((src, dst, et)):
                sp.dma_start(eI[:, j, 0:ECOL], v[0:ECOL * P].rearrange("(p c) -> p c", p=P)).then_inc(S("e_in"), 16)
            sp.wait_ge(S("e_dummy"), 3)
            for j, v in enumerate((src, dst, et)):
                sp.dma_start(eI[0:ETAIL, j, ECOL:EC], v[ECOL * P:E].rearrange("(p c) -> p c", c=1)).then_inc(S("e_in"), 16)
            sp.wait_ge(S("t_fill"), 2)
            sp.dma_start(tab_d.rearrange("(p t) c -> p (t c)", p=P), msg[:, 0:2 * GT]).then_inc(S("t_init"), 16)

            def xn_store(i):
                if i % 5 == 4:
                    g = i // 5
                    sp.wait_ge(S("xn_ok"), g + 1)
                    sp.dma_start(xn_d[5 * g * P:(5 * g + 5) * P, :].rearrange("(i p) d -> p i d", p=P),
                                 acc[:, 5 * g * D:(5 * g + 5) * D].rearrange("p (i d) -> p i d", d=D)).then_inc(S("xn_out"), 16)

            def h_matrix(m, par, more=None):
                for k in range(2):
                    load_w(sp, m + 1, k)
                sp.wait_ge(S("h_ev"), CE + 20 * m)
                sp.dma_start(brd[:, 1 - par, :], b_all[bass.ds(m + 1, 1), :].to_broadcast([P, D])).then_inc(S(f"b_in{1 - par}"), 16)
                for i in range(NT):
                    sp.wait_ge(S("h_ev"), CE + 20 * m + i + 1)
                    sp.dma_start(h_d[bass.ds((m * NT + i) * P, P), :], HS[:, i % HB, :]).then_inc(S(f"h_out{i % HB}"), 16)
                    if i in (6, 12):
                        load_w(sp, m + 1, 2 + (i == 12))
                    if more:
                        more(i)

            def load_x(i):
                rows = min(P, N - i * P)
                sp.dma_start(G[0:rows, i % 4, :], x[i * P:i * P + rows, :]).then_inc(S(f"xr{i % 4}"), 16)

            def residual(i):
                sp.wait_ge(S("res"), i + 1)
                sp.dma_start(z_d[i * P:(i + 1) * P, :], G[:, i % 4, :]).then_inc(S(f"r_out{i % 4}"), 16)
                if 2 <= i < NT - 2:
                    sp.wait_ge(S(f"r_out{(i + 2) % 4}"), 16 * ((i - 2) // 4 + 1))
                    load_x(i + 2)

            h_matrix(0, 0, xn_store)
            for ap, v in ((gcol, gam_col), (bcol, bet_col), (ins_s, insT)):
                sp.dma_start(ap[:], v).then_inc(S("c_in"), 16)
            for j, v in enumerate((gate, rmod, gamw)):
                sp.dma_start(rmg[:, :, j * NX:(j + 1) * NX], v).then_inc(S("c_in"), 16)
            for m in range(1, 4):
                h_matrix(m, m % 2)
            sp.wait_ge(S("stoff"), 1)
            sp.dma_start(G[:, 7, :], b_all[WO:WO + 1, :].to_broadcast([P, D])).then_inc(S("xrb"), 16)
            for i in range(4):
                load_x(i)
            h_matrix(4, 0, residual)
            h_matrix(5, 1)
            with sp.Fori(3, NREL // 2) as j:
                h_matrix(2 * j, 0)
                h_matrix(2 * j + 1, 1)
            def load_bw(e):
                sp.dma_start(bw[:, e % 2, :, :], betw[e * KC * P:(e + 1) * KC * P, :].rearrange(
                    "(k p) d -> p k d", p=P)).then_inc(S(f"bw_in{e % 2}"), 16)

            load_bw(0)
            for h in range(2):
                sp.wait_ge(S(f"sc{h}"), 16 * SCH * (MC // SCH // 2))
            sp.dma_start(tbl[:, :, :].rearrange("p t c -> p (t c)"), tab_d.rearrange("(p t) c -> p (t c)", p=P)).then_inc(S("t_in"), 16)
            sp.wait_ge(S("h_ev"), CE + 20 * (NREL + 1))
            load_bw(1)
            for j, m in enumerate((WK, WV)):
                sp.dma_start(brd[:, j, :], b_all[m:m + 1, :].to_broadcast([P, D])).then_inc(S("mb_in"), 16)
            sp.wait_ge(S(f"h_out{HB - 1}"), 16 * NREL * NT // HB)
            sp.dma_start(bb[0:NX, :], b_all[WX:WX + NX, :]).then_inc(S("eb_in"), 16)
            sp.wait_ge(S("xn_out"), 64)
            for s in range(4):
                sp.wait_ge(S(f"r_out{s}"), 16 * NT // 4)

            def step(it, M=None, A=None, L=None, B=None, C=None, Q=None, U=None, O=None, V=None, Y=None):
                if A is not None:
                    sp.wait_ge(S("m_z"), C1 + A)
                    tile = A - NT if second(it, Q) else A
                    sp.dma_start(zb, xn_d[bass.ds(tile * P, P), :]).then_inc(S("z_in"), 16)
                if M is not None:
                    for s in range(SPI):
                        load_w(sp, WQ + 2 * M + s // KC, s % KC)
                        e = (SPI * M + s) // 2
                        if s % 2 == 0 and e >= 2:
                            sp.wait_ge(S("bw_used"), KC * (e - 1))
                            load_bw(e)
                if isinstance(it, int) and it == 22:
                    sp.wait_ge(S("m_k2"), NT)
                    sp.dma_start(brd[:, 0, :], b_all[WQ:WQ + 1, :].to_broadcast([P, D])).then_inc(S("mb_in"), 16)
                if isinstance(it, int) and it == 23:
                    sp.wait_ge(S("bw_used"), NX * KC)
                    load_y(0)
                if Y is not None:
                    sp.wait_ge(S("m_y"), C1 + Y + 1)
                    load_y(Y + 1)

            def load_y(Y):
                sp.dma_start(yb, z_d[bass.ds(Y * P, P), :]).then_inc(S("y_in"), 16)

            schedule(sp, step)
            sp.wait_ge(S("m_y"), C1 + NT - 1)
            load_y(NT - 1)
            sp.wait_ge(S("m_y"), C1 + NT)
            sp.wait_ge(S("st_ev"), 2 + ST)

            def load_x(e):
                sp.dma_start(raw_x(KC * e, KC),
                             w_all[WX + e].rearrange("(k p) n -> p k n", p=P)).then_inc(S(f"x_raw{e}"), 16)

            for e in XO[:3]:
                load_x(e)
            for g in range(NT // 4):
                sp.wait_ge(S("f_z"), 4 * g + 4)
                sp.dma_start(xn_d[4 * g * P:(4 * g + 4) * P, :].rearrange("(t p) d -> p t d", p=P),
                             G[:, 4 * (g % 2):4 * (g % 2) + 4, :]).then_inc(S(f"f_st{g % 2}"), 16)
                if g == 2:
                    sp.wait_ge(S("f_x1"), NT)
                    for e in XO[3:7]:
                        load_x(e)
            sp.wait_ge(S("f_tr"), NT)
            sp.wait_ge(S("f_st0"), 16 * 3)
            sp.wait_ge(S("f_st1"), 16 * 2)
            load_x(XO[7])
            y_t = h_d[0:NSL * P, :].rearrange("(p t) d -> t p d", p=P)

            def store_y(i, u):
                sp.wait_ge(S("e_cp"), i + 1)
                dst = y_t[i] if isinstance(i, int) else y_t[bass.ds(i, 1)].rearrange("a p d -> (a p) d")
                sp.dma_start(dst, Wraw[:, u % 2, :]).then_inc(S(f"y_out{u % 2}"), 16)

            with sp.Fori(0, NSL // 4) as g:
                for u in range(4):
                    store_y(4 * g + u, u)
            for i in range(NSL // 4 * 4, NSL):
                store_y(i, i % 4)
            for i in range(NT):
                rows = min(P, N - i * P)
                sp.wait_ge(S("y_add"), 2 * i + 2)
                sp.dma_start(out[i * P:i * P + rows, :], acc[0:rows, i * D:(i + 1) * D]).then_inc(S("out_ok"), 16)
            sp.wait_ge(S("out_ok"), 16 * NT)

        @block.gpsimd
        def _(pool):
            ch = Chain(pool, "pool_ch")

            def waited():
                pool.sem_inc(S("pool_waited"), 1)

            pool.memset(eI[:, 0:2, ECOL:EC], NPAD - 1).then_inc(S("e_dummy"), 2)
            pool.memset(eI[:, 2:3, ECOL:EC], 0).then_inc(S("e_dummy"), 1)
            pool.wait_ge(S("e_dummy"), 3)
            pool.memset(acc[64:P, (NT - 1) * D:NT * D], 0.0).then_inc(S("x_pad"), 1)
            pool.wait_ge(S("x_pad"), 1)
            ch(pool.memset(ltri[:], 1.0))
            pool.affine_select(out=ltri[:], in_=ltri[:], compare_op=ALU.is_gt, fill=0.0, base=0,
                               pattern=[[1, P]], channel_multiplier=-1)
            pool.memset(ones[:], 1.0).then_inc(S("k_cst"), 1)
            ch(pool.memset(ident[:], 0.0))
            pool.affine_select(out=ident[:], in_=ident[:], compare_op=ALU.not_equal, fill=1.0, base=0,
                               pattern=[[-1, P]], channel_multiplier=1).then_inc(S("k_id"), 1)
            hs = msg[:, 0:2 * GT].rearrange("p (t c) -> p t c", c=2)
            pool.memset(hs[:, :, 0:1], 0).then_inc(S("t_fill"), 1)
            pool.memset(hs[:, :, 1:2], -1).then_inc(S("t_fill"), 1)
            pool.iota(iotaf[:], pattern=[[1, P]], base=0, channel_multiplier=0,
                      allow_small_or_imprecise_dtypes=True).then_inc(S("k_iota"), 1)
            pool.iota(spf[0:1, 0:ST], pattern=[[1, ST]], base=0, channel_multiplier=0,
                      allow_small_or_imprecise_dtypes=True).then_inc(S("k_iota"), 1)
            pool.memset(mhalf[:], -0.5)
            ch(pool.memset(vbias[:], 0.0))
            pool.affine_select(out=vbias[:, NT - 1:NT], in_=vbias[:, NT - 1:NT], compare_op=ALU.is_gt, fill=-1e30,
                               base=N - (NT - 1) * P, pattern=[[0, 1]], channel_multiplier=-1)
            ch(pool.memset(id8[:], 0.0))
            pool.affine_select(out=id8[:], in_=id8[:], compare_op=ALU.not_equal, fill=1.0, base=0,
                               pattern=[[1, NX], [-1, NX]], channel_multiplier=0).then_inc(S("k_tri"), 1)
            pool.iota(tokn[:], pattern=[[P, NT]], base=0, channel_multiplier=1,
                      allow_small_or_imprecise_dtypes=True).then_inc(S("k_tokn"), 1)
            for g in range(4):
                pool.wait_ge(S("ve"), g + 1)
                pool.tensor_tensor(rs[:, 5 * g:5 * g + 5], ve[:, 5 * g:5 * g + 5], mhalf[:, 0:5], ALU.pow).then_inc(S("rs"), 1)
            pool.wait_ge(S("adr"), 1)
            pool.wait_ge(S("t_init"), 16)
            def scatter(j):
                for h in range(2):
                    c = (2 * j + h) * SCH
                    if not isinstance(j, int):
                        pool.wait_ge(S(f"sc{h}"), 16 * SCH * j)
                        waited()
                    pool.tensor_copy(scr_i[:, h, :], adr[:, bass.ds(c, SCH)])
                    ch(pool.tensor_copy(scr_v[:, h, :, :], pay[:, bass.ds(c, SCH), :]))
                    if not isinstance(j, int):
                        waited()
                    for u in range(SCH):
                        pool.indirect_dma_start(
                            out=tab_d, out_offset=bass.IndirectOffsetOnAxis(ap=scr_i[:, h, u:u + 1], axis=0),
                            in_=scr_v[:, h, u, :], in_offset=None).then_inc(S(f"sc{h}"), 16)

            scatter(0)
            with pool.Fori(1, MC // SCH // 2) as j:
                ch.enter(j - 1, 2)
                scatter(j)
                ch.leave(MC // SCH // 2 - 1)
            pool.wait_ge(S("ve2"), 1)
            pool.tensor_tensor(rs2[:], ve2[:], mhalf[:], ALU.pow).then_inc(S("rs2"), 1)
            pool.wait_ge(S("t_in"), 16)
            for h in range(HB):
                pool.wait_ge(S(f"h_out{h}"), 16 * NREL * NT // HB)
            pool.wait_ge(S("rg_pe"), 1)

            def gathers(it):
                for h in range(2):
                    if not isinstance(it, int):
                        for s in range(4 * h, 4 * h + 4):
                            pool.wait_ge(S(f"g_odd{s}"), 16 * it)
                            pool.wait_ge(S(f"g_even{s % 4}"), 16 * (2 * it + h - 1))
                        waited()
                    ch(pool.tensor_copy(idxr[:, h, :], tbl[:, bass.ds(16 * it + 8 * h, 8), 0]))
                    for u in range(8):
                        s = 4 * h + u // 2
                        pool.wait_ge(S("st_pe" if u % 2 else "st_lo"), SPI * it + s + 1)
                        waited()
                        pool.indirect_dma_start(
                            out=odd[s] if u % 2 else even[s % 4], out_offset=None, in_=h_d,
                            in_offset=bass.IndirectOffsetOnAxis(ap=idxr[:, h, u:u + 1], axis=0)
                        ).then_inc(S(f"g_odd{s}" if u % 2 else f"g_even{s % 4}"), 16)

            gathers(0)
            with pool.Fori(1, IT) as it:
                ch.enter(it - 1, 2)
                gathers(it)
                ch.leave(IT - 1)
            for g in range(NT // 4):
                pool.wait_ge(S("f_ve"), g + 1)
                pool.tensor_tensor(rs[:, 4 * g:4 * g + 4], ve[:, 4 * g:4 * g + 4], mhalf[:, 0:4], ALU.pow).then_inc(S("f_rs"), 1)
            pool.wait_ge(S("f_st0"), 16 * 3)
            pool.wait_ge(S("f_st1"), 16 * 2)
            pool.wait_ge(S("toks"), 1)
            for i in range(NSL):
                if i >= 4:
                    pool.wait_ge(S("e_tr"), i - 3)
                pool.indirect_dma_start(
                    out=HS[:, i % 4, :], out_offset=None, in_=xn_d,
                    in_offset=bass.IndirectOffsetOnAxis(ap=toks[:, i:i + 1], axis=0)).then_inc(S(f"g_even{i % 4}"), 16)
            for u in range(2):
                pool.wait_ge(S(f"y_out{u}"), 16 * ((NSL + 1 - u) // 2))
            for i in range(2 * NT):
                if i >= 8:
                    pool.wait_ge(S("y_add"), i - 7)
                pool.indirect_dma_start(
                    out=G[:, i % 8, :], out_offset=None, in_=h_d,
                    in_offset=bass.IndirectOffsetOnAxis(ap=slot[:, i % 2, i // 2:i // 2 + 1], axis=0)).then_inc(S(f"g_odd{i % 8}"), 16)

        @block.scalar
        def _(act):
            ch = Chain(act, "act_ch")

            def w_half(q, par, ks=range(KC)):
                for k in ks:
                    hi_w(act, q, k, Wh[:, par, k, :])

            w_half(0, 0)
            for i in range(NT):
                act.wait_ge(S("t_pe"), i + 1)
                act.activation(xt3(xTh, i), psb[4 + i % 2][:].rearrange("p (k c) -> p k c", k=KC), ACT.Copy).then_inc(S("t_hi"), 1)
                if i % 5 == 2:
                    w_half(1, 1, [i // 5])

            def w_next(m, par):
                act.wait_ge(S("h_pe"), C1 + NT * m)
                w_half(m + 1, 1 - par)

            w_next(1, 1)
            with act.Fori(1, NREL // 2) as j:
                w_next(2 * j, 0)
                w_next(2 * j + 1, 1)

            def st_step(it, s):
                st = SPI * it + s
                act.wait_ge(S(f"g_even{s % 4}"), 16 * (2 * it + s // 4 + 1))
                act.wait_ge(S("st_pe"), CP - SR + st + 1)
                act.activation(cut(sph, xTh, s), even[s % 4], ACT.Copy).then_inc(S("st_hi"), 1)

            def z_part(A, tile):
                act.wait_ge(S("z_in"), 16 * (A + 1))
                act.wait_ge(S("m_tr"), C1 + A)
                act.activation(zz, zb, ACT.Identity, bias=nb2[:, bass.ds(tile, 1)],
                               scale=rs2[:, bass.ds(tile, 1)]).then_inc(S("m_z"), 1)

            def xm_part(A, last, n):
                act.wait_ge(S("m_tr"), C1 + A + 1)
                act.wait_ge(S("m_lo"), C1 + A)
                for k in range(KC):
                    xa = act.activation(xmf[:, k * P:(k + 1) * P], psb[4][:, k * P:(k + 1) * P], ACT.Identity,
                                        bias=bcol[:, k:k + 1], scale=gcol[:, k:k + 1])
                ch(xa)
                if last:
                    act.wait_ge(S(last), n)
                act.activation(mxs(xTh, 0), xmf, ACT.Copy).then_inc(S("m_hi"), 1)

            def step(it, M=None, A=None, L=None, B=None, C=None, Q=None, U=None, O=None, V=None, Y=None):
                if not isinstance(it, int) and A is not None:
                    ch.enter(it - (LOOP2 if Q is not None else LOOP1), 1)
                for s in range(SPI):
                    if M is not None:
                        hi_w(act, WQ + 2 * M + s // KC, s % KC, mw(xTh, 2 * M + s // KC, s % KC))
                    if s == 1 and A is not None:
                        z_part(A, A - NT if second(it, Q) else A)
                    if s == 3 and V is not None:
                        o_hi(V)
                    if s == 6 and B is not None:
                        act.wait_ge(S("m_k2"), B + 1)
                        act.activation(kE, kb, ACT.Exp, bias=vbias[:, bass.ds(B, 1)])
                        act.activation(kR, kb, ACT.Relu, bias=vbias[:, bass.ds(B, 1)]).then_inc(S("m_e"), 1)
                    if s == 6 and Q is not None:
                        act.wait_ge(S("m_k2"), NT + Q + 1)
                        act.activation(kE, kb, ACT.Exp)
                        act.activation(kR, kb, ACT.Relu).then_inc(S("m_e"), 1)
                    if s == 7 and A is not None:
                        if second(it, Q):
                            xm_part(A, "m_k", C1 + A) if Q is not None else xm_part(A, "m_p1", C1 + NT)
                        else:
                            xm_part(A, None if isinstance(A, int) and A == 0 else "m_p1", C1 + A)
                    if s == 7 and U is not None:
                        act.wait_ge(S("q_tr"), U + 1)
                        if not (isinstance(U, int) and U == 0):
                            act.wait_ge(S("o_pe"), U)
                        act.activation(qT, psb[7][:], ACT.Copy).then_inc(S("q_t"), 1)
                    if s == 7 and B is not None:
                        act.wait_ge(S("m_p1"), C1 + B + 1)
                        act.wait_ge(S("m_kv"), C1 + B)
                        act.activation(vt, psb[3][:], ACT.Copy).then_inc(S("m_v"), 1)
                    st_step(it, s)
                if not isinstance(it, int) and A is not None:
                    ch.leave(41 - LOOP2 if Q is not None else 21 - LOOP1)

            def o_hi(O):
                act.wait_ge(S("o_tr"), O + 1)
                act.wait_ge(S("o_p"), C1 + O)
                act.activation(mxs(xTh, 1), psb[7][:], ACT.Copy).then_inc(S("o_hi"), 1)

            act.wait_ge(S("c_in"), 96)
            act.wait_ge(S("k_tri"), 1)
            act.wait_ge(S("h_pe"), C1 + NT * (NREL + 1))
            act.wait_ge(S("nb2"), 1)
            schedule(act, step)
            o_hi(NT - 1)
            act.wait_ge(S("m_y"), C1 + NT)
            act.wait_ge(S("bb_ok"), 1)

            def hi_x(n):
                c = KC * XO[n // KC] + n % KC
                act.wait_ge(S(f"x_raw{c // KC}"), 16)
                act.activation(We[:, c, 0, :], raw_x(c), ACT.Copy).then_inc(S("w_hi"), 1)

            def gate_out(g):
                act.wait_ge(S("f_gt"), 4 * g + 4)
                if g >= 3:
                    act.wait_ge(S("f_gl"), g - 2)
                act.activation(HS[0:NX, g % 3, :], psb[gate_bank[g]][0:NX, :], ACT.Copy).then_inc(S("f_lt"), 1)

            def zf(i):
                if i % 4 == 0:
                    act.wait_ge(S("f_nb"), i // 4 + 1)
                if i >= 8:
                    act.wait_ge(S("f_tr"), i - 7)
                    if i % 4 == 0:
                        act.wait_ge(S(f"f_st{i // 4 % 2}"), 16 * (i // 8))
                act.activation(G[:, i % 8, :], at(i), ACT.Identity, bias=nb[:, i:i + 1], scale=rs[:, i:i + 1]).then_inc(S("f_z"), 1)

            for i in range(3):
                zf(i)
            for i in range(NT):
                if i + 3 < NT:
                    zf(i + 3)
                act.wait_ge(S("f_tr"), i + 1)
                if i >= 2:
                    act.wait_ge(S("f_gt"), i - 1)
                act.activation(sph[:, i % 2, :], psb[4 + i % 2][:], ACT.Copy).then_inc(S("f_hi"), 1)
                if i % 4 == 1 and i > 4:
                    gate_out(i // 4 - 1)
                if i >= 8:
                    hi_x(2 * (i - 8))
                    hi_x(2 * (i - 8) + 1)
            gate_out(NT // 4 - 1)
            act.wait_ge(S("f_lg"), 1)
            act.activation(r_ex, r_tmp, ACT.Exp).then_inc(S("f_ex"), 1)
            for c in range(2 * (NT - 8), NX * KC):
                hi_x(c)

            def e_hi(i, u, first=False):
                act.wait_ge(S("e_tr"), i + 1)
                if not first:
                    act.wait_ge(S("e_pe"), i - 1)
                act.activation(sph[:, u % 2, :], psb[4 + u % 2][:], ACT.Copy).then_inc(S("e_hi"), 1)

            for i in range(4):
                e_hi(i, i, first=i < 2)
            with act.Fori(1, NSL // 4) as g:
                for u in range(4):
                    e_hi(4 * g + u, u)
            for i in range(NSL // 4 * 4, NSL):
                e_hi(i, i % 4)

        @block.tensor
        def _(pe):
            def three(ps, lh, ll, rh, rl, first=True, last=True):
                for k in range(KC):
                    a = pe.matmul(ps, lh(k), rh(k), start=(first and k == 0), stop=False)
                    a = pe.matmul(ps, lh(k), rl(k), start=False, stop=False)
                    a = pe.matmul(ps, ll(k), rh(k), start=False, stop=(last and k == KC - 1))
                return a

            pe.wait_ge(S("k_id"), 1)

            def x_tr(i):
                if i % 5 == 0:
                    pe.wait_ge(S("xn_ok"), i // 5 + 1)
                if i >= 2:
                    pe.wait_ge(S("t_lo"), i - 1)
                for k in range(KC):
                    a = pe.transpose(psb[4 + i % 2][:, k * P:(k + 1) * P], acc[:, i * D + k * P:i * D + (k + 1) * P], ident[:])
                a.then_inc(S("t_pe"), 1)

            def prefix():
                pe.wait_ge(S("k_cst"), 1)
                pe.wait_ge(S("cnt"), NT)
                pe.matmul(psb[7][:, 0:NT], ltri[:], cnt[:], start=True, stop=True)
                pe.matmul(psb[7][:, 32:32 + NT], ones[:], cnt[:], start=True, stop=True).then_inc(S("pre"), 1)

            def h_matrix(m, par, before=None):
                pe.wait_ge(S("w_lo"), 2 + 4 * (m + 1))
                for i in range(NT):
                    if before:
                        before(i)
                    pe.wait_ge(S("h_ev"), 20 * m + i + 1)
                    three(psb[i % HB][:], lambda k: xt(xTh, k, i), lambda k: xt(xTl, k, i),
                          lambda k: Wh[:, par, k, :], lambda k: Wl[:, par, k, :]).then_inc(S("h_pe"), 1)

            def next_tr(i):
                if i + 1 < NT:
                    x_tr(i + 1)
                pe.wait_ge(S("t_lo"), i + 1)

            x_tr(0)
            h_matrix(0, 0, next_tr)
            h_matrix(1, 1, lambda i: prefix() if i == 8 else None)
            with pe.Fori(1, NREL // 2) as j:
                h_matrix(2 * j, 0)
                h_matrix(2 * j + 1, 1)
            h_matrix(NREL, 0)

            def st_step(it, s):
                st = SPI * it + s
                pe.wait_ge(S("st_ev"), st + 1)
                pe.wait_ge(S("st_lo"), 4 + st + 1)
                ps = psb[s % 2][:]
                pe.matmul(ps, ohr[:, s % SR, :], cut(sph, xTh, s), start=True, stop=False)
                pe.matmul(ps, ohr[:, s % SR, :], cut(spl, xTl, s), start=False, stop=False)
                pe.wait_ge(S(f"g_odd{s}"), 16 * (it + 1))
                pe.matmul(ps, ohf[:, s % SR, :], odd[s], start=False, stop=True).then_inc(S("st_pe"), 1)

            def proj(ps, s, q, name):
                three(ps, lambda k: mx(xTh, s, k), lambda k: mx(xTl, s, k),
                      lambda k: mw(xTh, q, k), lambda k: mw(xTl, q, k)).then_inc(S(name), 1)

            def o_tr(O):
                pe.wait_ge(S("o_n"), O + 1)
                for k in range(KC):
                    a = pe.transpose(psb[7][:, k * P:(k + 1) * P], on[:, k * P:(k + 1) * P], ident[:])
                a.then_inc(S("o_tr"), 1)

            def o_proj(O):
                pe.wait_ge(S("o_lo"), C1 + O + 1)
                pe.wait_ge(S("m_y"), C1 + O)
                proj(psb[3][:], 1, 3, "o_p")

            def step(it, M=None, A=None, L=None, B=None, C=None, Q=None, U=None, O=None, V=None, Y=None):
                for s in range(SPI):
                    if M is not None:
                        for r in range(2):
                            c = 2 * (SPI * M + s) + r
                            e, k = c // KC, c % KC
                            pe.wait_ge(S(f"bw_in{e % 2}"), 16 * (e // 2 + 1))
                            pe.matmul(psb[7][0:NX, :], ibr[:, e, k, :], bw[:, e % 2, k, :],
                                      start=False, stop=False, skip_group_check=True).then_inc(S("bw_used"), 1)
                    if s == 0 and C is not None:
                        pe.wait_ge(S("m_k3"), C + 1)
                        pe.wait_ge(S("m_v"), C1 + C + 1)
                        for k in range(KC):
                            c = slice(k * P, (k + 1) * P)
                            pe.matmul(psb[5][:, c], kt[:, c], vt[:, c], start=False, stop=False, skip_group_check=True)
                            a = pe.matmul(psb[6][:, 2 * k:2 * k + 2], kt[:, c], ones[:, 0:2], start=False, stop=False, skip_group_check=True)
                        a.then_inc(S("m_kv"), 1)
                    if s == 1 and B is not None:
                        pe.wait_ge(S("m_lo"), C1 + B + 1)
                        if not (isinstance(B, int) and B == 0):
                            pe.wait_ge(S("m_k2"), B)
                        proj(psb[2][:], 0, 1, "m_k")
                    if s == 1 and Q is not None:
                        pe.wait_ge(S("m_lo"), C1 + NT + Q + 1)
                        pe.wait_ge(S("m_k2"), NT + Q)
                        proj(psb[2][:], 0, 0, "m_k")
                    if s == 2 and A is not None:
                        pe.wait_ge(S("m_z"), C1 + A + 1)
                        pe.wait_ge(S("m_hi"), C1 + A)
                        for k in range(KC):
                            a = pe.transpose(psb[4][:, k * P:(k + 1) * P], zz[:, k * P:(k + 1) * P], ident[:])
                        a.then_inc(S("m_tr"), 1)
                    if s == 3 and B is not None:
                        pe.wait_ge(S("m_v"), C1 + B)
                        proj(psb[3][:], 0, 2, "m_p1")
                    if s == 3 and U is not None:
                        pe.wait_ge(S("m_k3"), NT + U + 1)
                        if V is not None:
                            pe.wait_ge(S("o_lo"), C1 + V + 1)
                        for k in range(KC):
                            a = pe.transpose(psb[7][:, k * P:(k + 1) * P], kt[:, k * P:(k + 1) * P], ident[:])
                        a.then_inc(S("q_tr"), 1)
                    if s == 4 and V is not None:
                        o_proj(V)
                    if s == 7 and O is not None:
                        if U is not None:
                            pe.wait_ge(S("q_t"), U + 1)
                        elif V is not None:
                            pe.wait_ge(S("o_lo"), C1 + V + 1)
                        o_tr(O)
                    if s == 7 and U is not None:
                        pe.wait_ge(S("kvs_ok"), 1)
                        pe.wait_ge(S("q_t"), U + 1)
                        if O is not None:
                            pe.wait_ge(S("o_n"), O + 1)
                        for k in range(KC):
                            c = slice(k * P, (k + 1) * P)
                            pe.matmul(psb[5][:, c], qT[:, c], kvs[:, k, :], start=(k == 0), stop=(k == KC - 1), skip_group_check=True)
                            a = pe.matmul(psb[6][:, 2 * k:2 * k + 2], qT[:, c], ks2[:, k, :], start=(k == 0), stop=(k == KC - 1), skip_group_check=True)
                        a.then_inc(S("o_pe"), 1)
                    st_step(it, s)

            pe.wait_ge(S("h_ev"), CE + 20 * (NREL + 1))
            pe.wait_ge(S("zeros"), 1)
            for b in (5, 6):
                pe.matmul(psb[b][:], qT[:, 0:P], qT, start=True, stop=False, skip_group_check=True)
            pe.matmul(psb[7][0:NX, :], qT[:, 0:NX], qT, start=True, stop=False, skip_group_check=True)
            pe.wait_ge(S("ib_ok"), 1)
            for k in range(KC):
                pe.matmul(psb[2][:, 0:2 * NX], isb[:, k, :], rmg[:, k, NX:3 * NX], start=(k == 0), stop=(k == KC - 1))
            for k in range(KC):
                a = pe.matmul(psb[3][0:NX, 0:2], rmg[:, k, 2 * NX:3 * NX], isb[:, k, 0:2], start=(k == 0), stop=(k == KC - 1))
            a.then_inc(S("rg_pe"), 1)
            schedule(pe, step)
            o_proj(NT - 1)
            pe.wait_ge(S("m_y"), C1 + NT)
            pe.wait_ge(S("st_ev"), 2 + ST)
            pe.wait_ge(S("bb_ok"), 1)

            def cut4(T, u):
                return lambda k: T[:, u % 2, k * P:(k + 1) * P]

            def gate_i(i):
                pe.wait_ge(S("f_lo"), i + 1)
                three(psb[gate_bank[i // 4]][0:NX, i % 4 * P:(i % 4 + 1) * P], lambda k: gth[:, k, :], lambda k: gtl[:, k, :],
                      cut4(sph, i), cut4(spl, i)).then_inc(S("f_gt"), 1)

            def gate_tr(g):
                pe.wait_ge(S("f_lt"), g + 1)
                for j in range(4):
                    t = 4 * g + j
                    a = pe.transpose(psb[6][:, t * NX:(t + 1) * NX], HS[0:NX, g % 3, j * P:(j + 1) * P], ident[0:NX, 0:NX])
                a.then_inc(S("f_gl"), 1)

            def z_tr(i):
                pe.wait_ge(S("f_z"), i + 1)
                if i >= 2:
                    pe.wait_ge(S("f_lo"), i - 1)
                for k in range(KC):
                    a = pe.transpose(psb[4 + i % 2][:, k * P:(k + 1) * P], G[:, i % 8, k * P:(k + 1) * P], ident[:])
                a.then_inc(S("f_tr"), 1)

            z_tr(0)
            z_tr(1)
            for i in range(NT):
                if i + 2 < NT:
                    z_tr(i + 2)
                gate_i(i)
                if i % 4 == 3 and i > 4:
                    gate_tr(i // 4 - 1)
            gate_tr(NT // 4 - 1)
            pe.wait_ge(S("f_cnt"), 1)
            pe.matmul(psb[5][:, 0:NX], ltri[:], rt[:, 0, :], start=True, stop=True)
            pe.matmul(psb[5][:, 32:32 + NX], ones[:], rt[:, 0, :], start=True, stop=True).then_inc(S("f_pre"), 1)
            for n in range(2 * NT):
                pe.wait_ge(S("oh"), n + 1)
                a = pe.matmul(psb[6][:, 0:NSL], oh_p[:, n // 4 % 2, n % 4, :], oh_t[:, n // 4 % 2, n % 4, :], start=(n == 0), stop=(n == 2 * NT - 1))
                a.then_inc(S("oh_pe"), 1)
            pe.wait_ge(S("e_col"), 1)

            def e_tr(i, u, turn):
                pe.wait_ge(S(f"g_even{u}"), G_PAIR + 16 * (turn + 1))
                if not (isinstance(i, int) and i < 2):
                    pe.wait_ge(S("e_lo"), i - 1)
                for k in range(KC):
                    a = pe.transpose(psb[4 + u % 2][:, k * P:(k + 1) * P], HS[:, u, k * P:(k + 1) * P], ident[:])
                a.then_inc(S("e_tr"), 1)

            def e_mul(i, u):
                col = pe.value_load(ecol[0:1, bass.ds(i, 1)], min_val=0, max_val=(NX - 1) * KC * 2 * D)
                pe.wait_ge(S("e_lo"), i + 1)
                if not (isinstance(i, int) and i < 4):
                    pe.wait_ge(S("e_cp"), i - 3)
                wf = We[:, :, :, :].rearrange("p c h d -> p (c h d)")
                three(psb[u][:], cut4(sph, u), cut4(spl, u),
                      lambda k: wf[:, bass.ds(col + 2 * k * D, D)],
                      lambda k: wf[:, bass.ds(col + (2 * k + 1) * D, D)]).then_inc(S("e_pe"), 1)

            e_tr(0, 0, 0)
            pe.wait_ge(S("w_lo"), 2 + 4 * (WX + NX))
            for i in range(4):
                e_tr(i + 1, (i + 1) % 4, (i + 1) // 4)
                e_mul(i, i)
            with pe.Fori(1, NSL // 4) as g:
                for u in range(4):
                    e_tr(4 * g + u + 1, (u + 1) % 4, g + (u + 1) // 4)
                    e_mul(4 * g + u, u)
            for i in range(NSL // 4 * 4, NSL):
                if i + 1 < NSL:
                    e_tr(i + 1, (i + 1) % 4, (i + 1) // 4)
                e_mul(i, i % 4)
            pe.wait_ge(S("e_cp"), NSL)
            pe.wait_ge(S("f_c"), 1)
            for g in range(NT // 4):
                if g:
                    pe.wait_ge(S("f_ct"), g)
                for j in range(4):
                    a = pe.transpose(psb[7][0:NX, j * P:(j + 1) * P], by_t(r_c)[:, 4 * g + j, :], ident[:])
                a.then_inc(S("f_c1"), 1)
                pe.wait_ge(S("f_ct"), g + 1)
                for i in range(4 * g, 4 * g + 4):
                    if i >= HB:
                        pe.wait_ge(S("f_ba"), i - HB + 1)
                    pe.matmul(psb[i % HB][:], cT[0:NX, (i % 4) * P:(i % 4 + 1) * P], br[0:NX, :],
                              start=True, stop=True).then_inc(S("f_bp"), 1)

        @block.vector
        def _(dve):
            ch = Chain(dve, "dve_ch")
            dve.sem_inc(S("h_ev"), HB)
            for name in ("m_tr", "m_y", "h_pe", "m_lo", "m_p1", "m_k", "m_hi", "m_v", "m_kv", "m_z", "o_lo", "o_p"):
                dve.sem_inc(S(name), C1)
            dve.sem_inc(S("w_lo"), 2)
            dve.sem_inc(S("st_ev"), 2)
            dve.sem_inc(S("st_lo"), 4)
            dve.sem_inc(S("st_pe"), CP)
            ti = tmp.bitcast(I32)

            def count_ops():
                T = eI[:, 0:2, :].rearrange("p a b -> p (a b)")
                dve.wait_ge(S("e_in"), 96)
                dve.wait_ge(S("t_init"), 16)
                yield lambda: ch(dve.tensor_scalar(ti, T, 7, None, ALU.arith_shift_right))
                yield lambda: ch(dve.tensor_copy(bk, ti))
                yield lambda: dve.tensor_scalar(pay[:, 0:MC, 1], T, P - 1, None, ALU.bitwise_and)
                for b in range(NT):
                    yield lambda b=b: dve.tensor_scalar(msk, bk, float(b), None, ALU.is_equal, ALU.add,
                                                        accum_out=cnt[:, b:b + 1]).then_inc(S("cnt"), 1)
                    yield lambda b=b: dve.wait_ge(S("cnt"), b + 1)

            def payload():
                dve.scalar_tensor_tensor(pay[:, 0:EC, 0], eI[:, 2, :], float(NPAD), eI[:, 1, :], ALU.mult, ALU.add)
                ch(dve.tensor_scalar(ti[:, 0:EC], eI[:, 2, :], float(NPAD), float(R * NPAD), ALU.mult, ALU.add))
                dve.tensor_tensor(pay[:, EC:MC, 0], ti[:, 0:EC], eI[:, 0, :], ALU.add)
                ch(dve.memset(pos, 0.0))


            def stats(mvt, g):
                for i in range(5 * g, 5 * g + 5):
                    a = dve.bn_stats(stn[:, i - 5 * g, :], at(i))
                ch(a)
                for i in range(5 * g, 5 * g + 5):
                    a = dve.bn_aggr(mvt[:, i, :], stn[:, i - 5 * g, :])
                ch(a)

            def norm(g):
                dve.wait_ge(S("rs"), g + 1)
                for i in range(5 * g, 5 * g + 5):
                    a = dve.tensor_scalar(at(i), at(i), mv[:, i, 0:1], rs[:, i:i + 1], ALU.subtract, ALU.mult)
                a.then_inc(S("xn_ok"), 1)

            def group_stats(g):
                dve.wait_ge(S(f"x_in{g}"), 16 if g < 3 else 32)
                stats(mv, g)
                dve.tensor_scalar(ve[:, 5 * g:5 * g + 5], mv[:, 5 * g:5 * g + 5, 1], EPS, None, ALU.add).then_inc(S("ve"), 1)

            def offsets():
                dve.wait_ge(S("pre"), 1)
                ch(dve.tensor_scalar(nsti[:], psb[7][:, 32:32 + NT], float(2 * P - 1), None, ALU.add))
                ch(dve.tensor_scalar(nsti[:], nsti[:], 8, None, ALU.arith_shift_right))
                ch(dve.tensor_copy(nst[:], nsti[:]))
                ch(dve.tensor_tensor_scan(excl[:], nst[:], nst[:], 0.0, ALU.add, ALU.max))
                ch(dve.tensor_tensor(excl[:], excl[:], nst[:], ALU.subtract))
                ch(dve.scalar_tensor_tensor(off[:], excl[:], float(2 * P), psb[7][:, 0:NT], ALU.mult, ALU.add))
                ch(dve.tensor_scalar(off[:], off[:], -1.0, None, ALU.add))

            def sort_ops():
                for b in range(NT):
                    yield lambda b=b: ch(dve.tensor_scalar(msk, bk, float(b), None, ALU.is_equal))
                    yield lambda b=b: ch(dve.tensor_tensor_scan(scn, msk, msk, 0.0, ALU.add, ALU.max))
                    yield lambda b=b: ch(dve.scalar_tensor_tensor(tmp, scn, off[:, b:b + 1], msk, ALU.add, ALU.mult))
                    yield lambda b=b: ch(dve.tensor_tensor(pos, pos, tmp, ALU.add))
                si, mi = scn.bitcast(I32), msk.bitcast(I32)
                yield lambda: ch(dve.tensor_copy(si, pos))
                yield lambda: dve.tensor_scalar(mi, si, P - 1, None, ALU.bitwise_and)
                yield lambda: ch(dve.tensor_scalar(ti, si, 7, None, ALU.arith_shift_right))
                yield lambda: dve.scalar_tensor_tensor(adr, mi, float(GT), ti, ALU.mult, ALU.add).then_inc(S("adr"), 1)
                yield lambda: dve.wait_ge(S("k_iota"), 2)
                yield lambda: ch(dve.memset(spf[0:1, ST:2 * ST], 0.0))
                for b in range(1, NT):
                    yield lambda b=b: ch(dve.scalar_tensor_tensor(
                        spf[0:1, ST:2 * ST], spf[0:1, 0:ST], excl[0:1, b:b + 1], spf[0:1, ST:2 * ST], ALU.is_ge, ALU.add))
                yield lambda: dve.tensor_scalar(stoff[:], spf[0:1, ST:2 * ST], float(D), None, ALU.mult).then_inc(S("stoff"), 1)

            def x_lo(i):
                dve.wait_ge(S("t_hi"), i + 1)
                dve.tensor_tensor(xt3(xTl, i), psb[4 + i % 2][:].rearrange("p (k c) -> p k c", k=KC),
                                  xt3(xTh, i).bitcast(F32), ALU.subtract).then_inc(S("t_lo"), 1)

            def residual(i):
                g = G[:, i % 4, :]
                dve.wait_ge(S(f"xr{i % 4}"), 16 * (i // 4 + 1))
                ch(dve.tensor_tensor(g, g, at(i), ALU.add))
                dve.wait_ge(S("xrb"), 16)
                dve.tensor_tensor(g, g, G[:, 7, :], ALU.add).then_inc(S("res"), 1)

            def h_matrix(j, par, nxt=True, between=None, more=None):
                m = 2 * j + par
                dve.wait_ge(S(f"b_in{par}"), 16 * (j + 1))
                for i in range(NT):
                    if between:
                        between(i)
                    dve.wait_ge(S("h_pe"), C1 + 20 * m + i + 1)
                    if nxt:
                        dve.wait_ge(S(f"h_out{i % HB}"), 16 * (5 * m + i // HB))
                    dst = HS[:, i % HB, :] if nxt else at(i)
                    dve.tensor_tensor(dst, psb[i % HB][:], brd[:, par, :], ALU.add).then_inc(S("h_ev"), 1)
                    if more:
                        more(i)
                    if nxt and i % 5 == 3:
                        lo_w(dve, m + 1, i // 5, Wl[:, 1 - par, i // 5, :], Wh[:, 1 - par, i // 5, :])

            group_stats(0)
            for k in range(2):
                lo_w(dve, 0, k, Wl[:, 0, k, :], Wh[:, 0, k, :])
            norm(0)
            for k in range(2, KC):
                lo_w(dve, 0, k, Wl[:, 0, k, :], Wh[:, 0, k, :])
            x_lo(0)
            group_stats(1)

            def norm_next(i):
                if i % 5 == 0 and i < 10:
                    group_stats(i // 5 + 2)
                if i % 5 == 2 and i < 15:
                    norm(i // 5 + 1)
                if i + 1 < NT:
                    x_lo(i + 1)

            def take(ops, n):
                for _ in range(n):
                    op = next(ops, None)
                    if op:
                        op()

            counts, ops = count_ops(), sort_ops()

            def sort_part(i):
                if i < 8:
                    take(counts, 6)
                elif i == 8:
                    assert next(counts, None) is None
                    payload()
                elif i == 10:
                    offsets()
                elif i > 10:
                    take(ops, 3)

            h_matrix(0, 0, between=norm_next)
            h_matrix(0, 1, between=sort_part)
            for m in (2, 3):
                h_matrix(m // 2, m % 2, between=lambda i: take(ops, 2 + (i % 4 == 0)))
            assert next(ops, None) is None
            h_matrix(2, 0, more=residual)

            def stats2(i):
                a = dve.bn_stats(stn[:, i % 5, :], at(i))
                if i % 5 == 4:
                    ch(a)
                    for t in range(i - 4, i + 1):
                        a = dve.bn_aggr(mv2[:, t, :], stn[:, t % 5, :])
                    ch(a)
                    if i == NT - 1:
                        dve.tensor_scalar(ve2[:], mv2[:, :, 1], EPS, None, ALU.add).then_inc(S("ve2"), 1)

            h_matrix(2, 1, between=stats2)
            with dve.Fori(3, NREL // 2) as mj:
                h_matrix(mj, 0)
                h_matrix(mj, 1)
            dve.wait_ge(S("xn_out"), 64)
            h_matrix(NREL // 2, 0, nxt=False)
            dve.memset(qT, 0.0).then_inc(S("zeros"), 1)
            ch(dve.tensor_reduce(isum[:], ins_s[:], AX.X, ALU.add))
            ch(dve.tensor_scalar(isum[:], isum[:], 1.0 / NI, None, ALU.mult))
            dve.tensor_tensor(ibr, id8[:].unsqueeze(2).to_broadcast([P, NX, KC, NX]),
                              isum[:].unsqueeze(1).unsqueeze(3).to_broadcast([P, NX, KC, NX]), ALU.mult)
            for k in range(KC):
                a = dve.tensor_scalar(isb[:, k, :], ones[:], isum[:, k:k + 1], None, ALU.mult)
            a.then_inc(S("ib_ok"), 1)
            ch(dve.tensor_copy(gth[:], rmg[:, :, 0:NX]))
            dve.tensor_tensor(gtl[:], rmg[:, :, 0:NX], gth[:].bitcast(F32), ALU.subtract)
            dve.wait_ge(S("rs2"), 1)
            dve.scalar_tensor_tensor(nb2[:], mv2[:, :, 0], -1.0, rs2[:], ALU.mult, ALU.mult).then_inc(S("nb2"), 1)
            dve.wait_ge(S("t_in"), 16)
            ch(dve.tensor_copy(loc[:, :, 1], tbl[:, :, 1]))
            dve.wait_ge(S("mb_in"), 32)

            def st_step(it, s):
                st = SPI * it + s
                dve.wait_ge(S("st_pe"), CP - SR + st + 1)
                dve.tensor_scalar(ohr[:, s % SR, :], iotaf[:], loc[:, bass.ds(2 * st, 1), 1], None, ALU.is_equal)
                dve.tensor_scalar(ohf[:, s % SR, :], iotaf[:], loc[:, bass.ds(2 * st + 1, 1), 1], None, ALU.is_equal)
                dve.wait_ge(S("st_hi"), st + 1)
                dve.tensor_tensor(cut(spl, xTl, s), even[s % 4], cut(sph, xTh, s).bitcast(F32),
                                  ALU.subtract).then_inc(S("st_lo"), 1)

            def st_add(st, b):
                col = dve.value_load(stoff[0:1, bass.ds(st, 1)], min_val=0, max_val=(NT - 1) * D)
                dve.wait_ge(S("st_pe"), CP + st + 1)
                dve.wait_ge(S("st_ev"), 2 + st)
                dve.tensor_tensor(acc[:, bass.ds(col, D)], psb[b][:], acc[:, bass.ds(col, D)], ALU.add).then_inc(S("st_ev"), 1)

            def o_lo(O):
                dve.wait_ge(S("o_hi"), O + 1)
                dve.tensor_tensor(mxs(xTl, 1), psb[7][:], mxs(xTh, 1).bitcast(F32), ALU.subtract).then_inc(S("o_lo"), 1)

            def o_n(O):
                dve.wait_ge(S("o_pe"), O + 1)
                ch(dve.tensor_scalar(nrm[:, 0:NX], psb[6][:, 0:NX], EPSN, None, ALU.add))
                ch(dve.reciprocal(nrm[:, NX:2 * NX], nrm[:, 0:NX]))
                dve.tensor_tensor(on.rearrange("p (h e) -> p h e", h=NX), psb[5][:].rearrange("p (h e) -> p h e", h=NX),
                                  nrm[:, NX:2 * NX].unsqueeze(2).to_broadcast([P, NX, D // NX]), ALU.mult).then_inc(S("o_n"), 1)

            def y(O):
                dve.wait_ge(S("o_p"), C1 + O + 1)
                dve.wait_ge(S("y_in"), 16 * (O + 1))
                dve.tensor_tensor(zmix(O), psb[3][:], yb, ALU.add).then_inc(S("m_y"), 1)

            def step(it, M=None, A=None, L=None, B=None, C=None, Q=None, U=None, O=None, V=None, Y=None):
                if not isinstance(it, int) and O is not None:
                    ch.enter(it - LOOP2, 2)
                for s in range(SPI):
                    if M is not None:
                        q = 2 * M + s // KC
                        lo_w(dve, WQ + q, s % KC, mw(xTl, q, s % KC), mw(xTh, q, s % KC))
                    if s == 0 and L is not None:
                        dve.wait_ge(S("m_hi"), C1 + L + 1)
                        dve.tensor_tensor(mxs(xTl, 0), xmf, mxs(xTh, 0).bitcast(F32), ALU.subtract).then_inc(S("m_lo"), 1)
                    if s == 0 and Y is not None:
                        y(Y)
                    if s == 3 and V is not None:
                        o_lo(V)
                    if s == 3 and O is not None:
                        o_n(O)
                    if s == 4 and isinstance(it, int) and it == 22:
                        kv_end()
                    if s == 5 and B is not None:
                        dve.wait_ge(S("m_k"), C1 + B + 1)
                        dve.tensor_tensor(kb, psb[2][:], brd[:, 0, :], ALU.add).then_inc(S("m_k2"), 1)
                    if s == 5 and Q is not None:
                        if isinstance(Q, int) and Q == 0:
                            dve.wait_ge(S("mb_in"), 48)
                        dve.wait_ge(S("m_k"), C1 + NT + Q + 1)
                        dve.tensor_tensor(kb, psb[2][:], brd[:, 0, :], ALU.add).then_inc(S("m_k2"), 1)
                    if s == 7 and B is not None:
                        dve.wait_ge(S("m_e"), B + 1)
                        dve.wait_ge(S("m_kv"), C1 + B)
                        dve.scalar_tensor_tensor(kt, kE, 1.0, kR, ALU.min, ALU.add).then_inc(S("m_k3"), 1)
                    if s == 7 and Q is not None:
                        dve.wait_ge(S("m_e"), NT + Q + 1)
                        if U is not None:
                            dve.wait_ge(S("q_tr"), U + 1)
                        dve.scalar_tensor_tensor(kt, kE, 1.0, kR, ALU.min, ALU.add).then_inc(S("m_k3"), 1)
                    st_step(it, s)
                    if s >= 2:
                        st_add(SPI * it + s - 2, s % 2)
                    elif not (isinstance(it, int) and it == 0):
                        st_add(SPI * (it - 1) + SPI + s - 2, s % 2)
                if isinstance(it, int) and it == 1:
                    dve.wait_ge(S("rg_pe"), 1)
                    dve.tensor_copy(rg[:], psb[2][:, 0:2 * NX])
                    ch(dve.tensor_copy(g8[:], psb[3][0:NX, 0:2]))
                    dve.wait_ge(S("eb_in"), 16)
                    dve.wait_ge(S("bw_used"), NX * KC)
                    dve.scalar_tensor_tensor(bb[0:NX, :], bb[0:NX, :], g8[:, 0:1], psb[7][0:NX, :], ALU.mult, ALU.add).then_inc(S("bb_ok"), 1)
                if isinstance(it, int) and it == 21:
                    ch(dve.memset(kvs[:, :, :], 0.0))
                    ch(dve.memset(ks2[:, :, :], 0.0))
                if not isinstance(it, int) and O is not None:
                    ch.leave(41 - LOOP2)

            def kv_end():
                dve.wait_ge(S("m_kv"), C1 + NT)
                for k in range(KC):
                    a = dve.tensor_scalar(vt[:, k * P:(k + 1) * P], brd[:, 1, k * P:(k + 1) * P],
                                          psb[6][:, 2 * k:2 * k + 1], None, ALU.mult)
                ch(a)
                for h in range(2):
                    r = slice(64 * h, 64 * h + 64)
                    c = slice(64 * h, 64 * h + 64)
                    dve.tensor_tensor(kvs[r, :, c], psb[5][r, :].rearrange("p (k c) -> p k c", k=KC)[:, :, c],
                                      vt[r, :].rearrange("p (k c) -> p k c", k=KC)[:, :, c], ALU.add)
                    a = dve.tensor_copy(ks2[r, :, h:h + 1], psb[6][r, 0:2 * KC].rearrange("p (k c) -> p k c", k=KC)[:, :, 0:1])
                a.then_inc(S("kvs_ok"), 1)

            schedule(dve, step)
            for st in (ST - 2, ST - 1):
                st_add(st, st % 2)
            y(NT - 2)
            o_lo(NT - 1)
            y(NT - 1)
            dve.wait_ge(S("m_y"), C1 + NT)
            def lo_x(n):
                c = KC * XO[n // KC] + n % KC
                dve.wait_ge(S("w_hi"), 4 * WX + n + 1)
                dve.tensor_tensor(We[:, c, 1, :], raw_x(c), We[:, c, 0, :].bitcast(F32),
                                  ALU.subtract).then_inc(S("w_lo"), 1)

            def x_part(i):
                dve.scalar_tensor_tensor(at(i), at(i), 0.0, zmix(i), ALU.max, ALU.add).then_inc(S("f_x1"), 1)
                if i % 4:
                    dve.wait_ge(S("f_x1"), i)
                    dve.bn_stats(stn[:, i % 4 - 1, :], at(i - 1))
                if i % 4 == 3:
                    dve.wait_ge(S("f_x1"), i + 1)
                    ch(dve.bn_stats(stn[:, 3, :], at(i)))
                    for t in range(i - 3, i + 1):
                        a = dve.bn_aggr(mv[:, t, :], stn[:, t % 4, :])
                    ch(a)
                    q = slice(i - 3, i + 1)
                    dve.tensor_scalar(ve[:, q], mv[:, q, 1], EPS, None, ALU.add).then_inc(S("f_ve"), 1)

            def nb_part(g):
                q = slice(4 * g, 4 * g + 4)
                dve.wait_ge(S("f_rs"), g + 1)
                dve.scalar_tensor_tensor(nb[:, q], mv[:, q, 0], -1.0, rs[:, q], ALU.mult, ALU.mult).then_inc(S("f_nb"), 1)

            def t_lo(i):
                dve.wait_ge(S("f_hi"), i + 1)
                dve.tensor_tensor(spl[:, i % 2, :], psb[4 + i % 2][:], sph[:, i % 2, :].bitcast(F32),
                                  ALU.subtract).then_inc(S("f_lo"), 1)

            dve.wait_ge(S("k_tokn"), 1)
            ch(dve.tensor_copy(br[0:NX, :], bb[0:NX, :]))
            for g in range(2):
                for i in range(4 * g, 4 * g + 4):
                    x_part(i)
                nb_part(g)
            for i in range(NT):
                if i % 4 == 0 and 4 <= i <= 12:
                    nb_part(i // 4 + 1)
                if i + 8 < NT:
                    x_part(i + 8)
                t_lo(i)
                if i >= 8:
                    lo_x(2 * (i - 8))
                    lo_x(2 * (i - 8) + 1)
            dve.wait_ge(S("f_gl"), NT // 4)
            lg = r_tmp
            ch(dve.tensor_tensor(by_t(lg), by_t(psb[6][:, 0:nr]), rg[:, 0:NX].unsqueeze(1).to_broadcast([P, NT, NX]), ALU.add))
            ch(dve.tensor_reduce(r_mx, by_t(lg), AX.X, ALU.max))
            dve.tensor_tensor(by_t(lg), by_t(lg), r_mx.unsqueeze(2).to_broadcast([P, NT, NX]), ALU.subtract).then_inc(S("f_lg"), 1)
            dve.wait_ge(S("f_ex"), 1)
            ch(dve.tensor_reduce(r_sum, by_t(r_ex), AX.X, ALU.add))
            ch(dve.reciprocal(r_sum, r_sum))
            ch(dve.tensor_tensor(by_t(r_ex), by_t(r_ex), r_sum.unsqueeze(2).to_broadcast([P, NT, NX]), ALU.mult))
            for e in range(NX):
                if e:
                    dve.tensor_tensor(r_gt[:, :, e, 0:e], by_t(r_ex)[:, :, 0:e], by_t(r_ex)[:, :, e:e + 1].to_broadcast([P, NT, e]), ALU.is_ge)
                a = dve.tensor_tensor(r_gt[:, :, e, e:NX], by_t(r_ex)[:, :, e:NX], by_t(r_ex)[:, :, e:e + 1].to_broadcast([P, NT, NX - e]), ALU.is_gt)
            ch(a)
            ch(dve.tensor_reduce(by_t(r_rk), r_gt, AX.X, ALU.add))
            rk_et = r_rk.rearrange("p (t e) -> p e t", e=NX)
            ch(dve.tensor_scalar(by_e(r_m), rk_et, 2.0, None, ALU.is_lt))
            dve.tensor_reduce(rt[:, 0, :], by_e(r_m), AX.X, ALU.add).then_inc(S("f_cnt"), 1)
            ch(dve.tensor_tensor_scan(r_pos, r_m, r_m, 0.0, ALU.add, ALU.max))
            dve.wait_ge(S("f_cnt"), 1)
            ch(dve.tensor_tensor_scan(rt[:, 1, :], rt[:, 0, :], rt[:, 0, :], 0.0, ALU.add, ALU.max))
            dve.scalar_tensor_tensor(r_c, r_rk, 2.0, r_ex, ALU.is_lt, ALU.mult).then_inc(S("f_c"), 1)
            ri = rt[:, 2, :].bitcast(I32)
            dve.wait_ge(S("f_pre"), 1)
            ch(dve.tensor_scalar(ri, psb[5][:, 32:32 + NX], float(P - 1), None, ALU.add))
            ch(dve.tensor_scalar(ri, ri, 7, None, ALU.arith_shift_right))
            ch(dve.tensor_copy(rt[:, 3, :], ri))
            ch(dve.tensor_tensor_scan(rt[:, 4, :], rt[:, 3, :], rt[:, 3, :], 0.0, ALU.add, ALU.max))
            ch(dve.tensor_tensor(rt[:, 3, :], rt[:, 4, :], rt[:, 3, :], ALU.subtract))
            ch(dve.scalar_tensor_tensor(rt[:, 5, :], rt[:, 3, :], float(P), psb[5][:, 0:NX], ALU.mult, ALU.add))
            ch(dve.tensor_tensor(rt[:, 5, :], rt[:, 5, :], rt[:, 1, :], ALU.subtract))
            ch(dve.tensor_tensor(rt[:, 5, :], rt[:, 5, :], rt[:, 0, :], ALU.add))
            ch(dve.tensor_tensor(by_e(r_pos), by_e(r_pos), rt[:, 5, :].unsqueeze(2).to_broadcast([P, NX, NT]), ALU.add))
            for j in range(2):
                ch(dve.tensor_scalar(by_e(r_m), rk_et, float(j), None, ALU.is_equal))
                ch(dve.tensor_tensor(r_tmp, r_m, r_pos, ALU.mult))
                ch(dve.tensor_reduce(posf[:, j, :], r_tmp.rearrange("p (e t) -> p t e", e=NX), AX.X, ALU.add))
            si, mi, ti = (rt[:, 6 + 3 * i:6 + 3 * i + 3, :].bitcast(I32).rearrange("p a b -> p (a b)") for i in range(3))
            for j in range(2):
                ch(dve.tensor_scalar(si[:, 0:NT], posf[:, j, :], -1.0, float(NSL * P - 1), ALU.add, ALU.min))
                dve.tensor_scalar(mi[:, 0:NT], si[:, 0:NT], P - 1, None, ALU.bitwise_and)
                ch(dve.tensor_scalar(ti[:, 0:NT], si[:, 0:NT], 7, None, ALU.arith_shift_right))
                dve.scalar_tensor_tensor(slot[:, j, :], mi[:, 0:NT], float(NSL), ti[:, 0:NT], ALU.mult, ALU.add).then_inc(S("slot"), 1)
                plo, phi = r_pos[:, 0:NT], r_pos[:, NT:2 * NT]
                dve.tensor_copy(plo, mi[:, 0:NT])
                ch(dve.tensor_copy(phi, ti[:, 0:NT]))
                for g in range(NT // 4):
                    m = j * NT // 4 + g
                    t = slice(4 * g, 4 * g + 4)
                    if m >= 2:
                        dve.wait_ge(S("oh_pe"), 4 * (m - 1))
                    dve.tensor_tensor(oh_p[:, m % 2], iotaf[:].unsqueeze(1).to_broadcast([P, 4, P]),
                                      plo[:, t].unsqueeze(2).to_broadcast([P, 4, P]), ALU.is_equal)
                    ch(dve.tensor_tensor(oh_t[:, m % 2], iotaf[:, 0:NSL].unsqueeze(1).to_broadcast([P, 4, NSL]),
                                         phi[:, t].unsqueeze(2).to_broadcast([P, 4, NSL]), ALU.is_equal))
                    dve.tensor_tensor(oh_t[:, m % 2], oh_t[:, m % 2],
                                      tokn[:, t].unsqueeze(2).to_broadcast([P, 4, NSL]), ALU.mult).then_inc(S("oh"), 4)
                if j == 0:
                    dve.wait_ge(S("slot"), 1)
            dve.wait_ge(S("oh_pe"), 2 * NT)
            dve.tensor_copy(toks[:], psb[6][:, 0:NSL]).then_inc(S("toks"), 1)
            for c in range(2 * (NT - 8), NX * KC):
                lo_x(c)
            ch(dve.tensor_tensor(by_t(r_ex), by_t(r_ex), rg[:, NX:2 * NX].unsqueeze(1).to_broadcast([P, NT, NX]), ALU.mult))
            for j in range(2):
                ch(dve.scalar_tensor_tensor(r_tmp, r_rk, float(j), r_ex, ALU.is_equal, ALU.mult))
                ch(dve.tensor_reduce(cgw[:, j, :], by_t(r_tmp), AX.X, ALU.add))
            ec = r_tmp[0:1, 0:NSL]
            ch(dve.memset(ec, 0.0))
            for e in range(1, NX):
                ch(dve.scalar_tensor_tensor(ec, iotaf[0:1, 0:NSL], rt[0:1, 3, e:e + 1], ec, ALU.is_ge, ALU.add))
            dve.tensor_scalar(ecol[:], ec, float(KC * 2 * D), None, ALU.mult).then_inc(S("e_col"), 1)

            def e_lo(i, u):
                dve.wait_ge(S("e_hi"), i + 1)
                dve.tensor_tensor(spl[:, u % 2, :], psb[4 + u % 2][:], sph[:, u % 2, :].bitcast(F32),
                                  ALU.subtract).then_inc(S("e_lo"), 1)

            def e_copy(i, u, n=None):
                dve.wait_ge(S("e_pe"), i + 1)
                if n is not None:
                    dve.wait_ge(S(f"y_out{u % 2}"), 16 * n)
                dve.tensor_copy(Wraw[:, u % 2, :], psb[u][:]).then_inc(S("e_cp"), 1)

            e_lo(0, 0)
            for i in range(4):
                e_lo(i + 1, (i + 1) % 4)
                e_copy(i, i, i // 2 if i >= 2 else None)
            with dve.Fori(1, NSL // 4) as g:
                for u in range(4):
                    e_lo(4 * g + u + 1, (u + 1) % 4)
                    e_copy(4 * g + u, u, 2 * g + u // 2)
            for i in range(NSL // 4 * 4, NSL):
                if i + 1 < NSL:
                    e_lo(i + 1, (i + 1) % 4)
                e_copy(i, i % 4, i // 2)
            for i in range(2 * NT):
                j, t = i % 2, i // 2
                if i % 8 == 0:
                    dve.wait_ge(S("f_c1"), i // 8 + 1)
                    dve.tensor_copy(cT[0:NX, :], psb[7][0:NX, :]).then_inc(S("f_ct"), 1)
                if j == 0:
                    dve.wait_ge(S("f_bp"), t + 1)
                    dve.tensor_tensor(at(t), at(t), psb[t % HB][:], ALU.add).then_inc(S("f_ba"), 1)
                    dve.wait_ge(S("f_ba"), t + 1)
                dve.wait_ge(S(f"g_odd{i % 8}"), G_BACK + 16 * (i // 8 + 1))
                if j:
                    dve.wait_ge(S("y_add"), i)
                dve.scalar_tensor_tensor(at(t), G[:, i % 8, :], cgw[:, j, t:t + 1], at(t), ALU.mult, ALU.add).then_inc(S("y_add"), 1)


def kernel(x, src, dst, edge_type_8, L0_gnn_W_self, L0_gnn_b_self, L0_gnn_W_rel, L0_gnn_b_rel, L0_mix_qkv_w,
           L0_mix_qkv_b, L0_mix_out_w, L0_mix_out_b, L0_mix_ln_gamma, L0_mix_ln_beta, L0_ffn_Ins_tk, L0_ffn_gate_w,
           L0_ffn_expert_w, L0_ffn_expert_b, L0_ffn_gamma_w, L0_ffn_beta_w, L0_ffn_rmod_w):
    import numpy as np
    import concourse.bacc as bacc
    from concourse.bass_utils import run_bass_kernel_spmd as run

    A = np.asarray
    w_all = np.concatenate([
        A(L0_gnn_W_rel).transpose(0, 2, 1), A(L0_gnn_W_self).T[None],
        A(L0_mix_qkv_w).reshape(3, D, D).transpose(0, 2, 1), A(L0_mix_out_w).T[None], A(L0_ffn_expert_w)])
    b_all = np.concatenate([A(L0_gnn_b_rel), A(L0_gnn_b_self)[None], A(L0_mix_qkv_b).reshape(3, D),
                            A(L0_mix_out_b)[None], A(L0_ffn_expert_b)])

    def by_k(a):
        return A(a).reshape(KC, P, -1).transpose(1, 0, 2)

    ins = {
        "x": A(x), "src": A(src), "dst": A(dst), "et": A(edge_type_8),
        "w_all": w_all.reshape(-1, D, D), "b_all": b_all,
        "gam_col": A(L0_mix_ln_gamma).reshape(KC, P).T, "bet_col": A(L0_mix_ln_beta).reshape(KC, P).T,
        "insT": by_k(A(L0_ffn_Ins_tk)[0].T), "gate": by_k(L0_ffn_gate_w), "rmod": by_k(L0_ffn_rmod_w),
        "gamw": by_k(A(L0_ffn_gamma_w).T), "betw": A(L0_ffn_beta_w).reshape(NX * D, D),
    }
    ins = {k: np.ascontiguousarray(v) for k, v in ins.items()}
    nc = bacc.Bacc("TRN2", target_bir_lowering=False, num_devices=1)
    aps = [nc.dram_tensor(f"in_{k}", v.shape, mybir.dt.from_np(v.dtype), kind="ExternalInput").ap() for k, v in ins.items()]
    out = nc.dram_tensor("out_0", (N, D), F32, kind="ExternalOutput").ap()
    h_d = nc.dram_tensor("h_scratch", (NREL * NPAD, D), F32, kind="Internal").ap()
    xn_d = nc.dram_tensor("xn_scratch", (NPAD, D), F32, kind="Internal").ap()
    z_d = nc.dram_tensor("z_scratch", (NPAD, D), F32, kind="Internal").ap()
    tab_d = nc.dram_tensor("table_scratch", (GT * P, 2), I32, kind="Internal").ap()
    build(nc, *aps, out, h_d, xn_d, z_d, tab_d)
    r = run(nc, [{f"in_{k}": v for k, v in ins.items()}], core_ids=[0])
    return r.results[0]["out_0"]
```
